# Optimizing a Trainium2 kernel written in Bass

```python
import numpy as np
import jax
import jax.numpy as jnp

def _softmax(x, axis=-1):
    return jax.nn.softmax(x, axis=axis)

def _gelu(x):
    return jax.nn.gelu(x, approximate=True)

def _silu(x):
    return jax.nn.silu(x)

def _sigmoid(x):
    return jax.nn.sigmoid(x)

def _layernorm(x, axis=-1, eps=1e-05):
    m = jnp.mean(x, axis=axis, keepdims=True)
    v = jnp.var(x, axis=axis, keepdims=True)
    return (x - m) / jnp.sqrt(v + eps)

def _scatter_add(tgt, idx, src, axis=0):
    return tgt.at[idx].add(src)

def _segment_sum(src, seg, n):
    return jax.ops.segment_sum(src, seg, n)
kernel_name = 'mk_flamingo_gated_d1_seqx_r2_9a1a53'

def setup_inputs(seed: int=0):
    np.random.seed(seed)
    _w = jnp.asarray

    def _rec_inputs():
        import jax
        import jax.numpy as jnp
        _rk = jax.random.key(seed)
        x = 7.22e-05 + 1 * jax.random.normal(jax.random.fold_in(_rk, 1), (8, 512, 512), jnp.float32)
        _lenS = 512 - jax.random.randint(jax.random.fold_in(_rk, 7), (8,), 0, max(1, 512 // 4) + 1, jnp.int32)
        _lenS2 = 512 - jax.random.randint(jax.random.fold_in(_rk, 8), (8,), 0, max(1, 512 // 4) + 1, jnp.int32)
        _ctx_1024P = jax.random.normal(jax.random.fold_in(_rk, 11), (8, 16, 512), jnp.float32)
        _ctx_1024c = jax.random.dirichlet(jax.random.fold_in(_rk, 511), 0.3 * jnp.ones((16,), jnp.float32), (8, 512))
        _ctx_1024t = jnp.einsum('bsk,bkd->bsd', _ctx_1024c, _ctx_1024P)
        _ctx_1024t = _ctx_1024t * jax.lax.rsqrt(jnp.mean(jnp.square(_ctx_1024t)) + 1e-12) * 0.953939
        ctx_1024 = -0.000514642 + 1.00011 * (_ctx_1024t + 0.3 * jax.random.normal(jax.random.fold_in(_rk, 611), (8, 512, 512), jnp.float32))
        _g = jax.random.normal(jax.random.fold_in(_rk, 9001), (2, 1), jnp.float32)
        _g = jnp.sign(_g) * jnp.maximum(jnp.abs(_g), 1.0) + (_g == 0) * 1.0
        g_xattn = _g[0]
        g_ffn = _g[1]
        return (x, ctx_1024, g_xattn, g_ffn)
    x, ctx_1024, g_xattn, g_ffn = _rec_inputs()

    def _L0_xattn_setup():
        import jax, jax.numpy as jnp
        import numpy as np
        B, L_ENC, L_DEC, D = (16, 256, 128, 512)
        key = jax.random.key(seed)
        k1, k2, k3, k4, k5, k6 = jax.random.split(key, 6)
        encoder_hc = jax.random.normal(k1, (B, L_ENC, D), dtype=jnp.float32)
        decoder_hq = jax.random.normal(k2, (B, L_DEC, D), dtype=jnp.float32)
        w_sim = jax.random.normal(k3, (3 * D,), dtype=jnp.float32) * 0.02
        b_sim = jax.random.normal(k4, (1,), dtype=jnp.float32) * 0.02
        W_qv = jax.random.normal(k5, (4 * D, D), dtype=jnp.float32) * 0.02
        b_qv = jax.random.normal(k6, (D,), dtype=jnp.float32) * 0.02
        return {'encoder_hc': encoder_hc, 'decoder_hq': decoder_hq, 'w_sim': w_sim, 'b_sim': b_sim, 'W_qv': W_qv, 'b_qv': b_qv}
    _L0_xattn_all = _L0_xattn_setup()
    _L0_xattn_in = {k: v for k, v in _L0_xattn_all.items() if k in ('w_sim', 'b_sim', 'W_qv', 'b_qv')}
    del _L0_xattn_all

    def _L0_ffn_setup():
        import jax, jax.numpy as jnp
        import numpy as np
        B, T, D = (4, 1024, 512)
        H, DH, E, SEL = (8, 64, 5, 2)

        def _topk_mask(logits, k):
            _, idx = jax.lax.top_k(logits, k)
            return jnp.sum(jax.nn.one_hot(idx, logits.shape[-1], dtype=logits.dtype), axis=-2)
        key = jax.random.key(seed)
        ks = jax.random.split(key, 7)
        s = 0.02
        x = jax.random.normal(ks[0], (B, T, D), dtype=jnp.float32)
        Wq = jax.random.normal(ks[1], (D, H * DH), dtype=jnp.float32) * s
        Wk = jax.random.normal(ks[2], (D, H * DH), dtype=jnp.float32) * s
        Ws = jax.random.normal(ks[3], (D, H * E), dtype=jnp.float32) * s
        Wd = jax.random.normal(ks[4], (D, H * E), dtype=jnp.float32) * s
        Wv = jax.random.normal(ks[5], (E, D, DH), dtype=jnp.float32) * s
        Wo = jax.random.normal(ks[6], (E, DH, D), dtype=jnp.float32) * s
        return {'x': x, 'Wq': Wq, 'Wk': Wk, 'Ws': Ws, 'Wd': Wd, 'Wv': Wv, 'Wo': Wo}
    _L0_ffn_all = _L0_ffn_setup()
    _L0_ffn_in = {k: v for k, v in _L0_ffn_all.items() if k in ('Wq', 'Wk', 'Ws', 'Wd', 'Wv', 'Wo')}
    del _L0_ffn_all
    return {'x': x, 'ctx_1024': ctx_1024, 'g_xattn': g_xattn, 'g_ffn': g_ffn, 'L0_xattn_w_sim': _L0_xattn_in['w_sim'], 'L0_xattn_b_sim': _L0_xattn_in['b_sim'], 'L0_xattn_W_qv': _L0_xattn_in['W_qv'], 'L0_xattn_b_qv': _L0_xattn_in['b_qv'], 'L0_ffn_Wq': _L0_ffn_in['Wq'], 'L0_ffn_Wk': _L0_ffn_in['Wk'], 'L0_ffn_Ws': _L0_ffn_in['Ws'], 'L0_ffn_Wd': _L0_ffn_in['Wd'], 'L0_ffn_Wv': _L0_ffn_in['Wv'], 'L0_ffn_Wo': _L0_ffn_in['Wo']}

def reference(x, ctx_1024, g_xattn, g_ffn, L0_xattn_w_sim, L0_xattn_b_sim, L0_xattn_W_qv, L0_xattn_b_qv, L0_ffn_Wq, L0_ffn_Wk, L0_ffn_Ws, L0_ffn_Wd, L0_ffn_Wv, L0_ffn_Wo):
    import jax
    import jax.numpy as jnp

    def _L0_xattn_ref(encoder_hc, decoder_hq, w_sim, b_sim, W_qv, b_qv):
        import jax, jax.numpy as jnp
        import numpy as np
        B, L_ENC, L_DEC, D = (16, 256, 128, 512)
        d = encoder_hc.shape[-1]
        w1, w2, w3 = (w_sim[:d], w_sim[d:2 * d], w_sim[2 * d:])
        Sim = (encoder_hc @ w1)[:, :, None] + (decoder_hq @ w2)[:, None, :] + jnp.einsum('bid,bjd->bij', encoder_hc * w3, decoder_hq) + b_sim[0]
        A = jax.nn.softmax(Sim, axis=2)
        hq_hat = jnp.einsum('bij,bjd->bid', A, decoder_hq)
        Batt = jax.nn.softmax(jnp.max(Sim, axis=2), axis=1)
        hc_bar = jnp.einsum('bi,bid->bd', Batt, encoder_hc)[:, None, :]
        hc_hat = jnp.broadcast_to(hc_bar, encoder_hc.shape)
        feats = jnp.concatenate([encoder_hc, hq_hat, encoder_hc * hq_hat, encoder_hc * hc_hat], axis=-1)
        hcq = feats @ W_qv + b_qv
        return hcq

    def _L0_ffn_ref(x, Wq, Wk, Ws, Wd, Wv, Wo):
        import jax, jax.numpy as jnp
        import numpy as np
        B, T, D = (4, 1024, 512)
        H, DH, E, SEL = (8, 64, 5, 2)

        def _topk_mask(logits, k):
            _, idx = jax.lax.top_k(logits, k)
            return jnp.sum(jax.nn.one_hot(idx, logits.shape[-1], dtype=logits.dtype), axis=-2)
        e, d, dh = Wv.shape
        h = Wq.shape[1] // dh
        b, t, _ = x.shape
        scale = dh ** (-0.5)
        q = (x @ Wq).reshape(b, t, h, dh).transpose(0, 2, 1, 3)
        k = (x @ Wk).reshape(b, t, h, dh).transpose(0, 2, 1, 3)
        gl_v = (x @ Ws).reshape(b, t, h, e)
        wv = _topk_mask(gl_v, SEL) * jax.nn.sigmoid(gl_v)
        xv = jnp.einsum('btd,edk->btek', x, Wv)
        v = jnp.einsum('bthe,btek->bhtk', wv, xv)
        scores = jnp.einsum('bhid,bhjd->bhij', q * scale, k)
        probs = jax.nn.softmax(scores, axis=-1)
        attn = jnp.einsum('bhij,bhjd->bihd', probs, v)
        gl_o = (x @ Wd).reshape(b, t, h, e)
        mask_o = _topk_mask(gl_o, SEL)
        out = jnp.einsum('bthe,bthk,ekd->btd', mask_o, attn, Wo)
        return out
    x = x + jnp.tanh(g_xattn[0]) * _L0_xattn_ref(_layernorm(x, axis=-1), ctx_1024, L0_xattn_w_sim, L0_xattn_b_sim, L0_xattn_W_qv, L0_xattn_b_qv)
    x = x + jnp.tanh(g_ffn[0]) * _L0_ffn_ref(_layernorm(x, axis=-1), L0_ffn_Wq, L0_ffn_Wk, L0_ffn_Ws, L0_ffn_Wd, L0_ffn_Wv, L0_ffn_Wo)
    return x

_drawn_inputs = setup_inputs


def setup_inputs(seed=0):
    import zlib

    import numpy as np

    out = dict(_drawn_inputs(seed))
    spreads = {}
    factors = {'L0_xattn_b_qv': 3.763,
     'L0_ffn_Wq': 8.0,
     'L0_ffn_Wk': 8.0,
     'L0_ffn_Ws': 5.314,
     'L0_ffn_Wd': 2.969}
    for name, (base, spread) in spreads.items():
        noise = np.random.default_rng([zlib.crc32(name.encode()), seed]).standard_normal(out[name].shape)
        drawn = base * np.exp(spread * noise) if base else spread * noise
        out[name] = jnp.asarray(drawn.astype(out[name].dtype))
    for name, factor in factors.items():
        out[name] = (out[name] * factor).astype(out[name].dtype)
    return out
```

```python
from contextlib import ExitStack

import concourse.bass as bass
from concourse import mybir

F32 = mybir.dt.float32
F32R = mybir.dt.float32r
I32 = mybir.dt.int32
BF16 = mybir.dt.bfloat16
ALU = mybir.AluOpType
ACT = mybir.ActivationFunctionType
AX_X = mybir.AxisListType.X

P = 128
EPS = 1e-5
PASSES = ((0, 0), (0, 1), (1, 0))


def mean_rstd(dve, stats, size, mean, work, rstd, done, count):
    both, diff, var, guess = work[:, 0:2], work[:, 2], work[:, 3], work[:, 4]
    steps = [count]

    def group(*instructions):
        for instruction in instructions:
            instruction.then_inc(done, 1)
        steps[0] = steps[0] + len(instructions)
        dve.wait_ge(done, steps[0])

    by_kind = stats.rearrange("p t k -> p k t")
    group(dve.tensor_tensor(both, by_kind[:, 1:3], by_kind[:, 4:6], ALU.add),
          dve.tensor_tensor(diff, by_kind[:, 1], by_kind[:, 4], ALU.subtract))
    group(dve.tensor_scalar(mean, both[:, 0], 0.5, None, ALU.mult),
          dve.tensor_scalar(var, both[:, 1], 1.0 / size, EPS, ALU.mult, ALU.add),
          dve.tensor_tensor(diff, diff, diff, ALU.mult))
    group(dve.scalar_tensor_tensor(var, diff, 0.25, var, ALU.mult, ALU.add))
    group(dve.tensor_scalar(guess.bitcast(I32), var.bitcast(I32), 1, None, ALU.logical_shift_right))
    group(dve.tensor_scalar(rstd.bitcast(I32), guess.bitcast(I32), -1.0, float(0x5F3759DF), ALU.mult, ALU.add))
    for _ in range(3):
        group(dve.tensor_tensor(guess, rstd, rstd, ALU.mult))
        group(dve.scalar_tensor_tensor(guess, guess, -0.5, var, ALU.mult, ALU.mult))
        group(dve.scalar_tensor_tensor(rstd, guess, 1.5, rstd, ALU.add, ALU.mult))


ROOT_STEPS = 17


def cross_attention(nc, x, ctx, ctx_t, g_xattn, w_sim, w_sim_cols, b_sim, w_qv, b_qv, x1):
    B, T, D = x.shape
    NT, ND = T // P, D // P
    SLOTS = 4
    W_CHUNKS = 2 * ND
    CHUNKS = NT + ND + NT
    assert W_CHUNKS % SLOTS == 0 and CHUNKS % SLOTS == 0 and NT == SLOTS == ND

    with ExitStack() as mem:
        def sb(name, shape, dt=F32):
            return mem.enter_context(nc.sbuf_tensor(name, shape, dt))

        def sem(name):
            return mem.enter_context(nc.semaphore(name))

        ident = sb("ident", [P, P])
        ones = sb("ones", [P, P])
        w1_row = sb("w1_row", [P, D])
        w_cols = sb("w_cols", [P, 3, ND])
        w2_col, w3_col = w_cols[:, 1, :], w_cols[:, 2, :]
        bsim_col = sb("bsim_col", [P, 1])
        gate = sb("gate", [P, 1])
        gate_raw = sb("gate_raw", [P, 1])
        bias_row = sb("bias_row", [P, D])
        we_raw = sb("we_raw", [P, ND, D])
        wc_raw = sb("wc_raw", [P, ND, D])
        wh = sb("wh", [P, 2, ND, D], F32R)
        weh = sb("weh", [P, 2, ND, D], F32R)
        wec = sb("wec", [P, 2, ND, D], F32R)
        stage = sb("stage", [P, SLOTS, D])
        x_sb = sb("x_sb", [P, NT, D])
        e_sb = sb("e_sb", [P, 2, D])
        e_t = sb("e_t", [P, ND, T])
        e_t2 = sb("e_t2", [P, 2, ND, T], F32R)
        es_t2 = sb("es_t2", [P, 2, ND, T], F32R)
        a_t2 = es_t2
        c_t2 = sb("c_t2", [P, 2, ND, T], F32R)
        c_2 = sb("c_2", [P, 2, NT, D], F32R)
        a_sb = sb("a_sb", [P, 2, T])
        h_t2 = sb("h_t2", [P, 2, ND, T], F32R)
        eh_t2 = sb("eh_t2", [P, 2, ND, T], F32R)
        tmp = sb("tmp", [P, ND, T])
        stats = sb("stats", [P, NT, 6])
        mean = sb("mean", [P, NT])
        work = sb("work", [P, 5, NT])
        rstd = sb("rstd", [P, NT])
        ew1 = sb("ew1", [P, NT])
        nmax = sb("nmax", [P, NT])
        den = sb("den", [P, NT])
        rden = sb("rden", [P, NT])
        mtot = sb("mtot", [P, NT])
        pmax = sb("pmax", [P, 1])
        gmax = sb("gmax", [1, 1])
        ngmax = sb("ngmax", [P, 1])
        bexp = sb("bexp", [P, NT])
        bsum = sb("bsum", [P, 1])
        rtot = sb("rtot", [P, 1])
        batt = sb("batt", [P, NT])
        hc = sb("hc", [P, ND])

        ps_s = mem.enter_context(nc.psum_tensor("ps_s", [P, 2, T], F32))
        ps_h = mem.enter_context(nc.psum_tensor("ps_h", [P, 2, T], F32))
        ps_f = mem.enter_context(nc.psum_tensor("ps_f", [P, 2, D], F32))
        ps_t = mem.enter_context(nc.psum_tensor("ps_t", [P, 4, P], F32))
        ps_b = mem.enter_context(nc.psum_tensor("ps_b", [P, T], F32))

        const_loaded = sem("const_loaded")
        wraw_loaded = sem("wraw_loaded")
        ident_ready = sem("ident_ready")
        gate_ready = sem("gate_ready")
        bias_ready = sem("bias_ready")
        slot_loaded = [sem(f"slot_loaded{s}") for s in range(SLOTS)]
        x_loaded = sem("x_loaded")
        x1_stored = sem("x1_stored")
        hi_cast = sem("hi_cast")
        lo_taken = sem("lo_taken")
        stats_done = sem("stats_done")
        newton = sem("newton")
        e_ready = sem("e_ready")
        ew1_ready = sem("ew1_ready")
        et_ps = sem("et_ps")
        et_copied = sem("et_copied")
        es_ready = sem("es_ready")
        es_hi = sem("es_hi")
        es_lo = sem("es_lo")
        et2_ready = sem("et2_ready")
        s_ready = sem("s_ready")
        nmax_ready = sem("nmax_ready")
        a_exp = sem("a_exp")
        rden_ready = sem("rden_ready")
        a_ready = sem("a_ready")
        at_ps = sem("at_ps")
        at_hi = sem("at_hi")
        at_lo = sem("at_lo")
        ht_ps = sem("ht_ps")
        ht_hi = sem("ht_hi")
        ht_lo = sem("ht_lo")
        eh_ready = sem("eh_ready")
        eh_hi = sem("eh_hi")
        eh_lo = sem("eh_lo")
        b_dve = sem("b_dve")
        b_pe = sem("b_pe")
        bexp_ready = sem("bexp_ready")
        hc_ready = sem("hc_ready")
        wec_ready = sem("wec_ready")
        wec_hi = sem("wec_hi")
        wec_lo = sem("wec_lo")
        feat_ps = sem("feat_ps")
        x1_ready = sem("x1_ready")
        xb_ready = sem("xb_ready")

        w_blocks = w_qv.rearrange("(m k p) n -> m p k n", m=4, p=P)
        x_dram = x.rearrange("b (t p) d -> b p t d", p=P)
        c_dram = ctx.rearrange("b (t p) d -> b p t d", p=P)
        ct_dram = ctx_t.rearrange("b (k p) j -> b p k j", p=P)
        x1_dram = x1.rearrange("b (t p) d -> b p t d", p=P)

        def of(dram, b):
            return dram[bass.ds(b, 1)].rearrange("o p t d -> (o p) t d")

        def slot_wait(eng, b, n):
            turn = n // SLOTS + 1 if b is None else b * (CHUNKS // SLOTS) + (W_CHUNKS + n) // SLOTS + 1
            eng.wait_ge(slot_loaded[n % SLOTS], turn * 16)

        block = mem.enter_context(nc.Block())

        @block.sync
        def _(sp):
            sp.dma_start(gate_raw[:], g_xattn.partition_broadcast(P)).then_inc(const_loaded, 16)
            sp.dma_start(w_cols[:], w_sim_cols).then_inc(const_loaded, 16)
            sp.dma_start(w1_row[:], w_sim[0:D].partition_broadcast(P)).then_inc(const_loaded, 16)
            sp.dma_start(bsim_col[:], b_sim.partition_broadcast(P)).then_inc(const_loaded, 16)
            sp.dma_start(bias_row[:], b_qv.partition_broadcast(P)).then_inc(const_loaded, 16)

            def load_weights():
                for n in range(W_CHUNKS):
                    if n >= SLOTS:
                        sp.wait_ge(lo_taken, n - SLOTS + 1)
                    sp.dma_start(stage[:, n % SLOTS, :], w_blocks[1 + n // ND, :, n % ND, :]).then_inc(
                        slot_loaded[n % SLOTS], 16)
                sp.dma_start(we_raw[:], w_blocks[0]).then_inc(wraw_loaded, 16)
                sp.dma_start(wc_raw[:], w_blocks[3]).then_inc(wraw_loaded, 16)

            def load_sequence(b):
                for t in range(NT):
                    sp.wait_ge(lo_taken, b * 2 * ND + W_CHUNKS - NT + t + 1)
                    sp.dma_start(stage[:, t, :], of(x_dram, b)[:, t, :]).then_inc(slot_loaded[t], 16)
                for k in range(ND):
                    sp.wait_ge(e_ready, b * NT + k + 1)
                    sp.dma_start(stage[:, k, :], of(ct_dram, b)[:, k, :]).then_inc(slot_loaded[k], 16)
                for t in range(NT):
                    sp.wait_ge(lo_taken, W_CHUNKS + b * 2 * ND + t + 1)
                    sp.dma_start(stage[:, t, :], of(c_dram, b)[:, t, :]).then_inc(slot_loaded[t], 16)

            def load_residual(b):
                sp.dma_start(x_sb[:], of(x_dram, b)).then_inc(x_loaded, 16)

            def store(b):
                for t in range(NT):
                    sp.wait_ge(x1_ready, b * NT + t + 1)
                    sp.dma_start(of(x1_dram, b)[:, t, :], x_sb[:, t, :]).then_inc(x1_stored, 16)

            load_weights()
            load_sequence(0)
            load_residual(0)
            with sp.Fori(0, B - 1) as b:
                load_sequence(b + 1)
                store(b)
                sp.wait_ge(x1_stored, (b + 1) * NT * 16)
                load_residual(b + 1)
            store(B - 1)
            sp.wait_ge(x1_stored, B * NT * 16)

        @block.gpsimd
        def _(pool):
            pool.memset(ident[:], 0.0).then_inc(ident_ready, 1)
            pool.memset(ones[:], 1.0).then_inc(ident_ready, 1)
            pool.wait_ge(ident_ready, 2)
            pool.affine_select(out=ident[:], in_=ident[:], compare_op=ALU.not_equal, fill=1.0, base=0,
                               pattern=[[-1, P]], channel_multiplier=1).then_inc(ident_ready, 1)

            def take_lo(b, n, cast, dst):
                pool.wait_ge(hi_cast, cast + 1)
                pool.tensor_tensor(dst[:, 1], stage[:, n % SLOTS, :], dst[:, 0].bitcast(F32),
                                   ALU.subtract).then_inc(lo_taken, 1)

            def split_sequence(b):
                for n in range(2 * ND):
                    dst = c_t2[:, :, n, :] if n < ND else c_2[:, :, n - ND, :]
                    take_lo(b, n, W_CHUNKS + b * 2 * ND + n, dst)

            def residual(b):
                pool.wait_ge(x_loaded, b * 16 + 16)
                pool.wait_ge(bias_ready, 1)
                pool.tensor_tensor(x_sb[:], x_sb[:], bias_row[:].unsqueeze(1).broadcast_to([P, NT, D]),
                                   ALU.add).then_inc(xb_ready, 1)

            for n in range(W_CHUNKS):
                take_lo(None, n, n, (wh if n < ND else weh)[:, :, n % ND, :])
            split_sequence(0)
            with pool.Fori(0, B - 1) as b:
                residual(b)
                pool.wait_ge(ht_ps, b * ND + ND)
                split_sequence(b + 1)
            residual(B - 1)

        @block.scalar
        def _(act):
            act.wait_ge(const_loaded, 5 * 16)
            act.activation(gate[:], gate_raw[:], ACT.Tanh).then_inc(gate_ready, 1)

            def cast_chunk(b, n, slot_n, dst):
                slot_wait(act, b, slot_n)
                act.activation(dst[:, 0], stage[:, slot_n % SLOTS, :], ACT.Copy).then_inc(hi_cast, 1)

            for n in range(W_CHUNKS):
                cast_chunk(None, n, n, (wh if n < ND else weh)[:, :, n % ND, :])

            def front(b):
                for t in range(NT):
                    act.wait_ge(et_ps, b * NT + t + 1)
                    act.activation(e_t[:, :, t * P:(t + 1) * P], ps_t[:], ACT.Copy).then_inc(et_copied, 1)
                for k in range(ND):
                    act.wait_ge(es_ready, b * ND + k + 1)
                    act.activation(es_t2[:, 0, k, :], tmp[:, k, :], ACT.Copy).then_inc(es_hi, 1)
                for n in range(2 * ND):
                    dst = c_t2[:, :, n, :] if n < ND else c_2[:, :, n - ND, :]
                    cast_chunk(b, n, NT + n, dst)

            def softmax_exp(b, t):
                act.wait_ge(nmax_ready, b * NT + t + 1)
                if t >= 2:
                    act.wait_ge(at_ps, b * NT + t - 1)
                act.activation(a_sb[:, t % 2, :], ps_s[:, t % 2, :], ACT.Exp, bias=nmax[:, t:t + 1],
                               accum_out=den[:, t:t + 1]).then_inc(a_exp, 1)

            def probs_hi(b, t):
                act.wait_ge(at_ps, b * NT + t + 1)
                act.activation(a_t2[:, 0, :, t * P:(t + 1) * P], ps_t[:], ACT.Copy).then_inc(at_hi, 1)

            def mid(b):
                for t in range(NT):
                    softmax_exp(b, t)
                    if t >= 1:
                        probs_hi(b, t - 1)
                probs_hi(b, NT - 1)
                act.wait_ge(b_dve, b * 6 + 4)
                act.activation(bexp[:], mtot[:], ACT.Exp, bias=ngmax[:, 0:1],
                               accum_out=bsum[:, 0:1]).then_inc(bexp_ready, 1)
                for k in range(ND):
                    act.wait_ge(ht_ps, b * ND + k + 1)
                    act.activation(h_t2[:, 0, k, :], ps_h[:, k % 2, :], ACT.Copy).then_inc(ht_hi, 1)
                    act.wait_ge(eh_ready, b * ND + k + 1)
                    act.activation(eh_t2[:, 0, k, :], tmp[:, k, :], ACT.Copy).then_inc(eh_hi, 1)
                for k in range(ND):
                    act.wait_ge(wec_ready, b * ND + k + 1)
                    act.activation(wec[:, 0, k, :], tmp[:, k, :], ACT.Copy).then_inc(wec_hi, 1)

            front(0)
            with act.Fori(0, B - 1) as b:
                mid(b)
                front(b + 1)
            mid(B - 1)

        @block.vector
        def _(dve):
            dve.wait_ge(gate_ready, 1)
            dve.tensor_scalar(bias_row[:], bias_row[:], gate[:, 0:1], None, ALU.mult).then_inc(bias_ready, 1)

            def front(b):
                for t in range(NT):
                    slot_wait(dve, b, t)
                    dve.bn_stats(stats[:, t, :], stage[:, t, :]).then_inc(stats_done, 1)
                dve.wait_ge(stats_done, b * NT + NT)
                mean_rstd(dve, stats[:], D, mean[:], work[:], rstd[:], newton, b * ROOT_STEPS)
                for t in range(NT):
                    if t >= 2:
                        dve.wait_ge(et_ps, b * NT + t - 1)
                        dve.wait_ge(ew1_ready, b * (NT + 1) + t - 1)
                    dve.tensor_scalar(e_sb[:, t % 2, :], stage[:, t, :], mean[:, t:t + 1], rstd[:, t:t + 1],
                                      ALU.subtract, ALU.mult).then_inc(e_ready, 1)
                    dve.wait_ge(e_ready, b * NT + t + 1)
                    dve.tensor_tensor_reduce(out=tmp[:, t, :], in0=e_sb[:, t % 2, :], in1=w1_row[:], scale=1.0,
                                             scalar=0.0, op0=ALU.mult, op1=ALU.add,
                                             accum_out=ew1[:, t:t + 1]).then_inc(ew1_ready, 1)
                dve.wait_ge(ew1_ready, b * (NT + 1) + NT)
                dve.tensor_scalar(ew1[:], ew1[:], bsim_col[:, 0:1], None, ALU.add).then_inc(ew1_ready, 1)
                dve.wait_ge(et_copied, b * NT + NT)
                for k in range(ND):
                    dve.tensor_scalar(tmp[:, k, :], e_t[:, k, :], w3_col[:, k:k + 1], w2_col[:, k:k + 1],
                                      ALU.mult, ALU.add).then_inc(es_ready, 1)
                for k in range(ND):
                    dve.wait_ge(es_hi, b * ND + k + 1)
                    dve.tensor_tensor(es_t2[:, 1, k, :], tmp[:, k, :], es_t2[:, 0, k, :].bitcast(F32),
                                      ALU.subtract).then_inc(es_lo, 1)

            def row_max(b, t):
                dve.wait_ge(s_ready, b * NT + t + 1)
                dve.tensor_reduce(nmax[:, t:t + 1], ps_s[:, t % 2, :], AX_X, ALU.max, negate=True).then_inc(
                    nmax_ready, 1)

            def normalise(b, t):
                dve.wait_ge(a_exp, b * NT + t + 1)
                dve.reciprocal(rden[:, t:t + 1], den[:, t:t + 1]).then_inc(rden_ready, 1)
                dve.wait_ge(rden_ready, b * NT + t + 1)
                dve.tensor_scalar(a_sb[:, t % 2, :], a_sb[:, t % 2, :], rden[:, t:t + 1], None,
                                  ALU.mult).then_inc(a_ready, 1)

            def probs_lo(b, t):
                dve.wait_ge(at_hi, b * NT + t + 1)
                dve.tensor_tensor(a_t2[:, 1, :, t * P:(t + 1) * P], ps_t[:],
                                  a_t2[:, 0, :, t * P:(t + 1) * P].bitcast(F32), ALU.subtract).then_inc(at_lo, 1)

            def mid(b):
                for t in range(NT):
                    row_max(b, t)
                    if t >= 1:
                        normalise(b, t - 1)
                    if t >= 2:
                        probs_lo(b, t - 2)
                normalise(b, NT - 1)
                probs_lo(b, NT - 2)
                dve.wait_ge(nmax_ready, b * NT + NT)
                dve.scalar_tensor_tensor(mtot[:], nmax[:], -1.0, ew1[:], ALU.mult, ALU.add).then_inc(b_dve, 1)
                dve.wait_ge(b_dve, b * 6 + 1)
                dve.reduce_max(pmax[:], mtot[:], AX_X).then_inc(b_dve, 1)
                probs_lo(b, NT - 1)
                dve.wait_ge(b_pe, b * 4 + 1)
                dve.tensor_reduce(gmax[:], ps_b[0:1, 0:P], AX_X, ALU.max, negate=True).then_inc(b_dve, 1)
                dve.tensor_copy(e_t2[:, 0], e_t[:]).then_inc(et2_ready, 1)
                dve.wait_ge(et2_ready, b * 2 + 1)
                dve.tensor_tensor(e_t2[:, 1], e_t[:], e_t2[:, 0].bitcast(F32), ALU.subtract).then_inc(et2_ready, 1)
                dve.wait_ge(b_pe, b * 4 + 2)
                dve.tensor_copy(ngmax[:], ps_b[:, 0:1]).then_inc(b_dve, 1)
                dve.wait_ge(b_pe, b * 4 + 3)
                dve.reciprocal(rtot[:], ps_b[:, 0:1]).then_inc(b_dve, 1)
                dve.wait_ge(b_dve, b * 6 + 5)
                dve.tensor_scalar(batt[:], bexp[:], rtot[:, 0:1], None, ALU.mult).then_inc(b_dve, 1)

                def h_parts(k):
                    dve.wait_ge(ht_hi, b * ND + k + 1)
                    dve.tensor_tensor(tmp[:, k, :], ps_h[:, k % 2, :], e_t[:, k, :], ALU.mult).then_inc(eh_ready, 1)
                    dve.tensor_tensor(h_t2[:, 1, k, :], ps_h[:, k % 2, :], h_t2[:, 0, k, :].bitcast(F32),
                                      ALU.subtract).then_inc(ht_lo, 1)

                def eh_low(k):
                    dve.wait_ge(eh_hi, b * ND + k + 1)
                    dve.tensor_tensor(eh_t2[:, 1, k, :], tmp[:, k, :], eh_t2[:, 0, k, :].bitcast(F32),
                                      ALU.subtract).then_inc(eh_lo, 1)

                for k in range(ND):
                    h_parts(k)
                    if k >= 1:
                        eh_low(k - 1)
                eh_low(ND - 1)
                dve.wait_ge(b_pe, b * 4 + 4)
                dve.wait_ge(eh_lo, b * ND + ND)
                for k in range(ND):
                    dve.tensor_tensor_reduce(out=tmp[:, k, :], in0=e_t[:, k, :], in1=ps_b[:], scale=1.0, scalar=0.0,
                                             op0=ALU.mult, op1=ALU.add, accum_out=hc[:, k:k + 1]).then_inc(hc_ready, 1)
                dve.wait_ge(wraw_loaded, 2 * 16)
                for k in range(ND):
                    dve.wait_ge(hc_ready, b * ND + k + 1)
                    dve.scalar_tensor_tensor(tmp[:, k, :], wc_raw[:, k, :], hc[:, k:k + 1], we_raw[:, k, :],
                                             ALU.mult, ALU.add).then_inc(wec_ready, 1)
                for k in range(ND):
                    dve.wait_ge(wec_hi, b * ND + k + 1)
                    dve.tensor_tensor(wec[:, 1, k, :], tmp[:, k, :], wec[:, 0, k, :].bitcast(F32),
                                      ALU.subtract).then_inc(wec_lo, 1)

            def tail(b):
                dve.wait_ge(xb_ready, b + 1)
                for t in range(NT):
                    dve.wait_ge(feat_ps, b * NT + t + 1)
                    dve.scalar_tensor_tensor(x_sb[:, t, :], ps_f[:, t % 2, :], gate[:, 0:1], x_sb[:, t, :],
                                             ALU.mult, ALU.add).then_inc(x1_ready, 1)

            front(0)
            with dve.Fori(0, B - 1) as b:
                mid(b)
                front(b + 1)
                tail(b)
            mid(B - 1)
            tail(B - 1)

        @block.tensor
        def _(pe):
            pe.wait_ge(ident_ready, 3)

            def product(out, left, right, start, stop):
                n = 0
                for k in range(ND):
                    for l, r in PASSES:
                        n += 1
                        last = pe.matmul(out, left(l, k), right(r, k), start=start and n == 1,
                                         stop=stop and n == ND * len(PASSES))
                return last

            def turn_e(b, t):
                pe.wait_ge(e_ready, b * NT + t + 1)
                if t:
                    pe.wait_ge(et_copied, b * NT + t)
                for k in range(ND):
                    last = pe.transpose(ps_t[:, k, :], e_sb[:, t % 2, k * P:(k + 1) * P], ident[:])
                last.then_inc(et_ps, 1)

            def scores(b, t):
                if t == 0:
                    pe.wait_ge(es_lo, b * ND + ND)
                    pe.wait_ge(lo_taken, W_CHUNKS + b * 2 * ND + ND)
                if t >= 2:
                    pe.wait_ge(a_exp, b * NT + t - 1)
                product(ps_s[:, t % 2, :], lambda l, k: es_t2[:, l, k, t * P:(t + 1) * P],
                        lambda r, k: c_t2[:, r, k, :], True, True).then_inc(s_ready, 1)

            def turn_a(b, t):
                pe.wait_ge(a_ready, b * NT + t + 1)
                if t == 0:
                    pe.wait_ge(et_copied, b * NT + NT)
                else:
                    pe.wait_ge(at_lo, b * NT + t)
                for k in range(NT):
                    last = pe.transpose(ps_t[:, k, :], a_sb[:, t % 2, k * P:(k + 1) * P], ident[:])
                last.then_inc(at_ps, 1)

            def attend(b, k):
                if k == 0:
                    pe.wait_ge(at_lo, b * NT + NT)
                    pe.wait_ge(lo_taken, W_CHUNKS + b * 2 * ND + 2 * ND)
                if k >= 2:
                    pe.wait_ge(ht_lo, b * ND + k - 1)
                product(ps_h[:, k % 2, :], lambda l, j: c_2[:, l, j, k * P:(k + 1) * P],
                        lambda r, j: a_t2[:, r, j, :], True, True).then_inc(ht_ps, 1)

            def row_weights(b, step):
                if step == 0:
                    pe.wait_ge(b_dve, b * 6 + 2)
                    pe.transpose(ps_b[0:1, 0:P], pmax[:], ident[:]).then_inc(b_pe, 1)
                elif step == 1:
                    pe.wait_ge(b_dve, b * 6 + 3)
                    pe.matmul(ps_b[:, 0:1], ones[0:1, :], gmax[:], start=True, stop=True).then_inc(b_pe, 1)
                elif step == 2:
                    pe.wait_ge(bexp_ready, b + 1)
                    pe.matmul(ps_b[:, 0:1], ones[:], bsum[:], start=True, stop=True).then_inc(b_pe, 1)
                else:
                    pe.wait_ge(b_dve, b * 6 + 6)
                    for t in range(NT):
                        last = pe.matmul(ps_b[:, t * P:(t + 1) * P], batt[:, t:t + 1].broadcast_to([P, P]), ident[:],
                                         start=True, stop=True)
                    last.then_inc(b_pe, 1)

            def feats(b, t, part):
                out = ps_f[:, t % 2, :]
                cols = slice(t * P, (t + 1) * P)
                if part == 0:
                    pe.wait_ge(wec_lo, b * ND + ND)
                    pe.wait_ge(et2_ready, b * 2 + 2)
                    if t >= 2:
                        pe.wait_ge(x1_ready, b * NT + t - 1)
                    product(out, lambda l, k: e_t2[:, l, k, cols], lambda r, k: wec[:, r, k, :], True, False)
                elif part == 1:
                    pe.wait_ge(ht_lo, b * ND + ND)
                    product(out, lambda l, k: h_t2[:, l, k, cols], lambda r, k: wh[:, r, k, :], False, False)
                else:
                    pe.wait_ge(eh_lo, b * ND + ND)
                    product(out, lambda l, k: eh_t2[:, l, k, cols], lambda r, k: weh[:, r, k, :], False,
                            True).then_inc(feat_ps, 1)

            def mid(b):
                for t in range(NT):
                    scores(b, t)
                    if t >= 1:
                        turn_a(b, t - 1)
                turn_a(b, NT - 1)
                row_weights(b, 0)
                attend(b, 0)
                row_weights(b, 1)
                row_weights(b, 2)
                attend(b, 1)
                row_weights(b, 3)
                attend(b, 2)
                attend(b, 3)

            def feats_first(b, turn):
                order = [(0, 0), (1, 0), (0, 1), (0, 2), (1, 1), (1, 2)]
                for n, (t, part) in enumerate(order):
                    feats(b, t, part)
                    if turn and n >= 2:
                        turn_e(b + 1, n - 2)

            def feats_last(b):
                for t in range(2, NT):
                    for part in range(3):
                        feats(b, t, part)

            for t in range(NT):
                turn_e(0, t)
            with pe.Fori(0, B - 1) as b:
                mid(b)
                feats_first(b, True)
                feats_last(b)
            mid(B - 1)
            feats_first(B - 1, False)
            feats_last(B - 1)


def expert_attention(nc, x1, g_ffn, wq, wk, w_vsd, wo, out):
    B, T, D = x1.shape
    NT, ND = T // P, D // P
    H, DH = 8, 64
    NV = wo.shape[0]
    E = NV // DH
    NL = H * E
    PAIRS = H // 2
    STEPS = H * NT
    KZ = -(-NV // P)
    REST = NV - (KZ - 1) * P
    SCALE = float(DH) ** -0.5
    SLOTS = NT
    W_CHUNKS = 3 * ND + KZ
    assert 2 * DH == P and w_vsd.shape[1] == NV + 2 * NL and wq.shape[1] == D and H * DH == D

    LAG = 2
    PV_AT = NT - 1 + LAG + 2
    TURN_O_AT = NT + PV_AT + NT - 1 + 2
    PAIR = 2 * NT
    LAST = PAIR * (PAIRS - 1) + TURN_O_AT
    PARTS = 2
    VALUE_AT = [None, 2, 6, 10, 15, 19, 23, 26]
    NORMALISE_AT = PAIR * (PAIRS - 1) - 4
    GATES_AT = PAIR * PAIRS + 1

    def shared(front):
        plan = [[] for _ in range(LAST + 1)]
        for p in range(PAIRS):
            plan[PAIR * p + TURN_O_AT].append(("turn_o", p, 0))
        for p in range(1, PAIRS):
            for part in range(PARTS):
                plan[PAIR * (p - 1) + LAG + part].append(("q", p, part))
                plan[PAIR * (p - 1) + LAG + PARTS + part].append(("k", p, part))
        if front:
            at = PAIR * (PAIRS - 1)
            for t in range(NT):
                plan[at + 2 * t].append(("turn_y", t, 0))
                plan[at + 2 * t + 1].append(("experts", t, 0))
            for part in range(PARTS):
                plan[at + 2 * NT + part].append(("q", 0, part))
                plan[at + 2 * NT + PARTS + part].append(("k", 0, part))
        return plan

    def ended(front, n):
        return [what[:2] for what in (shared(front)[n - 1] if 1 <= n <= LAST + 1 else [])
                if what[0] not in "qk" or what[2] == PARTS - 1]

    RING = 3
    AHEAD = [(what, t) for t in range(NT) for what in ("turn_y", "experts")] + [("q", 0), ("k", 0)]

    def uses(front):
        found = []
        for step in shared(front):
            for what in step:
                if what[:2] not in found:
                    found.append(what[:2])
        return found + [("turn_z", k) for k in range(KZ)] + [("result", t) for t in range(NT)]

    assert len(uses(True)) % RING == 0

    def bank_of(what, front, ahead):
        return (AHEAD.index(what) if ahead else len(AHEAD) + uses(front).index(what)) % RING

    with ExitStack() as mem:
        def sb(name, shape, dt=F32):
            return mem.enter_context(nc.sbuf_tensor(name, shape, dt))

        def sem(name):
            return mem.enter_context(nc.semaphore(name + "_2"))

        ident = sb("ident_2", [P, P])
        gate = sb("gate_2", [P, 1])
        gate_raw = sb("gate_raw_2", [P, 1])
        earlier = sb("earlier", [P, E, E], BF16)
        wq2 = sb("wq2", [P, 2, ND, D], F32R)
        wk2 = sb("wk2", [P, 2, ND, D], F32R)
        wx2 = sb("wx2", [P, 2, ND, NV + 2 * NL], F32R)
        wo2 = sb("wo2", [P, 2, KZ, D], F32R)
        stage = sb("stage_2", [P, SLOTS, D])
        y_t2 = sb("y_t2", [P, 2, ND, T], F32R)
        q_st = sb("q_st", [P, 2, 2, 2, T], F32R)
        k_st = sb("k_st", [P, 2, 2, T], F32R)
        xv = sb("xv", [P, NT, E, DH])
        logits = sb("logits", [P, 2, NT * H, E])
        above = sb("above", [P, NT * H, E, E], BF16)
        equal = sb("equal", [P, NT * H, E, E], BF16)
        rank = sb("rank", [P, 2, NT * H, E])
        pick = sb("pick", [P, 2, NT, H, E])
        sig = sb("sig", [P, NT * H, E])
        coef = sb("coef", [P, H, NT, E])
        v_acc = sb("v_acc", [P, 2, NT, DH])
        v_tmp = sb("v_tmp", [P, NT, DH])
        v_st = sb("v_st", [P, 4, NT, 2, DH], F32R)
        probs = sb("probs", [P, 2, T])
        pt2 = sb("pt2", [P, 2, 2, NT, T], F32R)
        o_tmp = sb("o_tmp", [P, T])
        o_t = sb("o_t", [P, 2, T])
        attn = sb("attn", [P, 2, NT, 2, DH])
        z = sb("z", [P, NT, KZ * P])
        z_tmp = sb("z_tmp", [P, NT, E, DH])
        z_t2 = sb("z_t2", [P, 2, KZ, T], F32R)
        x_res = sb("x_res", [P, NT, D])
        stats = sb("stats_2", [P, NT, 6])
        mean = sb("mean_2", [P, NT])
        work = sb("work_2", [P, 5, NT])
        rstd = sb("rstd_2", [P, NT])
        nmax = sb("nmax_2", [P, STEPS])
        den = sb("den_2", [P, H, NT])
        rden = sb("rden_2", [P, H, NT])

        ps_s = mem.enter_context(nc.psum_tensor("ps_s_2", [P, 2, T], F32))
        ps_p = mem.enter_context(nc.psum_tensor("ps_p_2", [P, 2, NT, P], F32))
        ps_o = mem.enter_context(nc.psum_tensor("ps_o_2", [P, T], F32))
        ps_r = mem.enter_context(nc.psum_tensor("ps_r_2", [P, RING, D], F32))

        const_loaded = sem("const_loaded")
        ident_ready = sem("ident_ready")
        gate_ready = sem("gate_ready")
        slot_loaded = [sem(f"slot_loaded{s}") for s in range(SLOTS)]
        xres_loaded = sem("xres_loaded")
        out_stored = sem("out_stored")
        hi_cast = sem("hi_cast")
        lo_taken = sem("lo_taken")
        stats_done = sem("stats_done")
        newton = sem("newton")
        y_ready = sem("y_ready")
        yt_ps = sem("yt_ps")
        yt_hi = sem("yt_hi")
        yt_lo = sem("yt_lo")
        ex_ps = sem("ex_ps")
        xv_ready = sem("xv_ready")
        logits_ready = sem("logits_ready")
        routed = sem("routed")
        sig_exp = sem("sig_exp")
        pick_ready = sem("pick_ready")
        q_ps = sem("q_ps")
        q_hi = sem("q_hi")
        q_lo = sem("q_lo")
        q_spread = [sem("q_spread0"), sem("q_spread1")]
        k_ps = sem("k_ps")
        k_hi = sem("k_hi")
        k_lo = sem("k_lo")
        v_steps = sem("v_steps")
        v_hi = sem("v_hi")
        v_ready = sem("v_ready")
        s_ready = sem("s_ready")
        nmax_ready = sem("nmax_ready")
        p_exp = sem("p_exp")
        pt_ps = sem("pt_ps")
        pt_hi = sem("pt_hi")
        pt_lo = sem("pt_lo")
        o_ps = sem("o_ps")
        o_half = sem("o_half")
        o_ready = sem("o_ready")
        to_ps = sem("to_ps")
        attn_ready = sem("attn_ready")
        rden_ready = sem("rden_ready")
        coef_ready = sem("coef_ready")
        z_steps = sem("z_steps")
        zt_ps = sem("zt_ps")
        zt_hi = sem("zt_hi")
        zt_lo = sem("zt_lo")
        res_ps = sem("res_ps")
        out_ready = sem("out_ready")

        x1_dram = x1.rearrange("b (t p) d -> b p t d", p=P)
        out_dram = out.rearrange("b (t p) d -> b p t d", p=P)

        def of(dram, b):
            return dram[bass.ds(b, 1)].rearrange("o p t d -> (o p) t d")

        def weight_chunk(n):
            k = n % ND
            rows = REST if n == W_CHUNKS - 1 else P
            src, dst = ((w_vsd, wx2), (wq, wq2), (wk, wk2), (wo, wo2))[n // ND]
            return src[k * P:k * P + rows, :], stage[0:rows, n % SLOTS, 0:src.shape[1]], dst[0:rows, :, k, :]

        def tile_slot(t):
            return (W_CHUNKS + t) % SLOTS

        def wait_chunk(eng, n):
            eng.wait_ge(slot_loaded[n % SLOTS], (n // SLOTS + 1) * 16)

        def wait_tile(eng, b, t):
            eng.wait_ge(slot_loaded[tile_slot(t)], b * 16 + ((W_CHUNKS + t) // SLOTS + 1) * 16)

        def heads_rows(a):
            own = slice(a * DH, a * DH + DH)
            return own, slice(DH - a * DH, P - a * DH)

        def wait_pair_slot(eng, b, p, ahead):
            if not ahead:
                eng.wait_ge(s_ready, b * STEPS + PAIR * (p - 1))

        block = mem.enter_context(nc.Block())

        @block.sync
        def _(sp):
            sp.dma_start(gate_raw[:], g_ffn.partition_broadcast(P)).then_inc(const_loaded, 16)
            for n in range(W_CHUNKS):
                if n >= SLOTS:
                    sp.wait_ge(lo_taken, n - SLOTS + 1)
                src, raw, _ = weight_chunk(n)
                sp.dma_start(raw, src).then_inc(slot_loaded[n % SLOTS], 16)

            def load_tiles(b, ahead):
                for t in range(NT):
                    if ahead:
                        sp.wait_ge(lo_taken, W_CHUNKS - SLOTS + t + 1)
                    else:
                        sp.wait_ge(yt_ps, b * NT - NT + t + 1)
                    sp.dma_start(stage[:, tile_slot(t), :], of(x1_dram, b)[:, t, :]).then_inc(
                        slot_loaded[tile_slot(t)], 16)

            def spread_q(b, p):
                sp.wait_ge(q_lo, b * H + 2 * p + 2)
                for a in range(2):
                    own, other = heads_rows(a)
                    sp.dma_start(q_st[other, p % 2, a, :, :].bitcast(F32),
                                 q_st[own, p % 2, a, :, :].bitcast(F32)).then_inc(q_spread[p % 2], 16)

            def sequence(b, front):
                if front:
                    load_tiles(b + 1, False)
                for p in range(1, PAIRS):
                    spread_q(b, p)
                if front:
                    spread_q(b + 1, 0)
                for t in range(NT):
                    sp.wait_ge(out_ready, b * NT + t + 1)
                    sp.dma_start(of(out_dram, b)[:, t, :], x_res[:, t, :]).then_inc(out_stored, 16)
                if front:
                    sp.wait_ge(out_stored, (b + 1) * NT * 16)
                    load_residual(b + 1)

            def load_residual(b):
                sp.dma_start(x_res[:], of(x1_dram, b)).then_inc(xres_loaded, 16)

            load_tiles(0, True)
            load_residual(0)
            spread_q(0, 0)
            with sp.Fori(0, B - 1) as b:
                sequence(b, True)
            sequence(B - 1, False)
            sp.wait_ge(out_stored, B * NT * 16)

        def mix_head(eng, b, h):
            p, a = h // 2, h % 2
            count = b * (2 * H - 1) + (2 * h - 1 if h else 0)
            zv = z[:, :, 0:NV].rearrange("p t (e k) -> p t e k", e=E)
            into = zv if h == 0 else z_tmp[:]
            eng.wait_ge(attn_ready, b * PAIRS + p + 1)
            eng.wait_ge(coef_ready, b * H + h + 1)
            if h:
                eng.wait_ge(z_steps, count)
            eng.tensor_tensor(into, attn[:, p % 2, :, a, :].unsqueeze(2).broadcast_to([P, NT, E, DH]),
                              coef[:, h, :, :].unsqueeze(3).broadcast_to([P, NT, E, DH]), ALU.mult).then_inc(z_steps, 1)
            if h:
                eng.wait_ge(z_steps, count + 1)
                eng.tensor_tensor(zv, zv, z_tmp[:], ALU.add).then_inc(z_steps, 1)

        POOL_HEADS = H // 2

        @block.gpsimd
        def _(pool):
            pool.memset(ident[:], 0.0).then_inc(ident_ready, 1)
            pool.memset(earlier[:], 1.0).then_inc(ident_ready, 1)
            pool.memset(z[:], 0.0).then_inc(ident_ready, 1)
            pool.memset(wo2[:, :, KZ - 1, :].bitcast(F32), 0.0).then_inc(ident_ready, 1)
            pool.wait_ge(ident_ready, 4)
            pool.affine_select(out=ident[:], in_=ident[:], compare_op=ALU.not_equal, fill=1.0, base=0,
                               pattern=[[-1, P]], channel_multiplier=1).then_inc(ident_ready, 1)
            pool.affine_select(out=earlier[:], in_=earlier[:], compare_op=ALU.is_gt, fill=0.0, base=0,
                               pattern=[[1, E], [-1, E]], channel_multiplier=0).then_inc(ident_ready, 1)
            for n in range(W_CHUNKS):
                _, raw, dst = weight_chunk(n)
                pool.wait_ge(hi_cast, n + 1)
                pool.tensor_tensor(dst[:, 1], raw, dst[:, 0].bitcast(F32),
                                   ALU.subtract).then_inc(lo_taken, 1)

            def mix_values(b, h, ahead):
                steps = 2 * E
                count = b * H * steps + h * steps
                if h == 0:
                    pool.wait_ge(pick_ready, b + 1)
                    pool.wait_ge(xv_ready, b * NT + NT)
                if h < POOL_HEADS and ahead:
                    pass
                else:
                    pool.wait_ge(o_ps, b * H + h - 3)
                acc = v_acc[:, h % 2]
                for e in range(E):
                    into = v_tmp[:] if e else acc
                    pool.tensor_tensor(into, xv[:, :, e, :],
                                       pick[:, 0, :, h, e:e + 1].broadcast_to([P, NT, DH]), ALU.mult).then_inc(v_steps, 1)
                    pool.wait_ge(v_steps, count + (2 * e if e else 1))
                    if e:
                        pool.tensor_tensor(acc, acc, v_tmp[:], ALU.add).then_inc(v_steps, 1)
                        pool.wait_ge(v_steps, count + 2 * e + 1)
                pool.wait_ge(v_hi, b * H + h + 1)
                pool.tensor_tensor(v_st[:, h % 4, :, 1, :], acc, v_st[:, h % 4, :, 0, :].bitcast(F32),
                                   ALU.subtract).then_inc(v_steps, 1)

            def sequence(b, front):
                for h in range(POOL_HEADS, H):
                    mix_values(b, h, False)
                for h in range(POOL_HEADS):
                    mix_head(pool, b, h)
                if front:
                    for h in range(POOL_HEADS):
                        mix_values(b + 1, h, False)

            for h in range(POOL_HEADS):
                mix_values(0, h, True)
            with pool.Fori(0, B - 1) as b:
                sequence(b, True)
            sequence(B - 1, False)

        @block.scalar
        def _(act):
            act.wait_ge(const_loaded, 16)
            act.activation(gate[:], gate_raw[:], ACT.Tanh).then_inc(gate_ready, 1)
            for n in range(W_CHUNKS):
                _, raw, dst = weight_chunk(n)
                wait_chunk(act, n)
                if n == W_CHUNKS - 1:
                    act.wait_ge(ident_ready, 4)
                act.activation(dst[:, 0], raw, ACT.Copy).then_inc(hi_cast, 1)

            def scores_exp(b, n):
                act.wait_ge(nmax_ready, b * STEPS + n + 1)
                if n >= 2:
                    act.wait_ge(pt_ps, b * STEPS + n - 1)
                act.activation(probs[:, n % 2, :], ps_s[:, n % 2, :], ACT.Exp, bias=nmax[:, n:n + 1],
                               accum_out=den[:, n // NT, n % NT:n % NT + 1]).then_inc(p_exp, 1)

            def probs_hi(b, n):
                h, t = n // NT, n % NT
                act.wait_ge(pt_ps, b * STEPS + n + 1)
                if t == 0 and h >= 2:
                    act.wait_ge(o_ps, b * H + h - 1)
                act.activation(pt2[:, h % 2, 0, :, t * P:(t + 1) * P], ps_p[:, n % 2], ACT.Copy).then_inc(pt_hi, 1)

            def value_hi(b, h, ahead):
                act.wait_ge(v_steps, b * H * 2 * E + (h + 1) * 2 * E - 1)
                act.activation(v_st[:, h % 4, :, 0, :], v_acc[:, h % 2], ACT.Copy).then_inc(v_hi, 1)

            def part_hi(b, what, front, ahead):
                name, n = what
                bank = bank_of(what, front, ahead)
                ps = ps_r[:, bank, :]
                if name == "turn_y":
                    act.wait_ge(yt_ps, b * NT + n + 1)
                    if n == 0 and not ahead:
                        act.wait_ge(k_ps, b * PAIRS)
                    act.activation(y_t2[:, 0, :, n * P:(n + 1) * P], ps.rearrange("p (k t) -> p k t", k=ND),
                                   ACT.Copy).then_inc(yt_hi, 1)
                elif name == "experts":
                    act.wait_ge(ex_ps, b * NT + n + 1)
                    if n == 0 and not ahead:
                        act.wait_ge(v_steps, b * H * 2 * E)
                        act.wait_ge(pick_ready, b)
                    act.activation(logits[:, :, n * H:(n + 1) * H, :],
                                   ps[:, NV:NV + 2 * NL].rearrange("p (s h e) -> p s h e", s=2, h=H),
                                   ACT.Copy).then_inc(logits_ready, 1)
                    act.activation(xv[:, n], ps[:, 0:NV].rearrange("p (e k) -> p e k", e=E),
                                   ACT.Copy).then_inc(xv_ready, 1)
                elif name == "q":
                    act.wait_ge(q_ps, b * PAIRS + n + 1)
                    wait_pair_slot(act, b, n, ahead)
                    for a in range(2):
                        own, _ = heads_rows(a)
                        act.activation(q_st[own, n % 2, a, 0, :], ps[own, :], ACT.Copy, scale=SCALE).then_inc(q_hi, 1)
                elif name == "k":
                    act.wait_ge(k_ps, b * PAIRS + n + 1)
                    wait_pair_slot(act, b, n, ahead)
                    for a in range(2):
                        own, _ = heads_rows(a)
                        act.activation(k_st[own, n % 2, a, :], ps[own, :], ACT.Copy).then_inc(k_hi, 1)
                elif name == "turn_o":
                    act.wait_ge(to_ps, b * PAIRS + n + 1)
                    if n >= 2:
                        act.wait_ge(z_steps, b * (2 * H - 1) + 4 * (n - 1) - 1)
                    act.activation(attn[:, n % 2], ps.rearrange("p (t a k) -> p t a k", t=NT, a=2),
                                   ACT.Copy).then_inc(attn_ready, 1)

            def out_half(b, h):
                act.wait_ge(o_ps, b * H + h + 1)
                if h:
                    act.wait_ge(o_ready, b * H + h)
                act.activation(o_tmp[DH:P, :], ps_o[0:DH, :], ACT.Copy).then_inc(o_half, 1)

            def gates_exp(b):
                act.wait_ge(logits_ready, b * NT + NT)
                act.activation(sig[:], logits[:, 0], ACT.Exp, scale=-1.0).then_inc(sig_exp, 1)

            def sequence(b, front):
                for n in range(LAST + 2):
                    if 0 <= n - LAG < STEPS:
                        probs_hi(b, n - LAG)
                    if n < STEPS:
                        scores_exp(b, n)
                    for h in range(H):
                        if n == NT * h + PV_AT + NT:
                            out_half(b, h)
                        if h and n == VALUE_AT[h]:
                            value_hi(b, h, False)
                    for what in ended(front, n):
                        part_hi(b if what[0] == "turn_o" or (what[0] in "qk" and what[1]) else b + 1, what, front, False)
                    if front and n == GATES_AT:
                        gates_exp(b + 1)
                for k in range(KZ):
                    act.wait_ge(zt_ps, b * KZ + k + 1)
                    act.activation(z_t2[:, 0, k, :], ps_r[:, bank_of(("turn_z", k), front, False), :],
                                   ACT.Copy).then_inc(zt_hi, 1)
                if front:
                    value_hi(b + 1, 0, False)

            for what in AHEAD:
                part_hi(0, what, True, True)
                if what == AHEAD[2 * NT - 1]:
                    gates_exp(0)
            value_hi(0, 0, True)
            with act.Fori(0, B - 1) as b:
                sequence(b, True)
            sequence(B - 1, False)

        @block.vector
        def _(dve):
            def normalise(b):
                for t in range(NT):
                    wait_tile(dve, b, t)
                    dve.bn_stats(stats[:, t, :], stage[:, tile_slot(t), :]).then_inc(stats_done, 1)
                dve.wait_ge(stats_done, b * NT + NT)
                mean_rstd(dve, stats[:], D, mean[:], work[:], rstd[:], newton, b * ROOT_STEPS)
                for t in range(NT):
                    tile = stage[:, tile_slot(t), :]
                    dve.tensor_scalar(tile, tile, mean[:, t:t + 1], rstd[:, t:t + 1], ALU.subtract,
                                      ALU.mult).then_inc(y_ready, 1)

            def row_max(b, n):
                dve.wait_ge(s_ready, b * STEPS + n + 1)
                dve.tensor_reduce(nmax[:, n:n + 1], ps_s[:, n % 2, :], AX_X, ALU.max, negate=True).then_inc(nmax_ready, 1)

            def probs_lo(b, n):
                h, t = n // NT, n % NT
                dve.wait_ge(pt_hi, b * STEPS + n + 1)
                dve.tensor_tensor(pt2[:, h % 2, 1, :, t * P:(t + 1) * P], ps_p[:, n % 2],
                                  pt2[:, h % 2, 0, :, t * P:(t + 1) * P].bitcast(F32), ALU.subtract).then_inc(pt_lo, 1)

            def part_lo(b, what, front, ahead):
                name, n = what
                bank = bank_of(what, front, ahead)
                ps = ps_r[:, bank, :]
                if name == "turn_y":
                    cols = slice(n * P, (n + 1) * P)
                    dve.wait_ge(yt_hi, b * NT + n + 1)
                    dve.tensor_tensor(y_t2[:, 1, :, cols], ps.rearrange("p (k t) -> p k t", k=ND),
                                      y_t2[:, 0, :, cols].bitcast(F32), ALU.subtract).then_inc(yt_lo, 1)
                elif name == "q":
                    for a in range(2):
                        own, _ = heads_rows(a)
                        dve.wait_ge(q_hi, b * H + 2 * n + a + 1)
                        dve.scalar_tensor_tensor(q_st[own, n % 2, a, 1, :], ps[own, :], SCALE,
                                                 q_st[own, n % 2, a, 0, :].bitcast(F32), ALU.mult,
                                                 ALU.subtract).then_inc(q_lo, 1)
                elif name == "k":
                    for a in range(2):
                        own, other = heads_rows(a)
                        dve.wait_ge(k_hi, b * H + 2 * n + a + 1)
                        dve.tensor_tensor(k_st[other, n % 2, a, :], ps[own, :], k_st[own, n % 2, a, :].bitcast(F32),
                                          ALU.subtract).then_inc(k_lo, 1)

            def out_sum(b, h):
                own, _ = heads_rows(h % 2)
                dve.wait_ge(o_half, b * H + h + 1)
                if h >= 4:
                    dve.wait_ge(to_ps, b * PAIRS + h // 2 - 1)
                dve.tensor_tensor(o_t[own, h // 2 % 2, :], ps_o[DH:P, :], o_tmp[DH:P, :], ALU.add).then_inc(o_ready, 1)

            def coefficients(b, h):
                dve.wait_ge(p_exp, b * STEPS + NT * h + NT)
                dve.reciprocal(rden[:, h, :], den[:, h, :]).then_inc(rden_ready, 1)
                dve.wait_ge(rden_ready, b * H + h + 1)
                dve.tensor_tensor(coef[:, h], pick[:, 1, :, h, :], rden[:, h, :].unsqueeze(2).broadcast_to([P, NT, E]),
                                  ALU.mult).then_inc(coef_ready, 1)

            def route(b, ahead):
                dve.wait_ge(logits_ready, b * NT + NT)
                dve.wait_ge(ident_ready, 6)
                if not ahead:
                    dve.wait_ge(v_steps, b * H * 2 * E)
                done = [b * ROUTE_STEPS]

                def after(instruction):
                    instruction.then_inc(routed, 1)
                    done[0] = done[0] + 1
                    dve.wait_ge(routed, done[0])

                wide = [P, NT * H, E, E]
                for s in range(2):
                    other = logits[:, s].unsqueeze(2).broadcast_to(wide)
                    this = logits[:, s].unsqueeze(3).broadcast_to(wide)
                    dve.tensor_tensor(above[:], other, this, ALU.is_gt).then_inc(routed, 1)
                    done[0] = done[0] + 1
                    after(dve.tensor_tensor(equal[:], other, this, ALU.is_equal))
                    after(dve.tensor_tensor(equal[:], equal[:], earlier[:].unsqueeze(1).broadcast_to(wide), ALU.mult))
                    after(dve.tensor_tensor(above[:], above[:], equal[:], ALU.add))
                    after(dve.tensor_reduce(rank[:, s], above[:], AX_X, ALU.add))
                flat = pick[:].rearrange("p s t h e -> p s (t h) e")
                after(dve.tensor_scalar(flat, rank[:], 1.5, None, ALU.is_lt))
                dve.wait_ge(sig_exp, b + 1)
                after(dve.tensor_scalar(sig[:], sig[:], 1.0, None, ALU.add))
                after(dve.reciprocal(sig[:], sig[:]))
                dve.tensor_tensor(flat[:, 0], flat[:, 0], sig[:], ALU.mult).then_inc(pick_ready, 1)

            ROUTE_STEPS = 13

            def sequence(b, front):
                for n in range(LAST + 2):
                    if n < STEPS:
                        row_max(b, n)
                    if 0 <= n - LAG < STEPS:
                        probs_lo(b, n - LAG)
                    for h in range(H):
                        if n == NT * h + PV_AT + NT:
                            out_sum(b, h)
                        if n == NT * h + NT:
                            coefficients(b, h)
                        if h >= POOL_HEADS and n == PAIR * (h // 2) + TURN_O_AT + 1:
                            mix_head(dve, b, h)
                    for what in ended(front, n):
                        part_lo(b if what[0] == "turn_o" or (what[0] in "qk" and what[1]) else b + 1, what, front, False)
                    if front and n == NORMALISE_AT:
                        normalise(b + 1)
                    if front and n == GATES_AT:
                        route(b + 1, False)
                for k in range(KZ):
                    bank = bank_of(("turn_z", k), front, False)
                    dve.wait_ge(zt_hi, b * KZ + k + 1)
                    dve.tensor_tensor(z_t2[:, 1, k, :], ps_r[:, bank, :], z_t2[:, 0, k, :].bitcast(F32),
                                      ALU.subtract).then_inc(zt_lo, 1)
                dve.wait_ge(xres_loaded, b * 16 + 16)
                dve.wait_ge(gate_ready, 1)
                for t in range(NT):
                    bank = bank_of(("result", t), front, False)
                    dve.wait_ge(res_ps, b * NT + t + 1)
                    dve.scalar_tensor_tensor(x_res[:, t, :], ps_r[:, bank, :], gate[:, 0:1], x_res[:, t, :],
                                             ALU.mult, ALU.add).then_inc(out_ready, 1)

            normalise(0)
            for what in AHEAD:
                part_lo(0, what, True, True)
                if what == AHEAD[2 * NT - 1]:
                    route(0, True)
            with dve.Fori(0, B - 1) as b:
                sequence(b, True)
            sequence(B - 1, False)

        @block.tensor
        def _(pe):
            pe.wait_ge(ident_ready, 6)

            def product(out, left, right, tiles):
                every = [(k, l, r) for k in range(tiles) for l, r in PASSES]
                for n, (k, l, r) in enumerate(every):
                    last = pe.matmul(out, left(l, k), right(r, k), start=n == 0, stop=n == len(every) - 1)
                return last

            def wait_read(b, what):
                name, n = what
                if name == "turn_y":
                    pe.wait_ge(yt_lo, b * NT + n + 1)
                elif name == "experts":
                    pe.wait_ge(logits_ready, b * NT + n + 1)
                    pe.wait_ge(xv_ready, b * NT + n + 1)
                elif name == "q":
                    pe.wait_ge(q_lo, b * H + 2 * n + 2)
                elif name == "k":
                    pe.wait_ge(k_lo, b * H + 2 * n + 2)
                elif name == "turn_o":
                    pe.wait_ge(attn_ready, b * PAIRS + n + 1)
                elif name == "turn_z":
                    pe.wait_ge(zt_lo, b * KZ + n + 1)
                else:
                    pe.wait_ge(out_ready, b * NT + n + 1)

            def owner(b, what):
                name, n = what
                return b + 1 if name in ("turn_y", "experts") or (name in "qk" and n == 0) else b

            def wait_bank(b, what, front, ahead):
                if ahead:
                    g = AHEAD.index(what)
                    if g >= RING:
                        wait_read(0, AHEAD[g - RING])
                    return
                order = uses(front)
                g = order.index(what)
                if g >= RING:
                    before = order[g - RING]
                    wait_read(owner(b, before), before)
                else:
                    for before in AHEAD[-RING:]:
                        wait_read(b, before)

            def shared_part(b, what, front, ahead):
                name, n, part = what
                own = 0 if ahead else owner(b, what[:2])
                ps = ps_r[:, bank_of(what[:2], front, ahead), :]
                if part == 0:
                    wait_bank(b, what[:2], front, ahead)
                if name == "turn_y":
                    pe.wait_ge(y_ready, own * NT + n + 1)
                    for k in range(ND):
                        last = pe.transpose(ps[:, k * P:(k + 1) * P], stage[:, tile_slot(n), k * P:(k + 1) * P], ident[:])
                    last.then_inc(yt_ps, 1)
                elif name == "experts":
                    pe.wait_ge(yt_lo, own * NT + n + 1)
                    if n == 0 and ahead:
                        pe.wait_ge(lo_taken, W_CHUNKS)
                    product(ps[:, 0:NV + 2 * NL], lambda l, k: y_t2[:, l, k, n * P:(n + 1) * P],
                            lambda r, k: wx2[:, r, k, :], ND).then_inc(ex_ps, 1)
                elif name in "qk":
                    if part == 0:
                        pe.wait_ge(yt_lo, own * NT + NT)
                    w2 = wq2 if name == "q" else wk2
                    every = [(k, l, r) for k in range(ND) for l, r in PASSES]
                    size = len(every) // PARTS
                    for m in range(part * size, part * size + size):
                        k, l, r = every[m]
                        last = pe.matmul(ps, w2[:, l, k, n * P:(n + 1) * P], y_t2[:, r, k, :], start=m == 0,
                                         stop=m == len(every) - 1)
                    if part == PARTS - 1:
                        last.then_inc(q_ps if name == "q" else k_ps, 1)
                elif name == "turn_o":
                    pe.wait_ge(o_ready, own * H + 2 * n + 2)
                    for t in range(NT):
                        last = pe.transpose(ps[:, t * P:(t + 1) * P], o_t[:, n % 2, t * P:(t + 1) * P], ident[:])
                    last.then_inc(to_ps, 1)

            def scores(b, n):
                h, t = n // NT, n % NT
                slot, a = h // 2 % 2, h % 2
                if n % PAIR == 0:
                    pe.wait_ge(q_spread[slot], b * (PAIRS // 2 * 32) + (h // 4 + 1) * 32)
                    pe.wait_ge(q_lo, b * H + h + 2)
                    pe.wait_ge(k_lo, b * H + h + 2)
                if n >= 2:
                    pe.wait_ge(p_exp, b * STEPS + n - 1)
                for part in range(2):
                    last = pe.matmul(ps_s[:, n % 2, :], q_st[:, slot, a, part, t * P:(t + 1) * P], k_st[:, slot, a, :],
                                     start=part == 0, stop=part == 1)
                last.then_inc(s_ready, 1)

            def turn_probs(b, n):
                pe.wait_ge(p_exp, b * STEPS + n + 1)
                if n >= 2:
                    pe.wait_ge(pt_lo, b * STEPS + n - 1)
                for k in range(NT):
                    last = pe.transpose(ps_p[:, n % 2, k, :], probs[:, n % 2, k * P:(k + 1) * P], ident[:])
                last.then_inc(pt_ps, 1)

            def values(b, h, k):
                if k == 0:
                    pe.wait_ge(pt_lo, b * STEPS + NT * h + NT)
                    pe.wait_ge(v_steps, b * H * 2 * E + (h + 1) * 2 * E)
                    if h:
                        pe.wait_ge(o_ready, b * H + h)
                for part in range(2):
                    last = pe.matmul(ps_o[:], v_st[:, h % 4, k, :, :], pt2[:, h % 2, part, k, :],
                                     start=k == 0 and part == 0, stop=k == NT - 1 and part == 1)
                if k == NT - 1:
                    last.then_inc(o_ps, 1)

            def sequence(b, front):
                plan = shared(front)
                for n in range(LAST + 1):
                    if n < STEPS:
                        scores(b, n)
                    if 0 <= n - LAG < STEPS:
                        turn_probs(b, n - LAG)
                    m = n - PV_AT
                    if 0 <= m < STEPS:
                        values(b, m // NT, m % NT)
                    for what in plan[n]:
                        shared_part(b, what, front, False)
                pe.wait_ge(z_steps, b * (2 * H - 1) + 2 * H - 1)
                for k in range(KZ):
                    what = ("turn_z", k)
                    wait_bank(b, what, front, False)
                    for t in range(NT):
                        last = pe.transpose(ps_r[:, bank_of(what, front, False), t * P:(t + 1) * P],
                                            z[:, t, k * P:(k + 1) * P], ident[:])
                    last.then_inc(zt_ps, 1)
                for t in range(NT):
                    what = ("result", t)
                    wait_bank(b, what, front, False)
                    pe.wait_ge(zt_lo, b * KZ + KZ)
                    product(ps_r[:, bank_of(what, front, False), :], lambda l, k: z_t2[:, l, k, t * P:(t + 1) * P],
                            lambda r, k: wo2[:, r, k, :], KZ).then_inc(res_ps, 1)

            for what in AHEAD:
                for part in range(PARTS if what[0] in "qk" else 1):
                    shared_part(0, (*what, part), True, True)
            with pe.Fori(0, B - 1) as b:
                sequence(b, True)
            sequence(B - 1, False)


def program(nc, x, ctx, ctx_t, g_xattn, g_ffn, w_sim, w_sim_cols, b_sim, w_qv, b_qv, wq, wk, w_vsd, wo, x1, out):
    cross_attention(nc, x, ctx, ctx_t, g_xattn, w_sim, w_sim_cols, b_sim, w_qv, b_qv, x1)
    expert_attention(nc, x1, g_ffn, wq, wk, w_vsd, wo, out)


def kernel(x, ctx_1024, g_xattn, g_ffn, L0_xattn_w_sim, L0_xattn_b_sim, L0_xattn_W_qv, L0_xattn_b_qv,
           L0_ffn_Wq, L0_ffn_Wk, L0_ffn_Ws, L0_ffn_Wd, L0_ffn_Wv, L0_ffn_Wo):
    import numpy as np
    import concourse.bacc as bacc
    from concourse.bass_utils import run_bass_kernel_spmd

    x, ctx = np.asarray(x), np.asarray(ctx_1024)
    w_sim, wv, wo = np.asarray(L0_xattn_w_sim), np.asarray(L0_ffn_Wv), np.asarray(L0_ffn_Wo)
    D = x.shape[2]
    arrays = {
        "x": x,
        "ctx": ctx,
        "ctx_t": ctx.transpose(0, 2, 1),
        "g_xattn": np.asarray(g_xattn),
        "g_ffn": np.asarray(g_ffn),
        "w_sim": w_sim,
        "w_sim_cols": w_sim.reshape(3, D // P, P).transpose(2, 0, 1),
        "b_sim": np.asarray(L0_xattn_b_sim),
        "w_qv": np.asarray(L0_xattn_W_qv),
        "b_qv": np.asarray(L0_xattn_b_qv),
        "wq": np.asarray(L0_ffn_Wq),
        "wk": np.asarray(L0_ffn_Wk),
        "w_vsd": np.concatenate([wv.transpose(1, 0, 2).reshape(D, -1), np.asarray(L0_ffn_Ws),
                                 np.asarray(L0_ffn_Wd)], axis=1),
        "wo": wo.reshape(-1, D),
    }
    nc = bacc.Bacc("TRN2", target_bir_lowering=False, num_devices=1)
    feed, args = {}, {}
    for name, a in arrays.items():
        a = np.ascontiguousarray(a)
        feed[f"in_{name}"] = a
        args[name] = nc.dram_tensor(f"in_{name}", a.shape, mybir.dt.from_np(a.dtype), kind="ExternalInput").ap()
    out = nc.dram_tensor("out_dram", x.shape, F32, kind="ExternalOutput").ap()
    x1 = nc.dram_tensor("x1_dram", x.shape, F32, kind="Internal").ap()
    program(nc, **args, x1=x1, out=out)
    r = run_bass_kernel_spmd(nc, [feed], core_ids=[0])
    return r.results[0]["out_dram"]
```

```python
from contextlib import ExitStack

import concourse.bass as bass
from concourse import mybir

F32 = mybir.dt.float32
F32R = mybir.dt.float32r
I32 = mybir.dt.int32
BF16 = mybir.dt.bfloat16
ALU = mybir.AluOpType
ACT = mybir.ActivationFunctionType
AX_X = mybir.AxisListType.X

P = 128
EPS = 1e-5
PASSES = ((0, 0), (0, 1), (1, 0))


def mean_rstd(dve, part, stats, size, mean, work, rstd, done, count):
    both, diff, var, guess = work[:, 0:2], work[:, 2], work[:, 3], work[:, 4]

    def written(n):
        dve.wait_ge(done, count + n)

    if part == 0:
        by_kind = stats.rearrange("p t k -> p k t")
        dve.tensor_tensor(both, by_kind[:, 1:3], by_kind[:, 4:6], ALU.add).then_inc(done, 1)
        dve.tensor_tensor(diff, by_kind[:, 1], by_kind[:, 4], ALU.subtract).then_inc(done, 1)
        written(2)
        dve.tensor_scalar(mean, both[:, 0], 0.5, None, ALU.mult).then_inc(done, 1)
        dve.tensor_scalar(var, both[:, 1], 1.0 / size, EPS, ALU.mult, ALU.add).then_inc(done, 1)
        dve.tensor_tensor(diff, diff, diff, ALU.mult).then_inc(done, 1)
        written(5)
        dve.scalar_tensor_tensor(var, diff, 0.25, var, ALU.mult, ALU.add).then_inc(done, 1)
    elif part == 1:
        written(6)
        dve.tensor_scalar(guess.bitcast(I32), var.bitcast(I32), 1, None, ALU.logical_shift_right).then_inc(done, 1)
        written(7)
        dve.tensor_scalar(rstd.bitcast(I32), guess.bitcast(I32), -1.0, float(0x5F3759DF), ALU.mult,
                          ALU.add).then_inc(done, 1)
    else:
        n = 3 * part + 2
        written(n)
        dve.tensor_tensor(guess, rstd, rstd, ALU.mult).then_inc(done, 1)
        written(n + 1)
        dve.scalar_tensor_tensor(guess, guess, -0.5, var, ALU.mult, ALU.mult).then_inc(done, 1)
        written(n + 2)
        dve.scalar_tensor_tensor(rstd, guess, 1.5, rstd, ALU.add, ALU.mult).then_inc(done, 1)


ROOT_PARTS = 5
ROOT_STEPS = 17


def cross_attention(nc, x, ctx, ctx_t, g_xattn, w_sim, w_sim_cols, b_sim, w_qv, b_qv, x1):
    B, T, D = x.shape
    NT, ND = T // P, D // P
    assert NT == ND == 4

    with ExitStack() as mem:
        def sb(name, shape, dt=F32):
            return mem.enter_context(nc.sbuf_tensor(name, shape, dt))

        def sem(name):
            return mem.enter_context(nc.semaphore(name))

        ident = sb("ident", [P, P])
        ones = sb("ones", [P, P])
        w1_row = sb("w1_row", [P, D])
        w_cols = sb("w_cols", [P, 3, ND])
        w2_col, w3_col = w_cols[:, 1, :], w_cols[:, 2, :]
        bsim_col = sb("bsim_col", [P, 1])
        gate = sb("gate", [P, 1])
        gate_raw = sb("gate_raw", [P, 1])
        bias_row = sb("bias_row", [P, D])
        we_raw = sb("we_raw", [P, ND, D])
        wc_raw = sb("wc_raw", [P, ND, D])
        wh = sb("wh", [P, 2, ND, D], F32R)
        weh = sb("weh", [P, 2, ND, D], F32R)
        wec = sb("wec", [P, 2, ND, D], F32R)
        stage = sb("stage", [P, NT, D])
        x_sb = sb("x_sb", [P, NT, D])
        e_sb = sb("e_sb", [P, 2, D])
        e_t = sb("e_t", [P, ND, T])
        e_t2 = sb("e_t2", [P, 2, ND, T], F32R)
        es_t2 = sb("es_t2", [P, 2, ND, T], F32R)
        a_t2 = es_t2
        c_t2 = sb("c_t2", [P, 2, ND, T], F32R)
        c_2 = sb("c_2", [P, 2, NT, D], F32R)
        a_sb = sb("a_sb", [P, 2, T])
        junk = a_sb
        h_t2 = sb("h_t2", [P, 2, ND, T], F32R)
        eh_t2 = sb("eh_t2", [P, 2, ND, T], F32R)
        tmp = sb("tmp", [P, ND, T])
        stats = sb("stats", [P, NT, 6])
        mean = sb("mean", [P, NT])
        work = sb("work", [P, 5, NT])
        rstd = sb("rstd", [P, NT])
        ew1 = sb("ew1", [P, NT])
        nmax = sb("nmax", [P, NT])
        den = sb("den", [P, NT])
        rden = sb("rden", [P, NT])
        mtot = sb("mtot", [P, NT])
        pmax = sb("pmax", [P, 1])
        gmax = sb("gmax", [1, 1])
        ngmax = sb("ngmax", [P, 1])
        bexp = sb("bexp", [P, NT])
        bsum = sb("bsum", [P, 1])
        rtot = sb("rtot", [P, 1])
        batt = sb("batt", [P, NT])
        hc = sb("hc", [P, ND])

        ps_s = mem.enter_context(nc.psum_tensor("ps_s", [P, 2, T], F32))
        ps_h = mem.enter_context(nc.psum_tensor("ps_h", [P, 2, T], F32))
        ps_f = mem.enter_context(nc.psum_tensor("ps_f", [P, 2, D], F32))
        ps_t = mem.enter_context(nc.psum_tensor("ps_t", [P, 4, P], F32))
        ps_b = mem.enter_context(nc.psum_tensor("ps_b", [P, T], F32))

        const_loaded = sem("const_loaded")
        wh_loaded = sem("wh_loaded")
        weh_loaded = sem("weh_loaded")
        wraw_loaded = sem("wraw_loaded")
        ident_ready = sem("ident_ready")
        gate_ready = sem("gate_ready")
        bias_ready = sem("bias_ready")
        slot_loaded = [sem(f"slot_loaded{t}") for t in range(NT)]
        res_loaded = sem("res_loaded")
        x1_stored = sem("x1_stored")
        w_hi = sem("w_hi")
        w_lo = sem("w_lo")
        ct_hi = sem("ct_hi")
        ct_lo = sem("ct_lo")
        c_hi = sem("c_hi")
        c_lo = sem("c_lo")
        stats_done = sem("stats_done")
        newton = sem("newton")
        e_ready = sem("e_ready")
        ew1_ready = sem("ew1_ready")
        et_ps = sem("et_ps")
        et_copied = sem("et_copied")
        es_ready = sem("es_ready")
        es_hi = sem("es_hi")
        es_lo = sem("es_lo")
        et_hi = sem("et_hi")
        et_lo = sem("et_lo")
        s_ready = sem("s_ready")
        nmax_ready = sem("nmax_ready")
        a_exp = sem("a_exp")
        rden_ready = sem("rden_ready")
        a_ready = sem("a_ready")
        at_ps = sem("at_ps")
        at_hi = sem("at_hi")
        at_lo = sem("at_lo")
        ht_ps = sem("ht_ps")
        ht_hi = sem("ht_hi")
        ht_lo = sem("ht_lo")
        eh_ready = sem("eh_ready")
        eh_hi = sem("eh_hi")
        eh_lo = sem("eh_lo")
        b_dve = sem("b_dve")
        b_pe = sem("b_pe")
        bexp_ready = sem("bexp_ready")
        hc_ready = sem("hc_ready")
        wec_ready = sem("wec_ready")
        wec_hi = sem("wec_hi")
        wec_lo = sem("wec_lo")
        feat_ps = sem("feat_ps")
        x1_ready = sem("x1_ready")
        xb_ready = sem("xb_ready")

        w_blocks = w_qv.rearrange("(m k p) n -> m p k n", m=4, p=P)
        x_dram = x.rearrange("b (t p) d -> b p t d", p=P)
        c_dram = ctx.rearrange("b (t p) d -> b p t d", p=P)
        ct_dram = ctx_t.rearrange("b (k p) j -> b p k j", p=P)
        x1_dram = x1.rearrange("b (t p) d -> b p t d", p=P)

        def of(dram, b):
            return dram[bass.ds(b, 1)].rearrange("o p t d -> (o p) t d")

        def cast_hi(act, pair, k, operand):
            return act.activation(pair[:, 0, k, :], operand[:, k, :], ACT.Copy)

        def take_lo(eng, pair, k, operand):
            return eng.tensor_tensor(pair[:, 1, k, :], operand[:, k, :], pair[:, 0, k, :].bitcast(F32), ALU.subtract)

        def stage_loaded(eng, b, t, use):
            eng.wait_ge(slot_loaded[t], b * (3 * 16) + (use + 1) * 16)

        wh_raw, weh_raw = x_sb, wc_raw

        block = mem.enter_context(nc.Block())

        @block.sync
        def _(sp):
            def load_x(b, first=False):
                for t in range(NT):
                    if not first:
                        sp.wait_ge(c_lo, b * NT - NT + t + 1)
                    sp.dma_start(stage[:, t, :], of(x_dram, b)[:, t, :]).then_inc(slot_loaded[t], 16)

            def load_ctx(b):
                for k in range(ND):
                    sp.wait_ge(e_ready, b * NT + k + 1)
                    sp.dma_start(stage[:, k, :], of(ct_dram, b)[:, k, :]).then_inc(slot_loaded[k], 16)
                for t in range(NT):
                    sp.wait_ge(ct_lo, b * ND + t + 1)
                    sp.dma_start(stage[:, t, :], of(c_dram, b)[:, t, :]).then_inc(slot_loaded[t], 16)

            def load_residual(b):
                sp.dma_start(x_sb[:], of(x_dram, b)).then_inc(res_loaded, 16)

            def store(b, t):
                sp.wait_ge(x1_ready, b * NT + t + 1)
                sp.dma_start(of(x1_dram, b)[:, t, :], x_sb[:, t, :]).then_inc(x1_stored, 16)

            def next_loads(b, more):
                load_ctx(b + 1)
                for t in range(NT - 1):
                    store(b, t)
                if more:
                    load_x(b + 2)
                store(b, NT - 1)
                sp.wait_ge(x1_stored, (b + 1) * NT * 16)
                load_residual(b + 1)

            load_x(0, True)
            sp.dma_start(w1_row[:], w_sim[0:D].partition_broadcast(P)).then_inc(const_loaded, 16)
            sp.dma_start(w_cols[:], w_sim_cols).then_inc(const_loaded, 16)
            sp.dma_start(gate_raw[:], g_xattn.partition_broadcast(P)).then_inc(const_loaded, 16)
            sp.dma_start(bsim_col[:], b_sim.partition_broadcast(P)).then_inc(const_loaded, 16)
            sp.dma_start(bias_row[:], b_qv.partition_broadcast(P)).then_inc(const_loaded, 16)
            sp.dma_start(wh_raw[:], w_blocks[1]).then_inc(wh_loaded, 16)
            load_ctx(0)
            sp.dma_start(weh_raw[:], w_blocks[2]).then_inc(weh_loaded, 16)
            sp.dma_start(we_raw[:], w_blocks[0]).then_inc(wraw_loaded, 16)
            load_x(1)
            sp.wait_ge(w_lo, ND)
            load_residual(0)
            sp.wait_ge(w_lo, 2 * ND)
            sp.dma_start(wc_raw[:], w_blocks[3]).then_inc(wraw_loaded, 16)
            with sp.Fori(0, B - 2) as b:
                next_loads(b, True)
            next_loads(B - 2, False)
            for t in range(NT):
                store(B - 1, t)
            sp.wait_ge(x1_stored, B * NT * 16)

        @block.gpsimd
        def _(pool):
            pool.memset(ident[:], 0.0).then_inc(ident_ready, 1)
            pool.memset(ones[:], 1.0).then_inc(ident_ready, 1)
            pool.wait_ge(ident_ready, 2)
            pool.affine_select(out=ident[:], in_=ident[:], compare_op=ALU.not_equal, fill=1.0, base=0,
                               pattern=[[-1, P]], channel_multiplier=1).then_inc(ident_ready, 1)

            def ctx_lo(b):
                for t in range(NT):
                    pool.wait_ge(c_hi, b * NT + t + 1)
                    take_lo(pool, c_2, t, stage).then_inc(c_lo, 1)

            def rest(b):
                for k in range(ND):
                    pool.wait_ge(et_hi, b * ND + k + 1)
                    take_lo(pool, e_t2, k, e_t).then_inc(et_lo, 1)
                for k in range(ND):
                    pool.wait_ge(eh_hi, b * ND + k + 1)
                    take_lo(pool, eh_t2, k, tmp).then_inc(eh_lo, 1)
                pool.wait_ge(res_loaded, b * 16 + 16)
                pool.wait_ge(bias_ready, 1)
                pool.tensor_tensor(x_sb[:], x_sb[:], bias_row[:].unsqueeze(1).broadcast_to([P, NT, D]),
                                   ALU.add).then_inc(xb_ready, 1)
                for k in range(ND):
                    pool.wait_ge(wec_hi, b * ND + k + 1)
                    take_lo(pool, wec, k, tmp).then_inc(wec_lo, 1)

            ctx_lo(0)
            for n in range(2 * ND):
                pool.wait_ge(w_hi, n + 1)
                take_lo(pool, *((wh, n, wh_raw) if n < ND else (weh, n - ND, weh_raw))).then_inc(w_lo, 1)
            with pool.Fori(0, B - 1) as b:
                rest(b)
                ctx_lo(b + 1)
            rest(B - 1)

        @block.scalar
        def _(act):
            act.wait_ge(const_loaded, 5 * 16)
            act.activation(gate[:], gate_raw[:], ACT.Tanh).then_inc(gate_ready, 1)

            def copy_e(b, t):
                act.wait_ge(et_ps, b * NT + t + 1)
                act.activation(e_t[:, :, t * P:(t + 1) * P], ps_t[:], ACT.Copy).then_inc(et_copied, 1)

            def ctx_t_hi(b, slots):
                for k in range(slots.start, slots.stop):
                    stage_loaded(act, b, k, 1)
                    cast_hi(act, c_t2, k, stage).then_inc(ct_hi, 1)

            def es_ctx_hi(b):
                for k in range(ND):
                    act.wait_ge(es_ready, b * ND + k + 1)
                    act.activation(es_t2[:, 0, k, :], tmp[:, k, :], ACT.Copy).then_inc(es_hi, 1)
                for t in range(NT):
                    stage_loaded(act, b, t, 2)
                    cast_hi(act, c_2, t, stage).then_inc(c_hi, 1)

            def weights_hi(pair, raw, loaded):
                act.wait_ge(loaded, 16)
                for k in range(ND):
                    cast_hi(act, pair, k, raw).then_inc(w_hi, 1)

            def softmax_exp(b, t):
                act.wait_ge(nmax_ready, b * NT + t + 1)
                if t >= 2:
                    act.wait_ge(at_ps, b * NT + t - 1)
                act.activation(a_sb[:, t % 2, :], ps_s[:, t % 2, :], ACT.Exp, bias=nmax[:, t:t + 1],
                               accum_out=den[:, t:t + 1]).then_inc(a_exp, 1)

            def probs_hi(b, t):
                act.wait_ge(at_ps, b * NT + t + 1)
                act.activation(a_t2[:, 0, :, t * P:(t + 1) * P], ps_t[:], ACT.Copy).then_inc(at_hi, 1)

            def softmax(b):
                for t in range(NT):
                    softmax_exp(b, t)
                    probs_hi(b, t)

            def attended(b, first):
                if not first:
                    act.wait_ge(feat_ps, b * NT)
                for k in range(ND):
                    act.activation(e_t2[:, 0, k, :], e_t[:, k, :], ACT.Copy).then_inc(et_hi, 1)
                for k in range(ND):
                    act.wait_ge(ht_ps, b * ND + k + 1)
                    act.activation(h_t2[:, 0, k, :], ps_h[:, k % 2, :], ACT.Copy).then_inc(ht_hi, 1)
                    act.wait_ge(eh_ready, b * ND + k + 1)
                    act.activation(eh_t2[:, 0, k, :], tmp[:, k, :], ACT.Copy).then_inc(eh_hi, 1)
                    if k == 1:
                        act.wait_ge(b_dve, b * 6 + 4)
                        act.activation(bexp[:], mtot[:], ACT.Exp, bias=ngmax[:, 0:1],
                                       accum_out=bsum[:, 0:1]).then_inc(bexp_ready, 1)
                for k in range(ND):
                    act.wait_ge(wec_ready, b * ND + k + 1)
                    act.activation(wec[:, 0, k, :], tmp[:, k, :], ACT.Copy).then_inc(wec_hi, 1)

            def front(b):
                for t in range(NT):
                    copy_e(b, t)
                    if t == 1:
                        ctx_t_hi(b, slice(0, 2))
                ctx_t_hi(b, slice(2, ND))
                es_ctx_hi(b)

            front(0)
            weights_hi(wh, wh_raw, wh_loaded)
            softmax(0)
            weights_hi(weh, weh_raw, weh_loaded)
            attended(0, True)
            with act.Fori(0, B - 1) as b:
                act.wait_ge(hc_ready, b * ND + ND)
                act.wait_ge(et_lo, b * ND + ND)
                front(b + 1)
                softmax(b + 1)
                attended(b + 1, False)

        @block.vector
        def _(dve):
            def row_stats(b):
                for t in range(NT):
                    stage_loaded(dve, b, t, 0)
                    dve.bn_stats(stats[:, t, :], stage[:, t, :]).then_inc(stats_done, 1)

            def root(b, part):
                if part == 0:
                    dve.wait_ge(stats_done, b * NT + NT)
                mean_rstd(dve, part, stats[:], D, mean[:], work[:], rstd[:], newton, b * ROOT_STEPS)

            def normalise_x(b, t):
                if t == 0:
                    dve.wait_ge(newton, b * ROOT_STEPS + ROOT_STEPS)
                if t >= 2:
                    dve.wait_ge(et_ps, b * NT + t - 1)
                    dve.wait_ge(ew1_ready, b * (NT + 1) + t - 1)
                dve.tensor_scalar(e_sb[:, t % 2, :], stage[:, t, :], mean[:, t:t + 1], rstd[:, t:t + 1],
                                  ALU.subtract, ALU.mult).then_inc(e_ready, 1)
                dve.wait_ge(e_ready, b * NT + t + 1)
                dve.tensor_tensor_reduce(out=junk[:, t % 2, :], in0=e_sb[:, t % 2, :], in1=w1_row[:], scale=1.0,
                                         scalar=0.0, op0=ALU.mult, op1=ALU.add,
                                         accum_out=ew1[:, t:t + 1]).then_inc(ew1_ready, 1)

            def ctx_t_lo(b, slots):
                for k in range(slots.start, slots.stop):
                    dve.wait_ge(ct_hi, b * ND + k + 1)
                    take_lo(dve, c_t2, k, stage).then_inc(ct_lo, 1)

            def scaled_e(b, k, first):
                if not first:
                    dve.wait_ge(wec_lo, b * ND - ND + k + 1)
                dve.tensor_scalar(tmp[:, k, :], e_t[:, k, :], w3_col[:, k:k + 1], w2_col[:, k:k + 1],
                                  ALU.mult, ALU.add).then_inc(es_ready, 1)

            def scaled_e_lo(b, k):
                dve.wait_ge(es_hi, b * ND + k + 1)
                take_lo(dve, es_t2, k, tmp).then_inc(es_lo, 1)

            def front(b, first):
                for t in range(2, NT):
                    normalise_x(b, t)
                ctx_t_lo(b, slice(0, 2))
                dve.wait_ge(ew1_ready, b * (NT + 1) + NT)
                dve.tensor_scalar(ew1[:], ew1[:], bsim_col[:, 0:1], None, ALU.add).then_inc(ew1_ready, 1)
                if not first:
                    residual(b - 1, 0)
                    residual(b - 1, 1)
                ctx_t_lo(b, slice(2, ND))
                dve.wait_ge(et_copied, b * NT + NT)
                for k in range(ND):
                    scaled_e(b, k, first)
                    if k >= 1:
                        scaled_e_lo(b, k - 1)
                scaled_e_lo(b, ND - 1)

            def row_max(b, t):
                dve.wait_ge(s_ready, b * NT + t + 1)
                dve.tensor_reduce(nmax[:, t:t + 1], ps_s[:, t % 2, :], AX_X, ALU.max, negate=True).then_inc(
                    nmax_ready, 1)

            def normalise(b, t):
                dve.wait_ge(a_exp, b * NT + t + 1)
                dve.reciprocal(rden[:, t:t + 1], den[:, t:t + 1]).then_inc(rden_ready, 1)
                dve.wait_ge(rden_ready, b * NT + t + 1)
                dve.tensor_scalar(a_sb[:, t % 2, :], a_sb[:, t % 2, :], rden[:, t:t + 1], None,
                                  ALU.mult).then_inc(a_ready, 1)

            def probs_lo(b, t):
                dve.wait_ge(at_hi, b * NT + t + 1)
                dve.tensor_tensor(a_t2[:, 1, :, t * P:(t + 1) * P], ps_t[:],
                                  a_t2[:, 0, :, t * P:(t + 1) * P].bitcast(F32), ALU.subtract).then_inc(at_lo, 1)

            def softmax(b, first):
                for t in range(NT):
                    row_max(b, t)
                    normalise(b, t)
                    if t == NT - 1:
                        dve.wait_ge(nmax_ready, b * NT + NT)
                        dve.scalar_tensor_tensor(mtot[:], nmax[:], -1.0, ew1[:], ALU.mult, ALU.add).then_inc(b_dve, 1)
                    probs_lo(b, t)
                    if t == 0 and not first:
                        residual(b - 1, 2)
                dve.wait_ge(b_dve, b * 6 + 1)
                dve.reduce_max(pmax[:], mtot[:], AX_X).then_inc(b_dve, 1)
                if not first:
                    residual(b - 1, NT - 1)

            def attended(b, more):
                if more:
                    row_stats(b + 1)
                    root(b + 1, 0)
                for k in range(ND):
                    dve.wait_ge(ht_hi, b * ND + k + 1)
                    dve.tensor_tensor(tmp[:, k, :], ps_h[:, k % 2, :], e_t[:, k, :], ALU.mult).then_inc(eh_ready, 1)
                    dve.tensor_tensor(h_t2[:, 1, k, :], ps_h[:, k % 2, :], h_t2[:, 0, k, :].bitcast(F32),
                                      ALU.subtract).then_inc(ht_lo, 1)
                    if k == 0:
                        dve.wait_ge(b_pe, b * 4 + 1)
                        dve.tensor_reduce(gmax[:], ps_b[0:1, 0:P], AX_X, ALU.max, negate=True).then_inc(b_dve, 1)
                    elif k == 1:
                        dve.wait_ge(b_pe, b * 4 + 2)
                        dve.tensor_copy(ngmax[:], ps_b[:, 0:1]).then_inc(b_dve, 1)
                    elif k == 2:
                        dve.wait_ge(b_pe, b * 4 + 3)
                        dve.reciprocal(rtot[:], ps_b[:, 0:1]).then_inc(b_dve, 1)
                        dve.wait_ge(b_dve, b * 6 + 5)
                        dve.tensor_scalar(batt[:], bexp[:], rtot[:, 0:1], None, ALU.mult).then_inc(b_dve, 1)
                    if more:
                        root(b + 1, k + 1)
                dve.wait_ge(b_pe, b * 4 + 4)
                for k in range(ND):
                    if k >= 2:
                        dve.wait_ge(hc_ready, b * ND + k - 1)
                    dve.tensor_tensor_reduce(out=junk[:, k % 2, :], in0=e_t[:, k, :], in1=ps_b[:], scale=1.0, scalar=0.0,
                                             op0=ALU.mult, op1=ALU.add, accum_out=hc[:, k:k + 1]).then_inc(hc_ready, 1)
                dve.wait_ge(wraw_loaded, 2 * 16)
                for k in range(ND):
                    dve.wait_ge(hc_ready, b * ND + k + 1)
                    dve.wait_ge(eh_lo, b * ND + k + 1)
                    dve.scalar_tensor_tensor(tmp[:, k, :], wc_raw[:, k, :], hc[:, k:k + 1], we_raw[:, k, :],
                                             ALU.mult, ALU.add).then_inc(wec_ready, 1)
                if more:
                    normalise_x(b + 1, 0)
                    normalise_x(b + 1, 1)

            def residual(b, t):
                if t == 0:
                    dve.wait_ge(xb_ready, b + 1)
                dve.wait_ge(feat_ps, b * NT + t + 1)
                dve.scalar_tensor_tensor(x_sb[:, t, :], ps_f[:, t % 2, :], gate[:, 0:1], x_sb[:, t, :],
                                         ALU.mult, ALU.add).then_inc(x1_ready, 1)

            row_stats(0)
            for part in range(ROOT_PARTS):
                root(0, part)
            dve.wait_ge(const_loaded, 5 * 16)
            normalise_x(0, 0)
            normalise_x(0, 1)
            front(0, True)
            dve.wait_ge(gate_ready, 1)
            dve.tensor_scalar(bias_row[:], bias_row[:], gate[:, 0:1], None, ALU.mult).then_inc(bias_ready, 1)
            softmax(0, True)
            with dve.Fori(0, B - 1) as b:
                attended(b, True)
                front(b + 1, False)
                softmax(b + 1, False)
            attended(B - 1, False)
            for t in range(NT):
                residual(B - 1, t)

        @block.tensor
        def _(pe):
            pe.wait_ge(ident_ready, 3)

            def product(out, left, right, start, stop):
                n = 0
                for k in range(ND):
                    for l, r in PASSES:
                        n += 1
                        last = pe.matmul(out, left(l, k), right(r, k), start=start and n == 1,
                                         stop=stop and n == ND * len(PASSES))
                return last

            def turn_e(b, t):
                pe.wait_ge(e_ready, b * NT + t + 1)
                if t:
                    pe.wait_ge(et_copied, b * NT + t)
                for k in range(ND):
                    last = pe.transpose(ps_t[:, k, :], e_sb[:, t % 2, k * P:(k + 1) * P], ident[:])
                last.then_inc(et_ps, 1)

            def scores(b, t):
                if t == 0:
                    pe.wait_ge(es_lo, b * ND + ND)
                    pe.wait_ge(ct_lo, b * ND + ND)
                if t >= 2:
                    pe.wait_ge(a_exp, b * NT + t - 1)
                product(ps_s[:, t % 2, :], lambda l, k: es_t2[:, l, k, t * P:(t + 1) * P],
                        lambda r, k: c_t2[:, r, k, :], True, True).then_inc(s_ready, 1)

            def turn_a(b, t):
                pe.wait_ge(a_ready, b * NT + t + 1)
                if t == 0:
                    pe.wait_ge(et_copied, b * NT + NT)
                else:
                    pe.wait_ge(at_lo, b * NT + t)
                for k in range(NT):
                    last = pe.transpose(ps_t[:, k, :], a_sb[:, t % 2, k * P:(k + 1) * P], ident[:])
                last.then_inc(at_ps, 1)

            def attend(b, k):
                if k == 0:
                    pe.wait_ge(at_lo, b * NT + NT)
                    pe.wait_ge(c_lo, b * NT + NT)
                if k >= 2:
                    pe.wait_ge(ht_lo, b * ND + k - 1)
                product(ps_h[:, k % 2, :], lambda l, j: c_2[:, l, j, k * P:(k + 1) * P],
                        lambda r, j: a_t2[:, r, j, :], True, True).then_inc(ht_ps, 1)

            def row_weights(b, step):
                if step == 0:
                    pe.wait_ge(b_dve, b * 6 + 2)
                    pe.transpose(ps_b[0:1, 0:P], pmax[:], ident[:]).then_inc(b_pe, 1)
                elif step == 1:
                    pe.wait_ge(b_dve, b * 6 + 3)
                    pe.matmul(ps_b[:, 0:1], ones[0:1, :], gmax[:], start=True, stop=True).then_inc(b_pe, 1)
                elif step == 2:
                    pe.wait_ge(bexp_ready, b + 1)
                    pe.matmul(ps_b[:, 0:1], ones[:], bsum[:], start=True, stop=True).then_inc(b_pe, 1)
                else:
                    pe.wait_ge(b_dve, b * 6 + 6)
                    for t in range(NT):
                        last = pe.matmul(ps_b[:, t * P:(t + 1) * P], batt[:, t:t + 1].broadcast_to([P, P]), ident[:],
                                         start=True, stop=True)
                    last.then_inc(b_pe, 1)

            def feats(b, t, part):
                out = ps_f[:, t % 2, :]
                cols = slice(t * P, (t + 1) * P)
                if part == 0:
                    if t >= 2:
                        pe.wait_ge(x1_ready, b * NT + t - 1)
                    pe.wait_ge(ht_lo, b * ND + ND)
                    pe.wait_ge(w_lo, ND)
                    product(out, lambda l, k: h_t2[:, l, k, cols], lambda r, k: wh[:, r, k, :], True, False)
                elif part == 1:
                    pe.wait_ge(eh_lo, b * ND + ND)
                    pe.wait_ge(w_lo, 2 * ND)
                    product(out, lambda l, k: eh_t2[:, l, k, cols], lambda r, k: weh[:, r, k, :], False, False)
                else:
                    pe.wait_ge(wec_lo, b * ND + ND)
                    pe.wait_ge(et_lo, b * ND + ND)
                    product(out, lambda l, k: e_t2[:, l, k, cols], lambda r, k: wec[:, r, k, :], False,
                            True).then_inc(feat_ps, 1)

            LAST_FEATS = [(2, 2), (3, 0), (3, 1), (3, 2)]

            def first_feats(b, more):
                for k in range(ND):
                    attend(b, k)
                    row_weights(b, k)
                for n, (t, part) in enumerate([(0, 0), (1, 0), (0, 1), (1, 1), (0, 2), (1, 2)]):
                    feats(b, t, part)
                    if more and n >= 2:
                        turn_e(b + 1, n - 2)
                for part in range(2):
                    feats(b, 2, part)

            def softmax(b, first):
                scores(b, 0)
                for t in range(NT):
                    if not first:
                        feats(b - 1, *LAST_FEATS[t])
                    elif t + 1 < NT:
                        scores(b, t + 1)
                    turn_a(b, t)
                    if not first and t + 1 < NT:
                        scores(b, t + 1)

            for t in range(NT):
                turn_e(0, t)
            softmax(0, True)
            with pe.Fori(0, B - 1) as b:
                first_feats(b, True)
                softmax(b + 1, False)
            first_feats(B - 1, False)
            for t, part in LAST_FEATS:
                feats(B - 1, t, part)


def expert_attention(nc, x1, g_ffn, wq, wk, w_vsd, wo, out):
    B, T, D = x1.shape
    NT, ND = T // P, D // P
    H, DH = 8, 64
    NV = wo.shape[0]
    E = NV // DH
    NL = H * E
    NX = NV + 2 * NL
    PAIRS = H // 2
    KZ = -(-NV // P)
    SCALE = float(DH) ** -0.5
    assert NT == ND == 4 and 2 * DH == P and w_vsd.shape[1] == NX and wq.shape[1] == D and H * DH == D

    SHARED = KZ * P - NV

    def tile_at(k):
        return min(k * P, NV - P)

    STEPS = H * NT
    LAG = 2
    PV_AT = [NT + LAG + 1, NT + LAG + 2, NT + LAG + 3, NT + LAG + 3]
    SUM_AT = PV_AT[-1] + 1
    TURN_O_AT = SUM_AT + NT + 2
    PAIR = 2 * NT
    PARTS = 2
    VALUE_AT = [5, 12, 18, 25]
    STATS_AT = -13
    TURN_Z_AT = TURN_O_AT + PAIR * (PAIRS - 1) + 4

    PLAN = {-11: [("turn_y", 0, 0), ("turn_y", 1, 0)], -10: [("turn_y", 2, 0), ("turn_y", 3, 0)]}
    for p, (q_at, k_at) in enumerate([(-9, -3), (2, 4), (7, 9), (17, 19)]):
        for part in range(PARTS):
            PLAN.setdefault(q_at + part, []).append(("q", p, part))
            PLAN.setdefault(k_at + part, []).append(("k", p, part))
        PLAN.setdefault(TURN_O_AT + PAIR * p, []).insert(0, ("turn_o", p, 0))
    for t in range(NT):
        PLAN.setdefault(-7 + t, []).append(("experts", t, 0))
        PLAN.setdefault(TURN_Z_AT + 1 + t, []).append(("result", t, 0))
    PLAN[TURN_Z_AT] = [("turn_z", k, 0) for k in range(KZ)]

    PE_CUT = ACT_CUT = 21
    DVE_CUT = 19
    assert min(PLAN) >= PE_CUT - STEPS and max(PLAN) < PE_CUT + STEPS

    RING = 3
    ORDER = []
    for n in range(PE_CUT, PE_CUT + STEPS):
        for what in PLAN.get(n, []) + PLAN.get(n - STEPS, []):
            if what[2] == 0:
                ORDER.append(what[:2])
    assert len(ORDER) % RING == 0 and all(n < PE_CUT for what in ORDER[-RING:] for n in PLAN if what + (0,) in PLAN[n])

    def bank_of(what):
        return ORDER.index(what) % RING

    def ended(n):
        return [what[:2] for what in PLAN.get(n, []) if what[0] not in "qk" or what[2] == PARTS - 1]

    with ExitStack() as mem:
        def sb(name, shape, dt=F32):
            return mem.enter_context(nc.sbuf_tensor(name, shape, dt))

        def sem(name):
            return mem.enter_context(nc.semaphore(name + "_2"))

        ident = sb("ident_2", [P, P])
        gate = sb("gate_2", [P, 1])
        gate_raw = sb("gate_raw_2", [P, 1])
        wq2 = sb("wq2", [P, 2, ND, D], F32R)
        wk2 = sb("wk2", [P, 2, ND, D], F32R)
        wx2 = sb("wx2", [P, 2, ND, NX], F32R)
        wo2 = sb("wo2", [P, 2, KZ, D], F32R)
        stage = sb("stage_2", [P, NT, D])
        y_t2 = sb("y_t2", [P, 2, ND, T], F32R)
        q_nat = sb("q_nat", [P, 2, T], F32R)
        q_st = sb("q_st", [P, 2, 2, 2, T], F32R)
        k_st = sb("k_st", [P, 2, 2, T], F32R)
        xv = sb("xv", [P, NT, E, DH])
        logits = sb("logits", [P, 2, NT * H, E])
        beaten = sb("beaten", [P, 2 * NT * H, E, E], BF16)
        rank = logits[:].rearrange("p s g e -> p (s g) e")
        pick = sb("pick", [P, 2, NT, H, E])
        sig = sb("sig", [P, NT * H, E])
        coef = sb("coef", [P, H, NT, E])
        v_acc = sb("v_acc", [P, 2, NT, 2, DH])
        v_tmp = sb("v_tmp", [P, NT, 2, DH])
        v_st = sb("v_st", [P, 4, NT, 2, DH], F32R)
        probs = sb("probs", [P, 2, T])
        pt2 = sb("pt2", [P, 2, 2, NT, T], F32R)
        o_tmp = sb("o_tmp", [P, T])
        o_t = sb("o_t", [P, T])
        attn = sb("attn", [P, NT, 2, DH])
        z = sb("z", [P, NT, NV])
        z_tmp = sb("z_tmp", [P, NT, E, DH])
        z_t2 = sb("z_t2", [P, 2, KZ, T], F32R)
        x_res = sb("x_res", [P, NT, D])
        stats = sb("stats_2", [P, NT, 6])
        mean = sb("mean_2", [P, NT])
        work = sb("work_2", [P, 5, NT])
        rstd = sb("rstd_2", [P, NT])
        nmax = sb("nmax_2", [P, STEPS])
        den = sb("den_2", [P, H, NT])
        rden = sb("rden_2", [P, H, NT])

        ps_s = mem.enter_context(nc.psum_tensor("ps_s_2", [P, 2, T], F32))
        ps_p = mem.enter_context(nc.psum_tensor("ps_p_2", [P, 2, NT, P], F32))
        ps_o = mem.enter_context(nc.psum_tensor("ps_o_2", [P, T], F32))
        ps_r = mem.enter_context(nc.psum_tensor("ps_r_2", [P, RING, D], F32))

        gate_loaded = sem("gate_loaded")
        cleared = sem("cleared")
        ident_ready = sem("ident_ready")
        gate_ready = sem("gate_ready")
        x1_loaded = sem("x1_loaded")
        xres_loaded = sem("xres_loaded")
        out_stored = sem("out_stored")
        w_loaded = {name: [sem(f"{name}_loaded{k}") for k in range(KZ if name == "wo" else ND)]
                    for name in ("wq", "wk", "wx", "wo")}
        w_hi = {name: sem(name + "_hi") for name in ("wq", "wk", "wx", "wo")}
        w_lo = {name: sem(name + "_lo") for name in ("wq", "wk", "wx", "wo")}
        stats_done = sem("stats_done")
        newton = sem("newton")
        y_ready = sem("y_ready")
        yt_ps = sem("yt_ps")
        yt_hi = sem("yt_hi")
        yt_lo = sem("yt_lo")
        ex_ps = sem("ex_ps")
        xv_ready = sem("xv_ready")
        logits_ready = sem("logits_ready")
        compared = sem("compared")
        gates = sem("gates")
        sig_exp = sem("sig_exp")
        pick_ready = sem("pick_ready")
        mask_ready = sem("mask_ready")
        q_ps = sem("q_ps")
        q_hi = sem("q_hi")
        q_lo = sem("q_lo")
        q_spread = [sem("q_spread0"), sem("q_spread1")]
        k_ps = sem("k_ps")
        k_hi = sem("k_hi")
        k_lo = sem("k_lo")
        v_steps = sem("v_steps")
        v_hi = sem("v_hi")
        v_lo = sem("v_lo")
        s_ready = sem("s_ready")
        nmax_ready = sem("nmax_ready")
        p_exp = sem("p_exp")
        pt_ps = sem("pt_ps")
        pt_hi = sem("pt_hi")
        pt_lo = sem("pt_lo")
        o_ps = sem("o_ps")
        o_half = sem("o_half")
        o_ready = sem("o_ready")
        to_ps = sem("to_ps")
        attn_ready = sem("attn_ready")
        rden_ready = sem("rden_ready")
        coef_ready = sem("coef_ready")
        z_dve = sem("z_dve")
        z_pool = sem("z_pool")
        zt_ps = sem("zt_ps")
        zt_hi = sem("zt_hi")
        zt_lo = sem("zt_lo")
        res_ps = sem("res_ps")
        out_ready = sem("out_ready")

        x1_dram = x1.rearrange("b (t p) d -> b p t d", p=P)
        out_dram = out.rearrange("b (t p) d -> b p t d", p=P)
        weights = {"wq": wq2, "wk": wk2, "wx": wx2, "wo": wo2}
        WEIGHT_TILES = [(name, k) for name in ("wq", "wk", "wx", "wo") for k in range(KZ if name == "wo" else ND)]

        def of(dram, b):
            return dram[bass.ds(b, 1)].rearrange("o p t d -> (o p) t d")

        def own_rows(name, k):
            return slice(SHARED if (name, k) == ("wo", KZ - 1) else 0, P)

        def weight_tile(name, half, k):
            return weights[name][own_rows(name, k), half, k, :]

        PASS = ([x_res[:, t, :] for t in range(NT)] + [probs[:, i, :] for i in range(2)] +
                [z_tmp[:].rearrange("p t e k -> p (t e k)")[:, i * D:(i + 1) * D] for i in range(2)])

        def passing(name, k):
            turn = WEIGHT_TILES.index((name, k)) % len(PASS)
            return PASS[turn][own_rows(name, k), 0:weights[name].shape[3]]

        def take_weight_lo(eng, name, k):
            eng.wait_ge(w_hi[name], k + 1)
            eng.tensor_tensor(weight_tile(name, 1, k), passing(name, k), weight_tile(name, 0, k).bitcast(F32),
                              ALU.subtract).then_inc(w_lo[name], 1)

        def head_rows(a):
            return slice(a * DH, a * DH + DH)

        V_STEPS = 2 * E - 1

        def pair_values(p, half):
            slot = p % 2 * 2
            return v_st[:, slot:slot + 2, :, half, :].rearrange("p a t k -> p t a k")

        Z_STEPS = 2 * H - 1

        def mix_product(eng, done, tiles, b, h):
            p, a = h // 2, h % 2
            zv = z[:, tiles, :].rearrange("p t (e k) -> p t e k", e=E)
            if a == 0:
                eng.wait_ge(attn_ready, b * PAIRS + p + 1)
            eng.wait_ge(coef_ready, b * H + h + 1)
            if h:
                eng.wait_ge(done, b * Z_STEPS + 2 * h - 1)
            shape = [P, tiles.stop - tiles.start, E, DH]
            eng.tensor_tensor(z_tmp[:, tiles] if h else zv, attn[:, tiles, a, :].unsqueeze(2).broadcast_to(shape),
                              coef[:, h, tiles, :].unsqueeze(3).broadcast_to(shape), ALU.mult).then_inc(done, 1)

        def mix_sum(eng, done, tiles, b, h):
            if h:
                zv = z[:, tiles, :].rearrange("p t (e k) -> p t e k", e=E)
                eng.wait_ge(done, b * Z_STEPS + 2 * h)
                eng.tensor_tensor(zv, zv, z_tmp[:, tiles], ALU.add).then_inc(done, 1)

        DVE_TILES, POOL_TILES = slice(0, NT // 2), slice(NT // 2, NT)

        block = mem.enter_context(nc.Block())

        @block.sync
        def _(sp):
            def load_x1(b):
                sp.dma_start(stage[:], of(x1_dram, b)).then_inc(x1_loaded, 16)

            def load_residual(b):
                sp.dma_start(x_res[:], of(x1_dram, b)).then_inc(xres_loaded, 16)

            def spread_q(b, p):
                sp.wait_ge(q_lo, b * PAIRS + p + 1)
                for a in range(2):
                    for half in range(2):
                        sp.dma_start(q_st[head_rows(half), p % 2, a, :, :].bitcast(F32),
                                     q_nat[head_rows(a), :, :].bitcast(F32)).then_inc(q_spread[p % 2], 16)

            def store(b):
                for t in range(NT):
                    sp.wait_ge(out_ready, b * NT + t + 1)
                    sp.dma_start(of(out_dram, b)[:, t, :], x_res[:, t, :]).then_inc(out_stored, 16)

            def steady(b, more):
                spread_q(b, 3)
                spread_q(b + 1, 0)
                if more:
                    sp.wait_ge(yt_ps, b * NT + 2 * NT)
                    load_x1(b + 2)
                spread_q(b + 1, 1)
                spread_q(b + 1, 2)
                store(b)
                sp.wait_ge(out_stored, (b + 1) * NT * 16)
                load_residual(b + 1)

            load_x1(0)
            sources = {"wq": wq, "wk": wk, "wx": w_vsd, "wo": wo}
            for n, (name, k) in enumerate(WEIGHT_TILES):
                if n >= len(PASS):
                    before, i = WEIGHT_TILES[n - len(PASS)]
                    sp.wait_ge(w_lo[before], i + 1)
                into = passing(name, k)
                sp.dma_start(into, sources[name][k * P:k * P + into.shape[0], :]).then_inc(w_loaded[name][k], 16)
            sp.dma_start(gate_raw[:], g_ffn.partition_broadcast(P)).then_inc(gate_loaded, 16)
            sp.wait_ge(w_lo["wx"], NT)
            load_residual(0)
            spread_q(0, 0)
            sp.wait_ge(yt_ps, NT)
            load_x1(1)
            spread_q(0, 1)
            spread_q(0, 2)
            with sp.Fori(0, B - 2) as b:
                steady(b, True)
            steady(B - 2, False)
            spread_q(B - 1, 3)
            store(B - 1)
            sp.wait_ge(out_stored, B * NT * 16)

        @block.gpsimd
        def _(pool):
            pool.memset(ident[:], 0.0).then_inc(cleared, 1)
            pool.memset(beaten[:], 0.0).then_inc(cleared, 1)
            pool.memset(wo2[0:SHARED, :, KZ - 1, :].bitcast(F32), 0.0).then_inc(cleared, 1)
            pool.wait_ge(cleared, 3)
            pool.affine_select(out=ident[:], in_=ident[:], compare_op=ALU.not_equal, fill=1.0, base=0,
                               pattern=[[-1, P]], channel_multiplier=1).then_inc(ident_ready, 1)
            for name, k in WEIGHT_TILES:
                if name in ("wq", "wk"):
                    take_weight_lo(pool, name, k)

            def mix_values(b, p, first=False):
                count = (b * PAIRS + p) * V_STEPS
                if p == 0:
                    pool.wait_ge(pick_ready, b + 1)
                    pool.wait_ge(xv_ready, b * NT + NT)
                if p >= 2 or not first:
                    pool.wait_ge(v_lo, b * PAIRS + p - 1)
                acc = v_acc[:, p % 2]
                shape = [P, NT, 2, DH]
                for e in range(E):
                    pool.tensor_tensor(v_tmp[:] if e else acc, xv[:, :, e, :].unsqueeze(2).broadcast_to(shape),
                                       pick[:, 0, :, 2 * p:2 * p + 2, e].unsqueeze(3).broadcast_to(shape),
                                       ALU.mult).then_inc(v_steps, 1)
                    pool.wait_ge(v_steps, count + 2 * e + (0 if e else 1))
                    if e:
                        pool.tensor_tensor(acc, acc, v_tmp[:], ALU.add).then_inc(v_steps, 1)
                        pool.wait_ge(v_steps, count + 2 * e + 1)

            def mix_pair(b, p):
                for h in (2 * p, 2 * p + 1):
                    mix_product(pool, z_pool, POOL_TILES, b, h)
                    mix_sum(pool, z_pool, POOL_TILES, b, h)

            for p in range(3):
                mix_values(0, p, True)
            with pool.Fori(0, B - 1) as b:
                mix_pair(b, 0)
                mix_values(b, 3)
                mix_pair(b, 1)
                mix_values(b + 1, 0)
                mix_pair(b, 2)
                mix_values(b + 1, 1)
                mix_pair(b, 3)
                mix_values(b + 1, 2)
            mix_pair(B - 1, 0)
            mix_values(B - 1, 3)
            for p in range(1, PAIRS):
                mix_pair(B - 1, p)

        @block.scalar
        def _(act):
            for name, k in WEIGHT_TILES:
                act.wait_ge(w_loaded[name][k], 16)
                act.activation(weight_tile(name, 0, k), passing(name, k), ACT.Copy).then_inc(w_hi[name], 1)
            act.wait_ge(gate_loaded, 16)
            act.activation(gate[:], gate_raw[:], ACT.Tanh).then_inc(gate_ready, 1)

            def scores_exp(b, n, first):
                act.wait_ge(nmax_ready, b * STEPS + n + 1)
                if n >= 2 or not first:
                    act.wait_ge(pt_ps, b * STEPS + n - 1)
                act.activation(probs[:, n % 2, :], ps_s[:, n % 2, :], ACT.Exp, bias=nmax[:, n:n + 1],
                               accum_out=den[:, n // NT, n % NT:n % NT + 1]).then_inc(p_exp, 1)

            def probs_hi(b, n, first):
                h, t = n // NT, n % NT
                act.wait_ge(pt_ps, b * STEPS + n + 1)
                if t == 0 and (h >= 2 or not first):
                    act.wait_ge(o_ps, b * H + h - 1)
                act.activation(pt2[:, h % 2, 0, :, t * P:(t + 1) * P], ps_p[:, n % 2], ACT.Copy).then_inc(pt_hi, 1)

            def value_hi(b, p, first):
                act.wait_ge(v_steps, (b * PAIRS + p + 1) * V_STEPS)
                if p >= 2 or not first:
                    act.wait_ge(o_ps, b * H + 2 * p - 2)
                act.activation(pair_values(p, 0), v_acc[:, p % 2], ACT.Copy).then_inc(v_hi, 1)

            def out_half(b, h, first):
                act.wait_ge(o_ps, b * H + h + 1)
                if h or not first:
                    act.wait_ge(o_ready, b * H + h)
                act.activation(o_tmp[DH:P, :], ps_o[0:DH, :], ACT.Copy).then_inc(o_half, 1)

            def part_hi(b, name, n, first):
                ps = ps_r[:, bank_of((name, n)), :]
                if name == "turn_y":
                    act.wait_ge(yt_ps, b * NT + n + 1)
                    if n == 0 and not first:
                        act.wait_ge(k_ps, b * PAIRS)
                    act.activation(y_t2[:, 0, :, n * P:(n + 1) * P], ps.rearrange("p (k t) -> p k t", k=ND),
                                   ACT.Copy).then_inc(yt_hi, 1)
                elif name == "experts":
                    act.wait_ge(ex_ps, b * NT + n + 1)
                    if n == 0 and not first:
                        act.wait_ge(v_steps, b * PAIRS * V_STEPS)
                        act.wait_ge(mask_ready, b)
                    act.activation(logits[:, :, n * H:(n + 1) * H, :],
                                   ps[:, NV:NX].rearrange("p (s h e) -> p s h e", s=2, h=H),
                                   ACT.Copy).then_inc(logits_ready, 1)
                    act.activation(xv[:, n], ps[:, 0:NV].rearrange("p (e k) -> p e k", e=E),
                                   ACT.Copy).then_inc(xv_ready, 1)
                elif name == "q":
                    act.wait_ge(q_ps, b * PAIRS + n + 1)
                    if n:
                        act.wait_ge(q_spread[(n - 1) % 2], b * (PAIRS * 32) + ((n - 1) // 2 + 1) * 64)
                    elif not first:
                        act.wait_ge(q_spread[1], b * (PAIRS * 32))
                    act.activation(q_nat[:, 0, :], ps, ACT.Copy, scale=SCALE).then_inc(q_hi, 1)
                elif name == "k":
                    act.wait_ge(k_ps, b * PAIRS + n + 1)
                    for a in range(2):
                        own = head_rows(a)
                        act.activation(k_st[own, n % 2, a, :], ps[own, :], ACT.Copy).then_inc(k_hi, 1)
                elif name == "turn_o":
                    act.wait_ge(to_ps, b * PAIRS + n + 1)
                    if n:
                        act.wait_ge(z_dve, b * Z_STEPS + 4 * n - 1)
                        act.wait_ge(z_pool, b * Z_STEPS + 4 * n - 1)
                    act.activation(attn[:], ps.rearrange("p (t a k) -> p t a k", t=NT, a=2),
                                   ACT.Copy).then_inc(attn_ready, 1)
                elif name == "turn_z":
                    act.wait_ge(zt_ps, b * KZ + n + 1)
                    act.activation(z_t2[:, 0, n, :], ps, ACT.Copy).then_inc(zt_hi, 1)

            def step(b, n, first=False):
                for h in range(H):
                    if n == NT * h + SUM_AT:
                        out_half(b, h, first)
                if 0 <= n - LAG < STEPS:
                    probs_hi(b, n - LAG, first)
                if 0 <= n < STEPS:
                    scores_exp(b, n, first)
                for name, i in ended(n - 1):
                    if name != "turn_z":
                        part_hi(b, name, i, first)
                if n == TURN_Z_AT:
                    for k in range(KZ):
                        part_hi(b, "turn_z", k, first)
                if n in VALUE_AT:
                    value_hi(b, VALUE_AT.index(n), first)
                if n == -3:
                    act.wait_ge(logits_ready, b * NT + NT)
                    act.activation(sig[:], logits[:, 0], ACT.Exp, scale=-1.0).then_inc(sig_exp, 1)

            for n in range(ACT_CUT - STEPS, ACT_CUT):
                step(0, n, True)
            with act.Fori(0, B - 1) as b:
                for n in range(ACT_CUT, ACT_CUT + STEPS):
                    step(b, n)
                    step(b + 1, n - STEPS)
            for n in range(ACT_CUT, ACT_CUT + STEPS):
                step(B - 1, n)

        @block.vector
        def _(dve):
            def row_stats(b):
                dve.wait_ge(x1_loaded, b * 16 + 16)
                for t in range(NT):
                    dve.bn_stats(stats[:, t, :], stage[:, t, :]).then_inc(stats_done, 1)

            def root(b, part):
                if part == 0:
                    dve.wait_ge(stats_done, b * NT + NT)
                mean_rstd(dve, part, stats[:], D, mean[:], work[:], rstd[:], newton, b * ROOT_STEPS)

            def normalise(b):
                dve.wait_ge(newton, b * ROOT_STEPS + ROOT_STEPS)
                for t in range(NT):
                    dve.tensor_scalar(stage[:, t, :], stage[:, t, :], mean[:, t:t + 1], rstd[:, t:t + 1], ALU.subtract,
                                      ALU.mult).then_inc(y_ready, 1)

            def row_max(b, n):
                dve.wait_ge(s_ready, b * STEPS + n + 1)
                dve.tensor_reduce(nmax[:, n:n + 1], ps_s[:, n % 2, :], AX_X, ALU.max, negate=True).then_inc(nmax_ready, 1)

            def probs_lo(b, n):
                h, t = n // NT, n % NT
                dve.wait_ge(pt_hi, b * STEPS + n + 1)
                dve.tensor_tensor(pt2[:, h % 2, 1, :, t * P:(t + 1) * P], ps_p[:, n % 2],
                                  pt2[:, h % 2, 0, :, t * P:(t + 1) * P].bitcast(F32), ALU.subtract).then_inc(pt_lo, 1)

            def value_lo(b, p):
                dve.wait_ge(v_hi, b * PAIRS + p + 1)
                dve.tensor_tensor(pair_values(p, 1), v_acc[:, p % 2], pair_values(p, 0).bitcast(F32),
                                  ALU.subtract).then_inc(v_lo, 1)

            def out_sum(b, h, first):
                p, a = h // 2, h % 2
                dve.wait_ge(o_half, b * H + h + 1)
                if a == 0 and (p or not first):
                    dve.wait_ge(to_ps, b * PAIRS + p)
                dve.tensor_tensor(o_t[head_rows(a), :], ps_o[DH:P, :], o_tmp[DH:P, :], ALU.add).then_inc(o_ready, 1)

            def coefficients(b, h):
                dve.wait_ge(p_exp, b * STEPS + NT * h + NT)
                dve.reciprocal(rden[:, h, :], den[:, h, :]).then_inc(rden_ready, 1)
                dve.wait_ge(rden_ready, b * H + h + 1)
                if h == 0:
                    dve.wait_ge(mask_ready, b + 1)
                dve.tensor_tensor(coef[:, h], pick[:, 1, :, h, :], rden[:, h, :].unsqueeze(2).broadcast_to([P, NT, E]),
                                  ALU.mult).then_inc(coef_ready, 1)

            def part_lo(b, name, n):
                ps = ps_r[:, bank_of((name, n)), :]
                if name == "turn_y":
                    cols = slice(n * P, (n + 1) * P)
                    dve.wait_ge(yt_hi, b * NT + n + 1)
                    dve.tensor_tensor(y_t2[:, 1, :, cols], ps.rearrange("p (k t) -> p k t", k=ND),
                                      y_t2[:, 0, :, cols].bitcast(F32), ALU.subtract).then_inc(yt_lo, 1)
                elif name == "q":
                    dve.wait_ge(q_hi, b * PAIRS + n + 1)
                    dve.scalar_tensor_tensor(q_nat[:, 1, :], ps, SCALE, q_nat[:, 0, :].bitcast(F32), ALU.mult,
                                             ALU.subtract).then_inc(q_lo, 1)
                elif name == "k":
                    for a in range(2):
                        own, other = head_rows(a), head_rows(1 - a)
                        dve.wait_ge(k_hi, b * H + 2 * n + a + 1)
                        dve.tensor_tensor(k_st[other, n % 2, a, :], ps[own, :], k_st[own, n % 2, a, :].bitcast(F32),
                                          ALU.subtract).then_inc(k_lo, 1)
                elif name == "turn_z":
                    dve.wait_ge(zt_hi, b * KZ + n + 1)
                    dve.tensor_tensor(z_t2[:, 1, n, :], ps, z_t2[:, 0, n, :].bitcast(F32),
                                      ALU.subtract).then_inc(zt_lo, 1)
                elif name == "result":
                    if n == 0:
                        dve.wait_ge(xres_loaded, b * 16 + 16)
                        dve.wait_ge(gate_ready, 1)
                    dve.wait_ge(res_ps, b * NT + n + 1)
                    dve.scalar_tensor_tensor(x_res[:, n, :], ps, gate[:, 0:1], x_res[:, n, :],
                                             ALU.mult, ALU.add).then_inc(out_ready, 1)

            COMPARISONS = 2 * (E - 1)

            def compare(b):
                dve.wait_ge(logits_ready, b * NT + NT)
                flat = logits[:].rearrange("p s g e -> p (s g) e")
                groups = 2 * NT * H
                for k in range(E):
                    for others, before in ((slice(k + 1, E), ALU.is_gt), (slice(0, k), ALU.is_ge)):
                        if others.stop > others.start:
                            dve.tensor_tensor(beaten[:, :, k, others], flat[:, :, others],
                                              flat[:, :, k:k + 1].broadcast_to([P, groups, others.stop - others.start]),
                                              before).then_inc(compared, 1)

            def count_better(b):
                dve.wait_ge(sig_exp, b + 1)
                dve.tensor_scalar(sig[:], sig[:], 1.0, None, ALU.add).then_inc(gates, 1)
                dve.wait_ge(compared, (b + 1) * COMPARISONS)
                dve.tensor_reduce(rank, beaten[:], AX_X, ALU.add).then_inc(gates, 1)

            def route_values(b, first):
                dve.wait_ge(gates, b * 3 + 1)
                dve.reciprocal(sig[:], sig[:]).then_inc(gates, 1)
                if not first:
                    dve.wait_ge(v_steps, b * PAIRS * V_STEPS)
                dve.wait_ge(gates, b * 3 + 3)
                dve.scalar_tensor_tensor(pick[:, 0].rearrange("p t h e -> p (t h) e"), rank[:, 0:NT * H], 1.5, sig[:],
                                         ALU.is_lt, ALU.mult).then_inc(pick_ready, 1)

            def route_out(b, first):
                if not first:
                    dve.wait_ge(coef_ready, b * H)
                dve.tensor_scalar(pick[:, 1].rearrange("p t h e -> p (t h) e"), rank[:, NT * H:], 1.5, None,
                                  ALU.is_lt).then_inc(mask_ready, 1)

            def step(b, n, first=False):
                if 0 <= n < STEPS:
                    row_max(b, n)
                for h in range(H):
                    if n == NT * h + SUM_AT:
                        out_sum(b, h, first)
                if 0 <= n - LAG < STEPS:
                    probs_lo(b, n - LAG)
                for h in range(H):
                    if n == NT * h + NT:
                        coefficients(b, h)
                for name, i in ended(n - 1):
                    if name not in ("turn_z", "turn_o", "experts"):
                        part_lo(b, name, i)
                if n == TURN_Z_AT:
                    for k in range(KZ):
                        part_lo(b, "turn_z", k)
                for p in range(PAIRS):
                    at = PAIR * p + TURN_O_AT + 1
                    if n == at:
                        mix_product(dve, z_dve, DVE_TILES, b, 2 * p)
                    if n == at + 1:
                        mix_sum(dve, z_dve, DVE_TILES, b, 2 * p)
                        mix_product(dve, z_dve, DVE_TILES, b, 2 * p + 1)
                    if n == at + 2:
                        mix_sum(dve, z_dve, DVE_TILES, b, 2 * p + 1)
                if n in VALUE_AT:
                    value_lo(b, VALUE_AT.index(n))
                if n == STATS_AT:
                    row_stats(b)
                    root(b, 0)
                    root(b, 1)
                if n == STATS_AT + 1:
                    for part in range(2, ROOT_PARTS):
                        root(b, part)
                    normalise(b)
                if n == -3:
                    compare(b)
                if n == -2:
                    count_better(b)
                if n == -1:
                    route_values(b, first)
                if n == 0:
                    route_out(b, first)

            dve.wait_ge(cleared, 3)
            for n in range(DVE_CUT - STEPS, DVE_CUT):
                step(0, n, True)
                if n == STATS_AT + 1:
                    for name, k in WEIGHT_TILES:
                        if name in ("wx", "wo"):
                            take_weight_lo(dve, name, k)
            with dve.Fori(0, B - 1) as b:
                for n in range(DVE_CUT, DVE_CUT + STEPS):
                    step(b, n)
                    step(b + 1, n - STEPS)
            for n in range(DVE_CUT, DVE_CUT + STEPS):
                step(B - 1, n)

        @block.tensor
        def _(pe):
            pe.wait_ge(ident_ready, 1)

            def wait_read(b, what):
                name, n = what
                if name == "turn_y":
                    pe.wait_ge(yt_lo, b * NT + n + 1)
                elif name == "experts":
                    pe.wait_ge(logits_ready, b * NT + n + 1)
                    pe.wait_ge(xv_ready, b * NT + n + 1)
                elif name == "q":
                    pe.wait_ge(q_lo, b * PAIRS + n + 1)
                elif name == "k":
                    pe.wait_ge(k_lo, b * H + 2 * n + 2)
                elif name == "turn_o":
                    pe.wait_ge(attn_ready, b * PAIRS + n + 1)
                elif name == "turn_z":
                    pe.wait_ge(zt_lo, b * KZ + n + 1)
                else:
                    pe.wait_ge(out_ready, b * NT + n + 1)

            AHEAD = {what[:2] for n in PLAN if n < PE_CUT for what in PLAN[n]}

            def wait_bank(b, what, first, last):
                place = ORDER.index(what) - RING
                while True:
                    before = ORDER[place]
                    offset = (before in AHEAD) - (what in AHEAD) - (place < 0)
                    if not (first and offset < 0) and not (last and offset > 0):
                        wait_read(b + offset, before)
                        return
                    place -= RING
                    if first and place < 0:
                        return

            def shared_part(b, name, n, part, first, last):
                ps = ps_r[:, bank_of((name, n)), :]
                if part == 0:
                    wait_bank(b, (name, n), first, last)
                if name == "turn_y":
                    pe.wait_ge(y_ready, b * NT + n + 1)
                    for k in range(ND):
                        end = pe.transpose(ps[:, k * P:(k + 1) * P], stage[:, n, k * P:(k + 1) * P], ident[:])
                    end.then_inc(yt_ps, 1)
                elif name in "qk":
                    if part == 0:
                        pe.wait_ge(yt_lo, b * NT + NT)
                        if first:
                            pe.wait_ge(w_lo["w" + name], ND)
                    w2 = wq2 if name == "q" else wk2
                    every = [(k, l, r) for k in range(ND) for l, r in PASSES]
                    size = len(every) // PARTS
                    for m in range(part * size, part * size + size):
                        k, l, r = every[m]
                        end = pe.matmul(ps, w2[:, l, k, n * P:(n + 1) * P], y_t2[:, r, k, :], start=m == 0,
                                        stop=m == len(every) - 1)
                    if part == PARTS - 1:
                        end.then_inc(q_ps if name == "q" else k_ps, 1)
                elif name == "experts":
                    pe.wait_ge(yt_lo, b * NT + n + 1)
                    if first:
                        pe.wait_ge(w_lo["wx"], ND)
                    every = [(k, l, r) for k in range(ND) for l, r in PASSES]
                    for m, (k, l, r) in enumerate(every):
                        end = pe.matmul(ps[:, 0:NX], y_t2[:, l, k, n * P:(n + 1) * P], wx2[:, r, k, :], start=m == 0,
                                        stop=m == len(every) - 1)
                    end.then_inc(ex_ps, 1)
                elif name == "turn_o":
                    pe.wait_ge(o_ready, b * H + 2 * n + 2)
                    for t in range(NT):
                        end = pe.transpose(ps[:, t * P:(t + 1) * P], o_t[:, t * P:(t + 1) * P], ident[:])
                    end.then_inc(to_ps, 1)
                elif name == "turn_z":
                    if n == 0:
                        pe.wait_ge(z_dve, (b + 1) * Z_STEPS)
                        pe.wait_ge(z_pool, (b + 1) * Z_STEPS)
                    for t in range(NT):
                        end = pe.transpose(ps[:, t * P:(t + 1) * P], z[:, t, tile_at(n):tile_at(n) + P], ident[:])
                    end.then_inc(zt_ps, 1)
                else:
                    if n == 0:
                        pe.wait_ge(zt_lo, b * KZ + KZ)
                        pe.wait_ge(w_lo["wo"], KZ)
                    every = [(k, l, r) for k in range(KZ) for l, r in PASSES]
                    for m, (k, l, r) in enumerate(every):
                        end = pe.matmul(ps, z_t2[:, l, k, n * P:(n + 1) * P], wo2[:, r, k, :],
                                        start=m == 0, stop=m == len(every) - 1)
                    end.then_inc(res_ps, 1)

            def scores(b, n, first):
                h, t = n // NT, n % NT
                slot, a = h // 2 % 2, h % 2
                if n % PAIR == 0:
                    pe.wait_ge(q_spread[slot], b * (PAIRS * 32) + (h // 4 + 1) * 64)
                    pe.wait_ge(k_lo, b * H + h + 2)
                if n >= 2 or not first:
                    pe.wait_ge(p_exp, b * STEPS + n - 1)
                for part in range(2):
                    end = pe.matmul(ps_s[:, n % 2, :], q_st[:, slot, a, part, t * P:(t + 1) * P], k_st[:, slot, a, :],
                                    start=part == 0, stop=part == 1)
                end.then_inc(s_ready, 1)

            def turn_probs(b, n, first):
                pe.wait_ge(p_exp, b * STEPS + n + 1)
                if n >= 2 or not first:
                    pe.wait_ge(pt_lo, b * STEPS + n - 1)
                for k in range(NT):
                    end = pe.transpose(ps_p[:, n % 2, k, :], probs[:, n % 2, k * P:(k + 1) * P], ident[:])
                end.then_inc(pt_ps, 1)

            def values(b, h, k, first):
                if k == 0:
                    pe.wait_ge(pt_lo, b * STEPS + NT * h + NT)
                    pe.wait_ge(v_lo, b * PAIRS + h // 2 + 1)
                    if h or not first:
                        pe.wait_ge(o_ready, b * H + h)
                for part in range(2):
                    end = pe.matmul(ps_o[:], v_st[:, h % 4, k, :, :], pt2[:, h % 2, part, k, :],
                                    start=k == 0 and part == 0, stop=k == NT - 1 and part == 1)
                if k == NT - 1:
                    end.then_inc(o_ps, 1)

            def step(b, n, first=False, last=False):
                if 0 <= n < STEPS:
                    scores(b, n, first)
                if 0 <= n - LAG < STEPS:
                    turn_probs(b, n - LAG, first)
                for h in range(H):
                    for k in range(NT):
                        if n == NT * h + PV_AT[k]:
                            values(b, h, k, first)
                for name, i, part in PLAN.get(n, []):
                    shared_part(b, name, i, part, first, last)

            for n in range(PE_CUT - STEPS, PE_CUT):
                step(0, n, first=True)
            with pe.Fori(0, B - 1) as b:
                for n in range(PE_CUT, PE_CUT + STEPS):
                    step(b, n)
                    step(b + 1, n - STEPS)
            for n in range(PE_CUT, PE_CUT + STEPS):
                step(B - 1, n, last=True)


def program(nc, x, ctx, ctx_t, g_xattn, g_ffn, w_sim, w_sim_cols, b_sim, w_qv, b_qv, wq, wk, w_vsd, wo, x1, out):
    cross_attention(nc, x, ctx, ctx_t, g_xattn, w_sim, w_sim_cols, b_sim, w_qv, b_qv, x1)
    expert_attention(nc, x1, g_ffn, wq, wk, w_vsd, wo, out)


def kernel(x, ctx_1024, g_xattn, g_ffn, L0_xattn_w_sim, L0_xattn_b_sim, L0_xattn_W_qv, L0_xattn_b_qv,
           L0_ffn_Wq, L0_ffn_Wk, L0_ffn_Ws, L0_ffn_Wd, L0_ffn_Wv, L0_ffn_Wo):
    import numpy as np
    import concourse.bacc as bacc
    from concourse.bass_utils import run_bass_kernel_spmd

    x, ctx = np.asarray(x), np.asarray(ctx_1024)
    w_sim, wv, wo = np.asarray(L0_xattn_w_sim), np.asarray(L0_ffn_Wv), np.asarray(L0_ffn_Wo)
    D = x.shape[2]
    arrays = {
        "x": x,
        "ctx": ctx,
        "ctx_t": ctx.transpose(0, 2, 1),
        "g_xattn": np.asarray(g_xattn),
        "g_ffn": np.asarray(g_ffn),
        "w_sim": w_sim,
        "w_sim_cols": w_sim.reshape(3, D // P, P).transpose(2, 0, 1),
        "b_sim": np.asarray(L0_xattn_b_sim),
        "w_qv": np.asarray(L0_xattn_W_qv),
        "b_qv": np.asarray(L0_xattn_b_qv),
        "wq": np.asarray(L0_ffn_Wq),
        "wk": np.asarray(L0_ffn_Wk),
        "w_vsd": np.concatenate([wv.transpose(1, 0, 2).reshape(D, -1), np.asarray(L0_ffn_Ws),
                                 np.asarray(L0_ffn_Wd)], axis=1),
        "wo": wo.reshape(-1, D),
    }
    nc = bacc.Bacc("TRN2", target_bir_lowering=False, num_devices=1)
    feed, args = {}, {}
    for name, a in arrays.items():
        a = np.ascontiguousarray(a)
        feed[f"in_{name}"] = a
        args[name] = nc.dram_tensor(f"in_{name}", a.shape, mybir.dt.from_np(a.dtype), kind="ExternalInput").ap()
    out = nc.dram_tensor("out_dram", x.shape, F32, kind="ExternalOutput").ap()
    x1 = nc.dram_tensor("x1_dram", x.shape, F32, kind="Internal").ap()
    program(nc, **args, x1=x1, out=out)
    r = run_bass_kernel_spmd(nc, [feed], core_ids=[0])
    return r.results[0]["out_dram"]
```

```python
from contextlib import ExitStack

import concourse.bass as bass
from concourse import mybir

F32 = mybir.dt.float32
F32R = mybir.dt.float32r
I32 = mybir.dt.int32
BF16 = mybir.dt.bfloat16
ALU = mybir.AluOpType
ACT = mybir.ActivationFunctionType
AX_X = mybir.AxisListType.X

P = 128
EPS = 1e-5
PASSES = ((0, 0), (0, 1), (1, 0))


def mean_rstd(dve, part, stats, size, mean, work, rstd, done, count):
    both, diff, var, guess = work[:, 0:2], work[:, 2], work[:, 3], work[:, 4]

    def written(n):
        dve.wait_ge(done, count + n)

    if part == 0:
        by_kind = stats.rearrange("p t k -> p k t")
        dve.tensor_tensor(both, by_kind[:, 1:3], by_kind[:, 4:6], ALU.add).then_inc(done, 1)
        dve.tensor_tensor(diff, by_kind[:, 1], by_kind[:, 4], ALU.subtract).then_inc(done, 1)
    elif part == 1:
        written(2)
        dve.tensor_scalar(mean, both[:, 0], 0.5, None, ALU.mult).then_inc(done, 1)
        dve.tensor_scalar(var, both[:, 1], 1.0 / size, EPS, ALU.mult, ALU.add).then_inc(done, 1)
        dve.tensor_tensor(diff, diff, diff, ALU.mult).then_inc(done, 1)
    elif part == 2:
        written(5)
        dve.scalar_tensor_tensor(var, diff, 0.25, var, ALU.mult, ALU.add).then_inc(done, 1)
    elif part == 3:
        written(6)
        dve.tensor_scalar(guess.bitcast(I32), var.bitcast(I32), 1, None, ALU.logical_shift_right).then_inc(done, 1)
    elif part == 4:
        written(7)
        dve.tensor_scalar(rstd.bitcast(I32), guess.bitcast(I32), -1.0, float(0x5F3759DF), ALU.mult,
                          ALU.add).then_inc(done, 1)
    else:
        written(part + 3)
        if part % 3 == 2:
            dve.tensor_tensor(guess, rstd, rstd, ALU.mult).then_inc(done, 1)
        elif part % 3 == 0:
            dve.scalar_tensor_tensor(guess, guess, -0.5, var, ALU.mult, ALU.mult).then_inc(done, 1)
        else:
            dve.scalar_tensor_tensor(rstd, guess, 1.5, rstd, ALU.add, ALU.mult).then_inc(done, 1)


ROOT_PARTS = 14
ROOT_STEPS = 17


def cross_attention(nc, x, ctx, ctx_t, g_xattn, w_sim, w_sim_cols, b_sim, w_qv, b_qv, x1, x1_norm):
    B, T, D = x.shape
    NT, ND = T // P, D // P
    assert NT == ND == 4

    with ExitStack() as mem:
        def sb(name, shape, dt=F32):
            return mem.enter_context(nc.sbuf_tensor(name, shape, dt))

        def sem(name):
            return mem.enter_context(nc.semaphore(name))

        ident = sb("ident", [P, P])
        ones = sb("ones", [P, P])
        w1_row = sb("w1_row", [P, D])
        w_cols = sb("w_cols", [P, 3, ND])
        w2_col, w3_col = w_cols[:, 1, :], w_cols[:, 2, :]
        bsim_col = sb("bsim_col", [P, 1])
        gate = sb("gate", [P, 1])
        gate_raw = sb("gate_raw", [P, 1])
        bias_row = sb("bias_row", [P, D])
        we_raw = sb("we_raw", [P, ND, D])
        wc_raw = sb("wc_raw", [P, ND, D])
        wh = sb("wh", [P, 2, ND, D], F32R)
        weh = sb("weh", [P, 2, ND, D], F32R)
        wec = sb("wec", [P, 2, ND, D], F32R)
        stage = sb("stage", [P, NT, D])
        x_sb = sb("x_sb", [P, NT, D])
        e_sb = sb("e_sb", [P, 2, D])
        e_t = sb("e_t", [P, ND, T])
        e_t2 = sb("e_t2", [P, 2, ND, T], F32R)
        es_t2 = sb("es_t2", [P, 2, ND, T], F32R)
        a_t2 = es_t2
        c_t2 = sb("c_t2", [P, 2, ND, T], F32R)
        c_2 = sb("c_2", [P, 2, NT, D], F32R)
        a_sb = sb("a_sb", [P, 2, T])
        junk = a_sb
        h_t2 = sb("h_t2", [P, 2, ND, T], F32R)
        eh_t2 = sb("eh_t2", [P, 2, ND, T], F32R)
        tmp = sb("tmp", [P, ND, T])
        stats = sb("stats", [P, NT, 6])
        mean = sb("mean", [P, NT])
        work = sb("work", [P, 5, NT])
        rstd = sb("rstd", [P, NT])
        x1_stats = sb("x1_stats", [P, NT, 6])
        all_stats = sb("all_stats", [P, B * NT, 6])
        all_mean = sb("all_mean", [P, B * NT])
        all_work = sb("all_work", [P, 5, B * NT])
        ew1 = sb("ew1", [P, NT])
        nmax = sb("nmax", [P, NT])
        den = sb("den", [P, NT])
        rden = sb("rden", [P, NT])
        mtot = sb("mtot", [P, NT])
        pmax = sb("pmax", [P, 1])
        gmax = sb("gmax", [1, 1])
        ngmax = sb("ngmax", [P, 1])
        bexp = sb("bexp", [P, NT])
        bsum = sb("bsum", [P, 1])
        rtot = sb("rtot", [P, 1])
        batt = sb("batt", [P, NT])
        hc = sb("hc", [P, ND])

        ps_s = mem.enter_context(nc.psum_tensor("ps_s", [P, 2, T], F32))
        ps_h = mem.enter_context(nc.psum_tensor("ps_h", [P, 2, T], F32))
        ps_f = mem.enter_context(nc.psum_tensor("ps_f", [P, 2, D], F32))
        ps_t = mem.enter_context(nc.psum_tensor("ps_t", [P, 4, P], F32))
        ps_b = mem.enter_context(nc.psum_tensor("ps_b", [P, T], F32))

        const_loaded = sem("const_loaded")
        wh_loaded = sem("wh_loaded")
        weh_loaded = sem("weh_loaded")
        wraw_loaded = sem("wraw_loaded")
        ident_ready = sem("ident_ready")
        gate_ready = sem("gate_ready")
        bias_ready = sem("bias_ready")
        slot_loaded = [sem(f"slot_loaded{t}") for t in range(NT)]
        res_loaded = sem("res_loaded")
        x1_stored = sem("x1_stored")
        w_hi = sem("w_hi")
        w_lo = sem("w_lo")
        ct_hi = sem("ct_hi")
        ct_lo = sem("ct_lo")
        c_hi = sem("c_hi")
        c_lo = sem("c_lo")
        stats_done = sem("stats_done")
        newton = sem("newton")
        x1_stats_done = sem("x1_stats_done")
        all_stats_done = sem("all_stats_done")
        x1_newton = sem("x1_newton")
        e_ready = sem("e_ready")
        ew1_ready = sem("ew1_ready")
        et_ps = sem("et_ps")
        et_copied = sem("et_copied")
        es_ready = sem("es_ready")
        es_hi = sem("es_hi")
        es_lo = sem("es_lo")
        et_hi = sem("et_hi")
        et_lo = sem("et_lo")
        s_ready = sem("s_ready")
        nmax_ready = sem("nmax_ready")
        a_exp = sem("a_exp")
        rden_ready = sem("rden_ready")
        a_ready = sem("a_ready")
        at_ps = sem("at_ps")
        at_hi = sem("at_hi")
        at_lo = sem("at_lo")
        ht_ps = sem("ht_ps")
        ht_hi = sem("ht_hi")
        ht_lo = sem("ht_lo")
        eh_ready = sem("eh_ready")
        eh_hi = sem("eh_hi")
        eh_lo = sem("eh_lo")
        b_dve = sem("b_dve")
        b_pe = sem("b_pe")
        bexp_ready = sem("bexp_ready")
        hc_ready = sem("hc_ready")
        wec_ready = sem("wec_ready")
        wec_hi = sem("wec_hi")
        wec_lo = sem("wec_lo")
        feat_ps = sem("feat_ps")
        x1_ready = sem("x1_ready")
        xb_ready = sem("xb_ready")

        w_blocks = w_qv.rearrange("(m k p) n -> m p k n", m=4, p=P)
        x_dram = x.rearrange("b (t p) d -> b p t d", p=P)
        c_dram = ctx.rearrange("b (t p) d -> b p t d", p=P)
        ct_dram = ctx_t.rearrange("b (k p) j -> b p k j", p=P)
        x1_dram = x1.rearrange("b (t p) d -> b p t d", p=P)

        def of(dram, b):
            return dram[bass.ds(b, 1)].rearrange("o p t d -> (o p) t d")

        def cast_hi(act, pair, k, operand):
            return act.activation(pair[:, 0, k, :], operand[:, k, :], ACT.Copy)

        def take_lo(eng, pair, k, operand):
            return eng.tensor_tensor(pair[:, 1, k, :], operand[:, k, :], pair[:, 0, k, :].bitcast(F32), ALU.subtract)

        def stage_loaded(eng, b, t, use):
            eng.wait_ge(slot_loaded[t], b * (3 * 16) + (use + 1) * 16)

        wh_raw, weh_raw = x_sb, wc_raw

        block = mem.enter_context(nc.Block())

        @block.sync
        def _(sp):
            def load_x(b, first=False):
                for t in range(NT):
                    if not first:
                        sp.wait_ge(c_lo, b * NT - NT + t + 1)
                    sp.dma_start(stage[:, t, :], of(x_dram, b)[:, t, :]).then_inc(slot_loaded[t], 16)

            def load_ctx(b):
                for k in range(ND):
                    sp.wait_ge(e_ready, b * NT + k + 1)
                    sp.dma_start(stage[:, k, :], of(ct_dram, b)[:, k, :]).then_inc(slot_loaded[k], 16)
                for t in range(NT):
                    sp.wait_ge(ct_lo, b * ND + t + 1)
                    sp.dma_start(stage[:, t, :], of(c_dram, b)[:, t, :]).then_inc(slot_loaded[t], 16)

            def load_residual(b):
                sp.dma_start(x_sb[:], of(x_dram, b)).then_inc(res_loaded, 16)

            def store(b, t):
                sp.wait_ge(x1_ready, b * NT + t + 1)
                sp.dma_start(of(x1_dram, b)[:, t, :], x_sb[:, t, :]).then_inc(x1_stored, 16)

            def next_loads(b, more):
                load_ctx(b + 1)
                for t in range(NT - 1):
                    store(b, t)
                if more:
                    load_x(b + 2)
                store(b, NT - 1)
                sp.wait_ge(x1_stored, (b + 1) * NT * 16)
                sp.wait_ge(x1_stats_done, (b + 1) * NT)
                load_residual(b + 1)

            load_x(0, True)
            sp.dma_start(w1_row[:], w_sim[0:D].partition_broadcast(P)).then_inc(const_loaded, 16)
            sp.dma_start(w_cols[:], w_sim_cols).then_inc(const_loaded, 16)
            sp.dma_start(gate_raw[:], g_xattn.partition_broadcast(P)).then_inc(const_loaded, 16)
            sp.dma_start(bsim_col[:], b_sim.partition_broadcast(P)).then_inc(const_loaded, 16)
            sp.dma_start(bias_row[:], b_qv.partition_broadcast(P)).then_inc(const_loaded, 16)
            sp.dma_start(wh_raw[:], w_blocks[1]).then_inc(wh_loaded, 16)
            load_ctx(0)
            sp.dma_start(weh_raw[:], w_blocks[2]).then_inc(weh_loaded, 16)
            sp.dma_start(we_raw[:], w_blocks[0]).then_inc(wraw_loaded, 16)
            load_x(1)
            sp.wait_ge(w_lo, ND)
            load_residual(0)
            sp.wait_ge(w_lo, 2 * ND)
            sp.dma_start(wc_raw[:], w_blocks[3]).then_inc(wraw_loaded, 16)
            with sp.Fori(0, B - 2) as b:
                next_loads(b, True)
            next_loads(B - 2, False)
            for t in range(NT):
                store(B - 1, t)
            sp.wait_ge(x1_stored, B * NT * 16)

        @block.gpsimd
        def _(pool):
            pool.memset(ident[:], 0.0).then_inc(ident_ready, 1)
            pool.memset(ones[:], 1.0).then_inc(ident_ready, 1)
            pool.wait_ge(ident_ready, 2)
            pool.affine_select(out=ident[:], in_=ident[:], compare_op=ALU.not_equal, fill=1.0, base=0,
                               pattern=[[-1, P]], channel_multiplier=1).then_inc(ident_ready, 1)

            def ctx_lo(b):
                for t in range(NT):
                    pool.wait_ge(c_hi, b * NT + t + 1)
                    take_lo(pool, c_2, t, stage).then_inc(c_lo, 1)

            def rest(b):
                for k in range(ND):
                    pool.wait_ge(et_hi, b * ND + k + 1)
                    take_lo(pool, e_t2, k, e_t).then_inc(et_lo, 1)
                for k in range(ND):
                    pool.wait_ge(eh_hi, b * ND + k + 1)
                    take_lo(pool, eh_t2, k, tmp).then_inc(eh_lo, 1)
                pool.wait_ge(res_loaded, b * 16 + 16)
                pool.wait_ge(bias_ready, 1)
                pool.tensor_tensor(x_sb[:], x_sb[:], bias_row[:].unsqueeze(1).broadcast_to([P, NT, D]),
                                   ALU.add).then_inc(xb_ready, 1)
                for k in range(ND):
                    pool.wait_ge(wec_hi, b * ND + k + 1)
                    take_lo(pool, wec, k, tmp).then_inc(wec_lo, 1)

            ctx_lo(0)
            for n in range(2 * ND):
                pool.wait_ge(w_hi, n + 1)
                take_lo(pool, *((wh, n, wh_raw) if n < ND else (weh, n - ND, weh_raw))).then_inc(w_lo, 1)
            with pool.Fori(0, B - 1) as b:
                rest(b)
                ctx_lo(b + 1)
            rest(B - 1)

        def turned_e(t):
            return ps_s[:, 0, :].rearrange("p (k t) -> p k t", k=ND) if t % 2 else ps_t[:]

        @block.scalar
        def _(act):
            act.wait_ge(const_loaded, 5 * 16)
            act.activation(gate[:], gate_raw[:], ACT.Tanh).then_inc(gate_ready, 1)

            def copy_e(b, t):
                act.wait_ge(et_ps, b * NT + t + 1)
                act.activation(e_t[:, :, t * P:(t + 1) * P], turned_e(t), ACT.Copy).then_inc(et_copied, 1)

            def ctx_t_hi(b, slots):
                for k in range(slots.start, slots.stop):
                    stage_loaded(act, b, k, 1)
                    cast_hi(act, c_t2, k, stage).then_inc(ct_hi, 1)

            def es_ctx_hi(b):
                for k in range(ND):
                    act.wait_ge(es_ready, b * ND + k + 1)
                    act.activation(es_t2[:, 0, k, :], tmp[:, k, :], ACT.Copy).then_inc(es_hi, 1)
                for t in range(NT):
                    stage_loaded(act, b, t, 2)
                    cast_hi(act, c_2, t, stage).then_inc(c_hi, 1)

            def weights_hi(pair, raw, loaded):
                act.wait_ge(loaded, 16)
                for k in range(ND):
                    cast_hi(act, pair, k, raw).then_inc(w_hi, 1)

            def softmax_exp(b, t):
                act.wait_ge(nmax_ready, b * NT + t + 1)
                if t >= 2:
                    act.wait_ge(at_ps, b * NT + t - 1)
                act.activation(a_sb[:, t % 2, :], ps_s[:, t % 2, :], ACT.Exp, bias=nmax[:, t:t + 1],
                               accum_out=den[:, t:t + 1]).then_inc(a_exp, 1)

            def probs_hi(b, t):
                act.wait_ge(at_ps, b * NT + t + 1)
                act.activation(a_t2[:, 0, :, t * P:(t + 1) * P], ps_t[:], ACT.Copy).then_inc(at_hi, 1)

            def softmax(b):
                for t in range(NT + 1):
                    if t < NT:
                        softmax_exp(b, t)
                    if t:
                        probs_hi(b, t - 1)

            def attended(b, first):
                if not first:
                    act.wait_ge(feat_ps, b * NT)
                for k in range(ND):
                    act.activation(e_t2[:, 0, k, :], e_t[:, k, :], ACT.Copy).then_inc(et_hi, 1)
                for k in range(ND):
                    act.wait_ge(ht_ps, b * ND + k + 1)
                    act.activation(h_t2[:, 0, k, :], ps_h[:, k % 2, :], ACT.Copy).then_inc(ht_hi, 1)
                    act.wait_ge(eh_ready, b * ND + k + 1)
                    act.activation(eh_t2[:, 0, k, :], tmp[:, k, :], ACT.Copy).then_inc(eh_hi, 1)
                    if k == 1:
                        act.wait_ge(b_dve, b * 6 + 4)
                        act.activation(bexp[:], mtot[:], ACT.Exp, bias=ngmax[:, 0:1],
                                       accum_out=bsum[:, 0:1]).then_inc(bexp_ready, 1)
                for k in range(ND):
                    act.wait_ge(wec_ready, b * ND + k + 1)
                    act.activation(wec[:, 0, k, :], tmp[:, k, :], ACT.Copy).then_inc(wec_hi, 1)

            def front(b):
                for t in range(NT):
                    copy_e(b, t)
                    if t == 1:
                        ctx_t_hi(b, slice(0, 2))
                ctx_t_hi(b, slice(2, ND))
                es_ctx_hi(b)

            front(0)
            weights_hi(wh, wh_raw, wh_loaded)
            softmax(0)
            weights_hi(weh, weh_raw, weh_loaded)
            attended(0, True)
            with act.Fori(0, B - 1) as b:
                act.wait_ge(hc_ready, b * ND + ND)
                act.wait_ge(et_lo, b * ND + ND)
                front(b + 1)
                softmax(b + 1)
                attended(b + 1, False)

        @block.vector
        def _(dve):
            def row_stats(b):
                for t in range(NT):
                    stage_loaded(dve, b, t, 0)
                    dve.bn_stats(stats[:, t, :], stage[:, t, :]).then_inc(stats_done, 1)

            def root(b, part):
                if part == 0:
                    dve.wait_ge(stats_done, b * NT + NT)
                mean_rstd(dve, part, stats[:], D, mean[:], work[:], rstd[:], newton, b * ROOT_STEPS)

            def normalise_x(b, t):
                if t == 0:
                    dve.wait_ge(newton, b * ROOT_STEPS + ROOT_STEPS)
                if t >= 2:
                    dve.wait_ge(et_ps, b * NT + t - 1)
                    dve.wait_ge(ew1_ready, b * (NT + 1) + t - 1)
                dve.tensor_scalar(e_sb[:, t % 2, :], stage[:, t, :], mean[:, t:t + 1], rstd[:, t:t + 1],
                                  ALU.subtract, ALU.mult).then_inc(e_ready, 1)
                dve.wait_ge(e_ready, b * NT + t + 1)
                dve.tensor_tensor_reduce(out=junk[:, t % 2, :], in0=e_sb[:, t % 2, :], in1=w1_row[:], scale=1.0,
                                         scalar=0.0, op0=ALU.mult, op1=ALU.add,
                                         accum_out=ew1[:, t:t + 1]).then_inc(ew1_ready, 1)

            def ctx_t_lo(b, slots):
                for k in range(slots.start, slots.stop):
                    dve.wait_ge(ct_hi, b * ND + k + 1)
                    take_lo(dve, c_t2, k, stage).then_inc(ct_lo, 1)

            def scaled_e(b, k, first):
                if not first:
                    dve.wait_ge(wec_lo, b * ND - ND + k + 1)
                dve.tensor_scalar(tmp[:, k, :], e_t[:, k, :], w3_col[:, k:k + 1], w2_col[:, k:k + 1],
                                  ALU.mult, ALU.add).then_inc(es_ready, 1)

            def scaled_e_lo(b, k):
                dve.wait_ge(es_hi, b * ND + k + 1)
                take_lo(dve, es_t2, k, tmp).then_inc(es_lo, 1)

            def front(b, first):
                for t in range(2, NT):
                    normalise_x(b, t)
                ctx_t_lo(b, slice(0, 2))
                dve.wait_ge(ew1_ready, b * (NT + 1) + NT)
                dve.tensor_scalar(ew1[:], ew1[:], bsim_col[:, 0:1], None, ALU.add).then_inc(ew1_ready, 1)
                if not first:
                    residual(b - 1, 0)
                dve.wait_ge(et_copied, b * NT + NT)
                for k in range(ND):
                    scaled_e(b, k, first)
                    if k == 1:
                        ctx_t_lo(b, slice(2, ND))
                    if k >= 1:
                        scaled_e_lo(b, k - 1)
                scaled_e_lo(b, ND - 1)
                if not first:
                    residual(b - 1, 1)
                    x1_row_stats(b - 1, 0)
                    x1_row_stats(b - 1, 1)

            def row_max(b, t):
                dve.wait_ge(s_ready, b * NT + t + 1)
                dve.tensor_reduce(nmax[:, t:t + 1], ps_s[:, t % 2, :], AX_X, ALU.max, negate=True).then_inc(
                    nmax_ready, 1)

            def normalise(b, t):
                dve.wait_ge(a_exp, b * NT + t + 1)
                dve.reciprocal(rden[:, t:t + 1], den[:, t:t + 1]).then_inc(rden_ready, 1)
                dve.wait_ge(rden_ready, b * NT + t + 1)
                dve.tensor_scalar(a_sb[:, t % 2, :], a_sb[:, t % 2, :], rden[:, t:t + 1], None,
                                  ALU.mult).then_inc(a_ready, 1)

            def probs_lo(b, t):
                dve.wait_ge(at_hi, b * NT + t + 1)
                dve.tensor_tensor(a_t2[:, 1, :, t * P:(t + 1) * P], ps_t[:],
                                  a_t2[:, 0, :, t * P:(t + 1) * P].bitcast(F32), ALU.subtract).then_inc(at_lo, 1)

            def softmax(b, first):
                row_max(b, 0)
                row_max(b, 1)
                for t in range(NT):
                    normalise(b, t)
                    if 2 <= t + 1 < NT:
                        row_max(b, t + 1)
                    if t == NT - 1:
                        dve.wait_ge(nmax_ready, b * NT + NT)
                        dve.scalar_tensor_tensor(mtot[:], nmax[:], -1.0, ew1[:], ALU.mult, ALU.add).then_inc(b_dve, 1)
                    probs_lo(b, t)
                    if t == 0 and not first:
                        residual(b - 1, 2)
                    if t == 1 and not first:
                        x1_row_stats(b - 1, 2)
                dve.wait_ge(b_dve, b * 6 + 1)
                dve.reduce_max(pmax[:], mtot[:], AX_X).then_inc(b_dve, 1)
                if not first:
                    residual(b - 1, NT - 1)

            def attended(b, first, more):
                if not first:
                    x1_row_stats(b - 1, NT - 1)
                if more:
                    row_stats(b + 1)
                for k in range(ND):
                    if k == 0:
                        dve.wait_ge(b_pe, b * 4 + 1)
                        dve.tensor_reduce(gmax[:], ps_b[0:1, 0:P], AX_X, ALU.max, negate=True).then_inc(b_dve, 1)
                    elif k == 1:
                        dve.wait_ge(b_pe, b * 4 + 2)
                        dve.tensor_copy(ngmax[:], ps_b[:, 0:1]).then_inc(b_dve, 1)
                    elif k == 2:
                        dve.wait_ge(b_pe, b * 4 + 3)
                        dve.reciprocal(rtot[:], ps_b[:, 0:1]).then_inc(b_dve, 1)
                        dve.wait_ge(b_dve, b * 6 + 5)
                        dve.tensor_scalar(batt[:], bexp[:], rtot[:, 0:1], None, ALU.mult).then_inc(b_dve, 1)
                    dve.wait_ge(ht_hi, b * ND + k + 1)
                    dve.tensor_tensor(h_t2[:, 1, k, :], ps_h[:, k % 2, :], h_t2[:, 0, k, :].bitcast(F32),
                                      ALU.subtract).then_inc(ht_lo, 1)
                    dve.tensor_tensor(tmp[:, k, :], ps_h[:, k % 2, :], e_t[:, k, :], ALU.mult).then_inc(eh_ready, 1)
                    if more:
                        for part in range(2 + 3 * k if k else 0, 5 + 3 * k):
                            root(b + 1, part)
                dve.wait_ge(b_pe, b * 4 + 4)
                for k in range(ND):
                    if k >= 2:
                        dve.wait_ge(hc_ready, b * ND + k - 1)
                    dve.tensor_tensor_reduce(out=junk[:, k % 2, :], in0=e_t[:, k, :], in1=ps_b[:], scale=1.0, scalar=0.0,
                                             op0=ALU.mult, op1=ALU.add, accum_out=hc[:, k:k + 1]).then_inc(hc_ready, 1)
                dve.wait_ge(wraw_loaded, 2 * 16)
                for k in range(ND):
                    dve.wait_ge(hc_ready, b * ND + k + 1)
                    dve.wait_ge(eh_lo, b * ND + k + 1)
                    dve.scalar_tensor_tensor(tmp[:, k, :], wc_raw[:, k, :], hc[:, k:k + 1], we_raw[:, k, :],
                                             ALU.mult, ALU.add).then_inc(wec_ready, 1)
                if not first:
                    keep_stats(b - 1)
                if more:
                    normalise_x(b + 1, 0)
                    normalise_x(b + 1, 1)
                if not first:
                    dve.wait_ge(all_stats_done, b)

            def residual(b, t):
                if t == 0:
                    dve.wait_ge(xb_ready, b + 1)
                dve.wait_ge(feat_ps, b * NT + t + 1)
                dve.scalar_tensor_tensor(x_sb[:, t, :], ps_f[:, t % 2, :], gate[:, 0:1], x_sb[:, t, :],
                                         ALU.mult, ALU.add).then_inc(x1_ready, 1)

            def x1_row_stats(b, t):
                dve.wait_ge(x1_ready, b * NT + t + 1)
                dve.bn_stats(x1_stats[:, t, :], x_sb[:, t, :]).then_inc(x1_stats_done, 1)

            def keep_stats(b):
                dve.wait_ge(x1_stats_done, b * NT + NT)
                dve.tensor_scalar(all_stats[:, bass.ds(b * NT, NT), :], x1_stats[:], 1.0, None,
                                  ALU.mult).then_inc(all_stats_done, 1)

            row_stats(0)
            for part in range(ROOT_PARTS):
                root(0, part)
            dve.wait_ge(const_loaded, 5 * 16)
            normalise_x(0, 0)
            normalise_x(0, 1)
            front(0, True)
            dve.wait_ge(gate_ready, 1)
            dve.tensor_scalar(bias_row[:], bias_row[:], gate[:, 0:1], None, ALU.mult).then_inc(bias_ready, 1)
            softmax(0, True)
            attended(0, True, True)
            with dve.Fori(0, B - 2) as b:
                front(b + 1, False)
                softmax(b + 1, False)
                attended(b + 1, False, True)
            front(B - 1, False)
            softmax(B - 1, False)
            attended(B - 1, False, False)
            for t in range(NT):
                residual(B - 1, t)
            for t in range(NT):
                x1_row_stats(B - 1, t)
            keep_stats(B - 1)
            dve.wait_ge(all_stats_done, B)
            all_rstd = x1_norm[:, 0]
            for part in range(ROOT_PARTS):
                mean_rstd(dve, part, all_stats[:], D, all_mean[:], all_work[:], all_rstd, x1_newton, 0)
            dve.wait_ge(x1_newton, ROOT_STEPS)
            dve.scalar_tensor_tensor(x1_norm[:, 1], all_mean[:], -1.0, all_rstd, ALU.mult,
                                     ALU.mult).then_inc(x1_newton, 1)
            dve.wait_ge(x1_newton, ROOT_STEPS + 1)

        @block.tensor
        def _(pe):
            pe.wait_ge(ident_ready, 3)

            def product(out, left, right, start, stop, ready=None):
                n = 0
                for k in range(ND):
                    if ready:
                        ready(k)
                    for l, r in PASSES:
                        n += 1
                        last = pe.matmul(out, left(l, k), right(r, k), start=start and n == 1,
                                         stop=stop and n == ND * len(PASSES))
                return last

            def turn_e(b, t):
                pe.wait_ge(e_ready, b * NT + t + 1)
                if t >= 2:
                    pe.wait_ge(et_copied, b * NT + t - 1)
                for k in range(ND):
                    last = pe.transpose(turned_e(t)[:, k, :], e_sb[:, t % 2, k * P:(k + 1) * P], ident[:])
                last.then_inc(et_ps, 1)

            def scores(b, t):
                def ready(k):
                    pe.wait_ge(es_lo, b * ND + k + 1)
                    pe.wait_ge(ct_lo, b * ND + k + 1)

                if t >= 2:
                    pe.wait_ge(a_exp, b * NT + t - 1)
                product(ps_s[:, t % 2, :], lambda l, k: es_t2[:, l, k, t * P:(t + 1) * P],
                        lambda r, k: c_t2[:, r, k, :], True, True, ready if t == 0 else None).then_inc(s_ready, 1)

            def turn_a(b, t):
                pe.wait_ge(a_ready, b * NT + t + 1)
                if t == 0:
                    pe.wait_ge(et_copied, b * NT + NT)
                else:
                    pe.wait_ge(at_lo, b * NT + t)
                for k in range(NT):
                    last = pe.transpose(ps_t[:, k, :], a_sb[:, t % 2, k * P:(k + 1) * P], ident[:])
                last.then_inc(at_ps, 1)

            def attend(b, k):
                if k == 0:
                    pe.wait_ge(at_lo, b * NT + NT)
                    pe.wait_ge(c_lo, b * NT + NT)
                if k >= 2:
                    pe.wait_ge(eh_ready, b * ND + k - 1)
                product(ps_h[:, k % 2, :], lambda l, j: c_2[:, l, j, k * P:(k + 1) * P],
                        lambda r, j: a_t2[:, r, j, :], True, True).then_inc(ht_ps, 1)

            def row_weights(b, step):
                if step == 0:
                    pe.wait_ge(b_dve, b * 6 + 2)
                    pe.transpose(ps_b[0:1, 0:P], pmax[:], ident[:]).then_inc(b_pe, 1)
                elif step == 1:
                    pe.wait_ge(b_dve, b * 6 + 3)
                    pe.matmul(ps_b[:, 0:1], ones[0:1, :], gmax[:], start=True, stop=True).then_inc(b_pe, 1)
                elif step == 2:
                    pe.wait_ge(bexp_ready, b + 1)
                    pe.matmul(ps_b[:, 0:1], ones[:], bsum[:], start=True, stop=True).then_inc(b_pe, 1)
                else:
                    pe.wait_ge(b_dve, b * 6 + 6)
                    for t in range(NT):
                        last = pe.matmul(ps_b[:, t * P:(t + 1) * P], batt[:, t:t + 1].broadcast_to([P, P]), ident[:],
                                         start=True, stop=True)
                    last.then_inc(b_pe, 1)

            def feats(b, t, part):
                out = ps_f[:, t % 2, :]
                cols = slice(t * P, (t + 1) * P)
                if part == 0:
                    if t >= 2:
                        pe.wait_ge(x1_ready, b * NT + t - 1)
                    pe.wait_ge(w_lo, ND)
                    product(out, lambda l, k: h_t2[:, l, k, cols], lambda r, k: wh[:, r, k, :], True, False,
                            lambda k: pe.wait_ge(ht_lo, b * ND + k + 1))
                elif part == 1:
                    pe.wait_ge(w_lo, 2 * ND)
                    product(out, lambda l, k: eh_t2[:, l, k, cols], lambda r, k: weh[:, r, k, :], False, False,
                            lambda k: pe.wait_ge(eh_lo, b * ND + k + 1))
                else:
                    pe.wait_ge(wec_lo, b * ND + ND)
                    pe.wait_ge(et_lo, b * ND + ND)
                    product(out, lambda l, k: e_t2[:, l, k, cols], lambda r, k: wec[:, r, k, :], False,
                            True).then_inc(feat_ps, 1)

            LAST_FEATS = [(2, 2), (3, 0), (3, 1), (3, 2)]

            def first_feats(b, more):
                for k in range(ND):
                    attend(b, k)
                    row_weights(b, k)
                for n, (t, part) in enumerate([(0, 0), (1, 0), (0, 1), (1, 1), (0, 2), (1, 2)]):
                    feats(b, t, part)
                    if more:
                        for t_next in {2: (0, 1), 3: (2,), 4: (3,)}.get(n, ()):
                            turn_e(b + 1, t_next)
                for part in range(2):
                    feats(b, 2, part)

            def softmax(b, first):
                scores(b, 0)
                for t in range(NT):
                    if t + 1 < NT:
                        scores(b, t + 1)
                    if not first and t != 1:
                        feats(b - 1, *LAST_FEATS[max(t - 1, 0)])
                    turn_a(b, t)
                if not first:
                    feats(b - 1, *LAST_FEATS[-1])

            for t in range(NT):
                turn_e(0, t)
            softmax(0, True)
            with pe.Fori(0, B - 1) as b:
                first_feats(b, True)
                softmax(b + 1, False)
            first_feats(B - 1, False)
            for t, part in LAST_FEATS:
                feats(B - 1, t, part)


def expert_attention(nc, x1, x1_norm, g_ffn, wq, wk, w_vsd, wo, out):
    B, T, D = x1.shape
    NT, ND = T // P, D // P
    H, DH = 8, 64
    NV = wo.shape[0]
    E = NV // DH
    NL = H * E
    NX = NV + 2 * NL
    PAIRS = H // 2
    KZ = -(-NV // P)
    SCALE = float(DH) ** -0.5
    assert NT == ND == 4 and 2 * DH == P and w_vsd.shape[1] == NX and wq.shape[1] == D and H * DH == D

    SHARED = KZ * P - NV

    def tile_at(k):
        return min(k * P, NV - P)

    STEPS = H * NT
    CUT = 21
    EARLY = 19
    TURN_Y_AT = [-11, -11, -10, -9]
    EXPERTS_AT = [[-8], [-8, -7], [-5, -4], [-4]]
    Q_AT = [[-6, -6], [2, 2], [6, 6], [18, 18]]
    K_AT = [[-2, -2], [4, 4], [10, 10], [19, 19]]
    PV_AT = [7, 8, 8, 9]
    TURN_O_AT = [17, 25, 34, 41]
    TURN_Z_AT = [45, 45, 45]
    RESULT_AT = [[46], [47], [48], [49]]
    NORMALISE_AT = -13
    GATES_AT = -3
    ROUTE_AT = [-1, -1, 2]
    VALUE_AT = [5, 12, 18, 23]
    MIX_PLACES = [[1, 1], [3, 0], [3, 1], [4, 0]]
    MIX_LAST = [[1, 2], [2, 0], [2, 2], [3, 0]]
    HI_BEHIND = {"turn_z": 0, "q": 1, "experts": 0}
    LO_BEHIND = {"q": 2, "k": 2, "turn_z": 0}
    LAG = 2
    SPLIT_LAG = LAG + 1
    SUM_AT = PV_AT[-1] + 1
    PAIR = 2 * NT
    AT = {}
    for t in range(NT):
        AT["turn_y", t] = [TURN_Y_AT[t]]
        AT["experts", t] = EXPERTS_AT[t]
        AT["result", t] = RESULT_AT[t]
    for p in range(PAIRS):
        AT["q", p] = Q_AT[p]
        AT["k", p] = K_AT[p]
        AT["turn_o", p] = [TURN_O_AT[p]]
    for k in range(KZ):
        AT["turn_z", k] = [TURN_Z_AT[k]]
    BEGINS = min(min(steps) for steps in AT.values())
    ENDS = max(max(steps) for steps in AT.values())

    assert CUT - STEPS <= BEGINS and EARLY - STEPS <= NORMALISE_AT and ENDS < CUT + STEPS and ENDS + 1 < EARLY + STEPS

    def parts_at(n):
        found = [(*what, part, len(steps)) for what, steps in AT.items() for part, at in enumerate(steps) if at == n]
        return sorted(found, key=lambda one: AT[one[:2]][0] == n)

    def ended(n):
        return [what[:2] for what in parts_at(n) if what[2] == what[3] - 1]

    RING = 3
    ORDER = [what[:2] for n in range(CUT, CUT + STEPS) for what in parts_at(n) + parts_at(n - STEPS) if what[2] == 0]
    AHEAD = [what for what in ORDER if AT[what][0] < CUT]
    assert len(ORDER) % RING == 0 and all(what in AHEAD for what in ORDER[-RING:])

    def bank_of(what):
        return ORDER.index(what) % RING

    with ExitStack() as mem:
        def sb(name, shape, dt=F32):
            return mem.enter_context(nc.sbuf_tensor(name, shape, dt))

        def sem(name):
            return mem.enter_context(nc.semaphore(name + "_2"))

        ident = sb("ident_2", [P, P])
        gate = sb("gate_2", [P, 1])
        gate_raw = sb("gate_raw_2", [P, 1])
        wq2 = sb("wq2", [P, 2, ND, D], F32R)
        wk2 = sb("wk2", [P, 2, ND, D], F32R)
        wx2 = sb("wx2", [P, 2, ND, NX], F32R)
        wo2 = sb("wo2", [P, 2, KZ, D], F32R)
        stage = sb("stage_2", [P, NT, D])
        y_t2 = sb("y_t2", [P, 2, ND, T], F32R)
        q_nat = sb("q_nat", [P, 2, T], F32R)
        q_st = sb("q_st", [P, 2, 2, 2, T], F32R)
        k_st = sb("k_st", [P, 2, 2, T], F32R)
        xv = sb("xv", [P, NT, E, DH])
        logits = sb("logits", [P, 2, NT * H, E])
        beaten = sb("beaten", [P, 2 * NT * H, E, E], BF16)
        rank = logits[:].rearrange("p s g e -> p (s g) e")
        pick = sb("pick", [P, 2, NT, H, E])
        sig = sb("sig", [P, NT * H, E])
        coef = sb("coef", [P, H, NT, E])
        v_acc = sb("v_acc", [P, 2, NT, 2, DH])
        v_tmp = sb("v_tmp", [P, NT, 2, DH])
        v_st = sb("v_st", [P, 4, NT, 2, DH], F32R)
        probs = sb("probs", [P, 2, T])
        pt2 = sb("pt2", [P, 2, 2, NT, T], F32R)
        o_tmp = sb("o_tmp", [P, T])
        o_t = sb("o_t", [P, T])
        attn = sb("attn", [P, NT, 2, DH])
        z = sb("z", [P, NT, NV])
        z_tmp = sb("z_tmp", [P, NT, E, DH])
        z_t2 = sb("z_t2", [P, 2, KZ, T], F32R)
        x_res = sb("x_res", [P, NT, D])
        norm = sb("norm", [P, 2, NT])
        nmax = sb("nmax_2", [P, STEPS])
        den = sb("den_2", [P, H, NT])
        rden = sb("rden_2", [P, H, NT])

        ps_s = mem.enter_context(nc.psum_tensor("ps_s_2", [P, 2, T], F32))
        ps_p = mem.enter_context(nc.psum_tensor("ps_p_2", [P, 2, NT, P], F32))
        ps_o = mem.enter_context(nc.psum_tensor("ps_o_2", [P, T], F32))
        ps_r = mem.enter_context(nc.psum_tensor("ps_r_2", [P, RING, D], F32))

        gate_loaded = sem("gate_loaded")
        cleared = sem("cleared")
        ident_ready = sem("ident_ready")
        gate_ready = sem("gate_ready")
        x1_loaded = sem("x1_loaded")
        xres_loaded = sem("xres_loaded")
        out_stored = sem("out_stored")
        w_loaded = {name: [sem(f"{name}_loaded{k}") for k in range(KZ if name == "wo" else ND)]
                    for name in ("wq", "wk", "wx", "wo")}
        w_hi = {name: sem(name + "_hi") for name in ("wq", "wk", "wx", "wo")}
        w_lo = {name: sem(name + "_lo") for name in ("wq", "wk", "wx", "wo")}
        norm_ready = sem("norm_ready")
        y_dve = sem("y_dve")
        y_act = sem("y_act")
        yt_ps = sem("yt_ps")
        yt_hi = sem("yt_hi")
        yt_lo = sem("yt_lo")
        ex_ps = sem("ex_ps")
        xv_ready = sem("xv_ready")
        logits_ready = sem("logits_ready")
        compared = sem("compared")
        gates = sem("gates")
        sig_exp = sem("sig_exp")
        pick_ready = sem("pick_ready")
        mask_ready = sem("mask_ready")
        q_ps = sem("q_ps")
        q_hi = sem("q_hi")
        q_lo = sem("q_lo")
        q_spread = [sem("q_spread0"), sem("q_spread1")]
        k_ps = sem("k_ps")
        k_hi = sem("k_hi")
        k_lo = sem("k_lo")
        v_steps = sem("v_steps")
        v_hi = sem("v_hi")
        v_lo = sem("v_lo")
        s_ready = sem("s_ready")
        nmax_ready = sem("nmax_ready")
        p_exp = sem("p_exp")
        pt_ps = sem("pt_ps")
        pt_hi = sem("pt_hi")
        pt_lo = sem("pt_lo")
        o_ps = sem("o_ps")
        o_half = sem("o_half")
        o_ready = sem("o_ready")
        to_ps = sem("to_ps")
        attn_ready = sem("attn_ready")
        rden_ready = sem("rden_ready")
        coef_ready = sem("coef_ready")
        z_dve = sem("z_dve")
        z_pool = sem("z_pool")
        zt_ps = sem("zt_ps")
        zt_hi = sem("zt_hi")
        zt_lo = sem("zt_lo")
        res_ps = sem("res_ps")
        out_ready = sem("out_ready")

        x1_dram = x1.rearrange("b (t p) d -> b p t d", p=P)
        out_dram = out.rearrange("b (t p) d -> b p t d", p=P)
        weights = {"wq": wq2, "wk": wk2, "wx": wx2, "wo": wo2}
        WEIGHT_TILES = [(name, k) for name in ("wx", "wq", "wk", "wo") for k in range(KZ if name == "wo" else ND)]

        def of(dram, b):
            return dram[bass.ds(b, 1)].rearrange("o p t d -> (o p) t d")

        def own_rows(name, k):
            return slice(SHARED if (name, k) == ("wo", KZ - 1) else 0, P)

        def weight_tile(name, half, k):
            return weights[name][own_rows(name, k), half, k, :]

        def pieces(buffer):
            dims = "abcde"[:len(buffer.shape) - 1]
            flat = buffer[:].rearrange(f"p {' '.join(dims)} -> p ({' '.join(dims)})") if len(dims) > 1 else buffer[:]
            return [flat[:, i * D:(i + 1) * D] for i in range(flat.shape[1] // D)]

        PASS = [piece for buffer in (v_acc, v_tmp, o_tmp, probs, z_tmp, z, attn, o_t, x_res) for piece in pieces(buffer)]
        assert len(WEIGHT_TILES) <= len(PASS)

        def passing(name, k):
            return PASS[WEIGHT_TILES.index((name, k))][own_rows(name, k), 0:weights[name].shape[3]]

        SPLIT_AT = {"wx": NORMALISE_AT, "wq": NORMALISE_AT + 1, "wk": EXPERTS_AT[0][0], "wo": EXPERTS_AT[2][0]}
        VECTOR_SPLITS = {"wx": SPLIT_AT["wx"], "wo": SPLIT_AT["wo"] + 1}

        def take_weight_lo(eng, name, k):
            eng.wait_ge(w_hi[name], k + 1)
            eng.tensor_tensor(weight_tile(name, 1, k), passing(name, k), weight_tile(name, 0, k).bitcast(F32),
                              ALU.subtract).then_inc(w_lo[name], 1)

        def head_rows(a):
            return slice(a * DH, a * DH + DH)

        COMPARISONS = 2 * (E - 1)

        V_STEPS = 2 * E - 1

        def pair_values(p, half):
            slot = p % 2 * 2
            return v_st[:, slot:slot + 2, :, half, :].rearrange("p a t k -> p t a k")

        Z_STEPS = 2 * H - 1

        def mix_product(eng, done, tiles, b, h):
            p, a = h // 2, h % 2
            zv = z[:, tiles, :].rearrange("p t (e k) -> p t e k", e=E)
            if a == 0:
                eng.wait_ge(attn_ready, b * PAIRS + p + 1)
            eng.wait_ge(coef_ready, b * PAIRS + p + 1)
            if h:
                eng.wait_ge(done, b * Z_STEPS + 2 * h - 1)
            shape = [P, tiles.stop - tiles.start, E, DH]
            eng.tensor_tensor(z_tmp[:, tiles] if h else zv, attn[:, tiles, a, :].unsqueeze(2).broadcast_to(shape),
                              coef[:, h, tiles, :].unsqueeze(3).broadcast_to(shape), ALU.mult).then_inc(done, 1)

        def mix_sum(eng, done, tiles, b, h):
            if h:
                zv = z[:, tiles, :].rearrange("p t (e k) -> p t e k", e=E)
                eng.wait_ge(done, b * Z_STEPS + 2 * h)
                eng.tensor_tensor(zv, zv, z_tmp[:, tiles], ALU.add).then_inc(done, 1)

        def vector_tiles(p):
            return 1 if p == 1 else 2


        block = mem.enter_context(nc.Block())

        @block.sync
        def _(sp):
            def load_x1(b):
                sp.dma_start(stage[:], of(x1_dram, b)).then_inc(x1_loaded, 16)

            def load_residual(b):
                sp.dma_start(x_res[:], of(x1_dram, b)).then_inc(xres_loaded, 16)

            def spread_q(b, p):
                sp.wait_ge(q_lo, b * PAIRS + p + 1)
                for a in range(2):
                    for half in range(2):
                        sp.dma_start(q_st[head_rows(half), p % 2, a, :, :].bitcast(F32),
                                     q_nat[head_rows(a), :, :].bitcast(F32)).then_inc(q_spread[p % 2], 16)

            def store(b):
                for t in range(NT):
                    sp.wait_ge(out_ready, b * NT + t + 1)
                    sp.dma_start(of(out_dram, b)[:, t, :], x_res[:, t, :]).then_inc(out_stored, 16)

            def steady(b, more):
                spread_q(b, 3)
                spread_q(b + 1, 0)
                if more:
                    sp.wait_ge(yt_ps, b * NT + 2 * NT)
                    load_x1(b + 2)
                spread_q(b + 1, 1)
                spread_q(b + 1, 2)
                store(b)
                sp.wait_ge(out_stored, (b + 1) * NT * 16)
                load_residual(b + 1)

            load_x1(0)
            sources = {"wq": wq, "wk": wk, "wx": w_vsd, "wo": wo}
            for name, k in WEIGHT_TILES:
                into = passing(name, k)
                sp.dma_start(into, sources[name][k * P:k * P + into.shape[0], :]).then_inc(w_loaded[name][k], 16)
            sp.dma_start(gate_raw[:], g_ffn.partition_broadcast(P)).then_inc(gate_loaded, 16)
            sp.wait_ge(w_lo["wo"], KZ)
            load_residual(0)
            spread_q(0, 0)
            sp.wait_ge(yt_ps, NT)
            load_x1(1)
            spread_q(0, 1)
            spread_q(0, 2)
            with sp.Fori(0, B - 2) as b:
                steady(b, True)
            steady(B - 2, False)
            spread_q(B - 1, 3)
            store(B - 1)
            sp.wait_ge(out_stored, B * NT * 16)

        @block.gpsimd
        def _(pool):
            pool.memset(ident[:], 0.0).then_inc(cleared, 1)
            pool.memset(beaten[:], 0.0).then_inc(cleared, 1)
            pool.memset(wo2[0:SHARED, :, KZ - 1, :].bitcast(F32), 0.0).then_inc(cleared, 1)
            pool.wait_ge(cleared, 3)
            pool.affine_select(out=ident[:], in_=ident[:], compare_op=ALU.not_equal, fill=1.0, base=0,
                               pattern=[[-1, P]], channel_multiplier=1).then_inc(ident_ready, 1)
            for name, k in WEIGHT_TILES:
                if name not in VECTOR_SPLITS:
                    take_weight_lo(pool, name, k)

            def mix_values(b, p, first=False):
                count = (b * PAIRS + p) * V_STEPS
                if p == 0:
                    pool.wait_ge(pick_ready, b + 1)
                    pool.wait_ge(xv_ready, b * NT + NT)
                if p >= 2 or not first:
                    pool.wait_ge(v_lo, b * PAIRS + p - 1)
                acc = v_acc[:, p % 2]
                shape = [P, NT, 2, DH]
                for e in range(E):
                    pool.tensor_tensor(v_tmp[:] if e else acc, xv[:, :, e, :].unsqueeze(2).broadcast_to(shape),
                                       pick[:, 0, :, 2 * p:2 * p + 2, e].unsqueeze(3).broadcast_to(shape),
                                       ALU.mult).then_inc(v_steps, 1)
                    pool.wait_ge(v_steps, count + 2 * e + (0 if e else 1))
                    if e:
                        pool.tensor_tensor(acc, acc, v_tmp[:], ALU.add).then_inc(v_steps, 1)
                        pool.wait_ge(v_steps, count + 2 * e + 1)

            def mix_pair(b, p):
                for h in (2 * p, 2 * p + 1):
                    mix_product(pool, z_pool, slice(vector_tiles(p), NT), b, h)
                    mix_sum(pool, z_pool, slice(vector_tiles(p), NT), b, h)

            for p in range(3):
                mix_values(0, p, True)
            with pool.Fori(0, B - 1) as b:
                mix_values(b, 3)
                mix_pair(b, 0)
                mix_pair(b, 1)
                mix_values(b + 1, 0)
                mix_pair(b, 2)
                mix_values(b + 1, 1)
                mix_pair(b, 3)
                mix_values(b + 1, 2)
            mix_values(B - 1, 3)
            for p in range(PAIRS):
                mix_pair(B - 1, p)

        @block.scalar
        def _(act):
            def take_weights(name):
                for k in range(weights[name].shape[2]):
                    act.wait_ge(w_loaded[name][k], 16)
                    act.activation(weight_tile(name, 0, k), passing(name, k), ACT.Copy).then_inc(w_hi[name], 1)

            def normalise(b):
                act.wait_ge(norm_ready, b + 1)
                act.wait_ge(x1_loaded, b * 16 + 16)
                for t in (2, 3):
                    act.activation(stage[:, t, :], stage[:, t, :], ACT.Identity, bias=norm[:, 1, t:t + 1],
                                   scale=norm[:, 0, t:t + 1]).then_inc(y_act, 1)

            def scores_exp(b, n, first):
                act.wait_ge(nmax_ready, b * STEPS + n + 1)
                if n >= 2 or not first:
                    act.wait_ge(pt_ps, b * STEPS + n - 1)
                act.activation(probs[:, n % 2, :], ps_s[:, n % 2, :], ACT.Exp, bias=nmax[:, n:n + 1],
                               accum_out=den[:, n // NT, n % NT:n % NT + 1]).then_inc(p_exp, 1)

            def probs_hi(b, n, first):
                h, t = n // NT, n % NT
                act.wait_ge(pt_ps, b * STEPS + n + 1)
                if t == 0 and (h >= 2 or not first):
                    act.wait_ge(o_ps, b * H + h - 1)
                act.activation(pt2[:, h % 2, 0, :, t * P:(t + 1) * P], ps_p[:, n % 2], ACT.Copy).then_inc(pt_hi, 1)

            def value_hi(b, p, first):
                act.wait_ge(v_steps, (b * PAIRS + p + 1) * V_STEPS)
                if p >= 2 or not first:
                    act.wait_ge(o_ps, b * H + 2 * p - 2)
                act.activation(pair_values(p, 0), v_acc[:, p % 2], ACT.Copy).then_inc(v_hi, 1)

            def out_half(b, h, first):
                act.wait_ge(o_ps, b * H + h + 1)
                if h or not first:
                    act.wait_ge(o_ready, b * H + h)
                act.activation(o_tmp[DH:P, :], ps_o[0:DH, :], ACT.Copy).then_inc(o_half, 1)

            def part_hi(b, name, n, first):
                ps = ps_r[:, bank_of((name, n)), :]
                if name == "turn_y":
                    act.wait_ge(yt_ps, b * NT + n + 1)
                    if n == 0 and not first:
                        act.wait_ge(k_ps, b * PAIRS)
                    act.activation(y_t2[:, 0, :, n * P:(n + 1) * P], ps.rearrange("p (k t) -> p k t", k=ND),
                                   ACT.Copy).then_inc(yt_hi, 1)
                elif name == "experts":
                    act.wait_ge(ex_ps, b * NT + n + 1)
                    if n == 0 and not first:
                        act.wait_ge(v_steps, b * PAIRS * V_STEPS)
                        act.wait_ge(mask_ready, b)
                    act.activation(logits[:, :, n * H:(n + 1) * H, :],
                                   ps[:, NV:NX].rearrange("p (s h e) -> p s h e", s=2, h=H),
                                   ACT.Copy).then_inc(logits_ready, 1)
                    act.activation(xv[:, n], ps[:, 0:NV].rearrange("p (e k) -> p e k", e=E),
                                   ACT.Copy).then_inc(xv_ready, 1)
                elif name == "q":
                    act.wait_ge(q_ps, b * PAIRS + n + 1)
                    if n:
                        act.wait_ge(q_spread[(n - 1) % 2], b * (PAIRS * 32) + ((n - 1) // 2 + 1) * 64)
                    elif not first:
                        act.wait_ge(q_spread[1], b * (PAIRS * 32))
                    act.activation(q_nat[:, 0, :], ps, ACT.Copy, scale=SCALE).then_inc(q_hi, 1)
                elif name == "k":
                    act.wait_ge(k_ps, b * PAIRS + n + 1)
                    for a in range(2):
                        own = head_rows(a)
                        act.activation(k_st[own, n % 2, a, :], ps[own, :], ACT.Copy).then_inc(k_hi, 1)
                elif name == "turn_o":
                    act.wait_ge(to_ps, b * PAIRS + n + 1)
                    if n:
                        act.wait_ge(z_dve, b * Z_STEPS + 4 * n - 1)
                        act.wait_ge(z_pool, b * Z_STEPS + 4 * n - 1)
                    act.activation(attn[:], ps.rearrange("p (t a k) -> p t a k", t=NT, a=2),
                                   ACT.Copy).then_inc(attn_ready, 1)
                elif name == "turn_z":
                    act.wait_ge(zt_ps, b * KZ + n + 1)
                    act.activation(z_t2[:, 0, n, :], ps, ACT.Copy).then_inc(zt_hi, 1)

            def step(b, n, part, first=False):
                if part == 0:
                    for h in range(H):
                        if n == NT * h + SUM_AT:
                            out_half(b, h, first)
                    if 0 <= n - SPLIT_LAG < STEPS:
                        probs_hi(b, n - SPLIT_LAG, first)
                    if 0 <= n < STEPS:
                        scores_exp(b, n, first)
                    return
                behind = 2 - part
                for name, i in ended(n - behind):
                    if behind == HI_BEHIND.get(name, 1):
                        part_hi(b, name, i, first)
                if part == 1:
                    return
                if n in VALUE_AT:
                    value_hi(b, VALUE_AT.index(n), first)
                if n == NORMALISE_AT:
                    normalise(b)
                if n == GATES_AT:
                    act.wait_ge(logits_ready, b * NT + NT)
                    act.activation(sig[:], logits[:, 0], ACT.Exp, scale=-1.0).then_inc(sig_exp, 1)

            for n in range(EARLY - STEPS, EARLY):
                for part in range(3):
                    step(0, n, part, True)
                for name in weights:
                    if n == SPLIT_AT[name]:
                        take_weights(name)
                if n == 0:
                    act.wait_ge(gate_loaded, 16)
                    act.activation(gate[:], gate_raw[:], ACT.Tanh).then_inc(gate_ready, 1)
            with act.Fori(0, B - 1) as b:
                for n in range(EARLY, EARLY + STEPS):
                    for part in range(3):
                        step(b, n, part)
                        step(b + 1, n - STEPS, part)
            for n in range(EARLY, EARLY + STEPS):
                for part in range(3):
                    step(B - 1, n, part)

        @block.vector
        def _(dve):
            def take_norm(b):
                if not (isinstance(b, int) and b == 0):
                    dve.wait_ge(y_act, b * 2)
                dve.tensor_scalar(norm[:], x1_norm[:, :, bass.ds(b * NT, NT)], 1.0, None, ALU.mult).then_inc(norm_ready, 1)

            def normalise(b):
                dve.wait_ge(norm_ready, b + 1)
                dve.wait_ge(x1_loaded, b * 16 + 16)
                for t in (0, 1):
                    dve.tensor_scalar(stage[:, t, :], stage[:, t, :], norm[:, 0, t:t + 1], norm[:, 1, t:t + 1], ALU.mult,
                                      ALU.add).then_inc(y_dve, 1)

            def row_max(b, n):
                dve.wait_ge(s_ready, b * STEPS + n + 1)
                dve.tensor_reduce(nmax[:, n:n + 1], ps_s[:, n % 2, :], AX_X, ALU.max, negate=True).then_inc(nmax_ready, 1)

            def probs_lo(b, n):
                h, t = n // NT, n % NT
                dve.wait_ge(pt_hi, b * STEPS + n + 1)
                dve.tensor_tensor(pt2[:, h % 2, 1, :, t * P:(t + 1) * P], ps_p[:, n % 2],
                                  pt2[:, h % 2, 0, :, t * P:(t + 1) * P].bitcast(F32), ALU.subtract).then_inc(pt_lo, 1)

            def value_lo(b, p):
                dve.wait_ge(v_hi, b * PAIRS + p + 1)
                dve.tensor_tensor(pair_values(p, 1), v_acc[:, p % 2], pair_values(p, 0).bitcast(F32),
                                  ALU.subtract).then_inc(v_lo, 1)

            def out_sum(b, h, first):
                p, a = h // 2, h % 2
                dve.wait_ge(o_half, b * H + h + 1)
                if a == 0 and (p or not first):
                    dve.wait_ge(to_ps, b * PAIRS + p)
                dve.tensor_tensor(o_t[head_rows(a), :], ps_o[DH:P, :], o_tmp[DH:P, :], ALU.add).then_inc(o_ready, 1)

            def row_sums(b, p):
                dve.wait_ge(p_exp, b * STEPS + PAIR * p + PAIR)
                heads = slice(2 * p, 2 * p + 2)
                dve.reciprocal(rden[:, heads, :], den[:, heads, :]).then_inc(rden_ready, 1)

            def coefficients(b, p):
                heads = slice(2 * p, 2 * p + 2)
                dve.wait_ge(rden_ready, b * PAIRS + p + 1)
                if p == 0:
                    dve.wait_ge(mask_ready, b + 1)
                dve.tensor_tensor(coef[:, heads], pick[:, 1, :, heads, :].rearrange("p t h e -> p h t e"),
                                  rden[:, heads, :].unsqueeze(3).broadcast_to([P, 2, NT, E]),
                                  ALU.mult).then_inc(coef_ready, 1)

            def part_lo(b, name, n):
                ps = ps_r[:, bank_of((name, n)), :]
                if name == "turn_y":
                    cols = slice(n * P, (n + 1) * P)
                    dve.wait_ge(yt_hi, b * NT + n + 1)
                    dve.tensor_tensor(y_t2[:, 1, :, cols], ps.rearrange("p (k t) -> p k t", k=ND),
                                      y_t2[:, 0, :, cols].bitcast(F32), ALU.subtract).then_inc(yt_lo, 1)
                elif name == "q":
                    dve.wait_ge(q_hi, b * PAIRS + n + 1)
                    dve.scalar_tensor_tensor(q_nat[:, 1, :], ps, SCALE, q_nat[:, 0, :].bitcast(F32), ALU.mult,
                                             ALU.subtract).then_inc(q_lo, 1)
                elif name == "k":
                    for a in range(2):
                        own, other = head_rows(a), head_rows(1 - a)
                        dve.wait_ge(k_hi, b * H + 2 * n + a + 1)
                        dve.tensor_tensor(k_st[other, n % 2, a, :], ps[own, :], k_st[own, n % 2, a, :].bitcast(F32),
                                          ALU.subtract).then_inc(k_lo, 1)
                elif name == "turn_z":
                    dve.wait_ge(zt_hi, b * KZ + n + 1)
                    dve.tensor_tensor(z_t2[:, 1, n, :], ps, z_t2[:, 0, n, :].bitcast(F32),
                                      ALU.subtract).then_inc(zt_lo, 1)
                elif name == "result":
                    if n == 0:
                        dve.wait_ge(xres_loaded, b * 16 + 16)
                        dve.wait_ge(gate_ready, 1)
                    dve.wait_ge(res_ps, b * NT + n + 1)
                    dve.scalar_tensor_tensor(x_res[:, n, :], ps, gate[:, 0:1], x_res[:, n, :],
                                             ALU.mult, ALU.add).then_inc(out_ready, 1)

            def compare(b, experts):
                dve.wait_ge(logits_ready, b * NT + NT)
                flat = logits[:].rearrange("p s g e -> p (s g) e")
                groups = 2 * NT * H
                for k in experts:
                    for others, before in ((slice(k + 1, E), ALU.is_gt), (slice(0, k), ALU.is_ge)):
                        if others.stop > others.start:
                            dve.tensor_tensor(beaten[:, :, k, others], flat[:, :, others],
                                              flat[:, :, k:k + 1].broadcast_to([P, groups, others.stop - others.start]),
                                              before).then_inc(compared, 1)

            def count_better(b):
                dve.wait_ge(sig_exp, b + 1)
                dve.tensor_scalar(sig[:], sig[:], 1.0, None, ALU.add).then_inc(gates, 1)
                dve.wait_ge(compared, (b + 1) * COMPARISONS)
                dve.tensor_reduce(rank, beaten[:], AX_X, ALU.add).then_inc(gates, 1)

            def route_values(b, first):
                dve.wait_ge(gates, b * 3 + 1)
                dve.reciprocal(sig[:], sig[:]).then_inc(gates, 1)
                if not first:
                    dve.wait_ge(v_steps, b * PAIRS * V_STEPS)
                dve.wait_ge(gates, b * 3 + 3)
                dve.scalar_tensor_tensor(pick[:, 0].rearrange("p t h e -> p (t h) e"), rank[:, 0:NT * H], 1.5, sig[:],
                                         ALU.is_lt, ALU.mult).then_inc(pick_ready, 1)

            def route_out(b, first):
                if not first:
                    dve.wait_ge(coef_ready, b * PAIRS)
                dve.tensor_scalar(pick[:, 1].rearrange("p t h e -> p (t h) e"), rank[:, NT * H:], 1.5, None,
                                  ALU.is_lt).then_inc(mask_ready, 1)

            def step(b, n, part, first=False):
                spread(b, n, (0, 1, None, 2)[part])
                if part == 0:
                    if n == NORMALISE_AT:
                        take_norm(b)
                    if 0 <= n - SPLIT_LAG < STEPS:
                        probs_lo(b, n - SPLIT_LAG)
                    for h in range(H):
                        if n == NT * h + SUM_AT:
                            out_sum(b, h, first)
                else:
                    behind = 3 - part
                    for what in ended(n - behind):
                        if behind == LO_BEHIND.get(what[0] + "0" if what[0] in "qk" and what[1] == 0 else what[0], 1):
                            part_lo(b, *what)
                if part == 3:
                    if n - 1 in VALUE_AT:
                        value_lo(b, VALUE_AT.index(n - 1))
                    if n == GATES_AT:
                        compare(b, range(0, E // 2))
                    if n == GATES_AT + 1:
                        compare(b, range(E // 2, E))
                    if n == ROUTE_AT[0]:
                        count_better(b)
                    if n == ROUTE_AT[1]:
                        route_values(b, first)
                    if n == ROUTE_AT[2]:
                        route_out(b, first)
                    if n == NORMALISE_AT:
                        normalise(b)

            def spread(b, n, place):
                for p in range(PAIRS):
                    at = TURN_O_AT[p]
                    if (n, place) == (PAIR * p + PAIR, 0):
                        row_sums(b, p)
                    if (n, place) == (PAIR * p + PAIR, 2):
                        coefficients(b, p)
                    for (step_at, place_at), mix, h in zip(MIX_LAST if p == PAIRS - 1 else MIX_PLACES,
                                                           (mix_product, mix_sum) * 2, (0, 0, 1, 1)):
                        if (n, place) == (at + step_at, place_at):
                            mix(dve, z_dve, slice(0, vector_tiles(p)), b, 2 * p + h)

            dve.wait_ge(cleared, 3)
            for n in range(EARLY - STEPS, EARLY):
                if n >= 0:
                    row_max(0, n)
                for part in range(4):
                    step(0, n, part, True)
                for name, k in WEIGHT_TILES:
                    if VECTOR_SPLITS.get(name) == n:
                        take_weight_lo(dve, name, k)
            with dve.Fori(0, B - 1) as b:
                for n in range(EARLY, EARLY + STEPS):
                    row_max(*((b, n) if n < STEPS else (b + 1, n - STEPS)))
                    for part in range(4):
                        step(b, n, part)
                        step(b + 1, n - STEPS, part)
            for n in range(EARLY, EARLY + STEPS):
                if n < STEPS:
                    row_max(B - 1, n)
                for part in range(4):
                    step(B - 1, n, part)

        @block.tensor
        def _(pe):
            pe.wait_ge(ident_ready, 1)

            def wait_read(b, what):
                name, n = what
                if name == "turn_y":
                    pe.wait_ge(yt_lo, b * NT + n + 1)
                elif name == "experts":
                    pe.wait_ge(logits_ready, b * NT + n + 1)
                    pe.wait_ge(xv_ready, b * NT + n + 1)
                elif name == "q":
                    pe.wait_ge(q_lo, b * PAIRS + n + 1)
                elif name == "k":
                    pe.wait_ge(k_lo, b * H + 2 * n + 2)
                elif name == "turn_o":
                    pe.wait_ge(attn_ready, b * PAIRS + n + 1)
                elif name == "turn_z":
                    pe.wait_ge(zt_lo, b * KZ + n + 1)
                else:
                    pe.wait_ge(out_ready, b * NT + n + 1)

            def wait_bank(b, what, first, last):
                place = ORDER.index(what) - RING
                while True:
                    before = ORDER[place]
                    offset = (before in AHEAD) - (what in AHEAD) - (place < 0)
                    if not (first and offset < 0) and not (last and offset > 0):
                        wait_read(b + offset, before)
                        return
                    place -= RING
                    if first and place < 0:
                        return

            def taken(every, part, parts):
                return range(len(every) * part // parts, len(every) * (part + 1) // parts)

            def shared_part(b, name, n, part, parts, first, last):
                ps = ps_r[:, bank_of((name, n)), :]
                if part == 0:
                    wait_bank(b, (name, n), first, last)
                if name == "turn_y":
                    pe.wait_ge(*((y_dve, b * 2 + n + 1) if n < 2 else (y_act, b * 2 + n - 1)))
                    for k in range(ND):
                        end = pe.transpose(ps[:, k * P:(k + 1) * P], stage[:, n, k * P:(k + 1) * P], ident[:])
                    end.then_inc(yt_ps, 1)
                elif name in "qk":
                    if part == 0:
                        pe.wait_ge(yt_lo, b * NT + NT)
                        if first:
                            pe.wait_ge(w_lo["w" + name], ND)
                    w2 = wq2 if name == "q" else wk2
                    every = [(k, l, r) for k in range(ND) for l, r in PASSES]
                    for m in taken(every, part, parts):
                        k, l, r = every[m]
                        end = pe.matmul(ps, w2[:, l, k, n * P:(n + 1) * P], y_t2[:, r, k, :], start=m == 0,
                                        stop=m == len(every) - 1)
                    if part == parts - 1:
                        end.then_inc(q_ps if name == "q" else k_ps, 1)
                elif name == "experts":
                    if part == 0:
                        pe.wait_ge(yt_lo, b * NT + n + 1)
                        if first:
                            pe.wait_ge(w_lo["wx"], ND)
                    every = [(k, l, r) for k in range(ND) for l, r in PASSES]
                    for m in taken(every, part, parts):
                        k, l, r = every[m]
                        end = pe.matmul(ps[:, 0:NX], y_t2[:, l, k, n * P:(n + 1) * P], wx2[:, r, k, :], start=m == 0,
                                        stop=m == len(every) - 1)
                    if part == parts - 1:
                        end.then_inc(ex_ps, 1)
                elif name == "turn_o":
                    pe.wait_ge(o_ready, b * H + 2 * n + 2)
                    for t in range(NT):
                        end = pe.transpose(ps[:, t * P:(t + 1) * P], o_t[:, t * P:(t + 1) * P], ident[:])
                    end.then_inc(to_ps, 1)
                elif name == "turn_z":
                    if n == 0:
                        pe.wait_ge(z_dve, (b + 1) * Z_STEPS)
                        pe.wait_ge(z_pool, (b + 1) * Z_STEPS)
                    for t in range(NT):
                        end = pe.transpose(ps[:, t * P:(t + 1) * P], z[:, t, tile_at(n):tile_at(n) + P], ident[:])
                    end.then_inc(zt_ps, 1)
                else:
                    if n == 0 and part == 0:
                        pe.wait_ge(zt_lo, b * KZ + KZ)
                        pe.wait_ge(w_lo["wo"], KZ)
                    every = [(k, l, r) for k in range(KZ) for l, r in PASSES]
                    for m in taken(every, part, parts):
                        k, l, r = every[m]
                        end = pe.matmul(ps, z_t2[:, l, k, n * P:(n + 1) * P], wo2[:, r, k, :],
                                        start=m == 0, stop=m == len(every) - 1)
                    if part == parts - 1:
                        end.then_inc(res_ps, 1)

            def scores(b, n, first):
                h, t = n // NT, n % NT
                slot, a = h // 2 % 2, h % 2
                if n % PAIR == 0:
                    pe.wait_ge(q_spread[slot], b * (PAIRS * 32) + (h // 4 + 1) * 64)
                    pe.wait_ge(k_lo, b * H + h + 2)
                if n >= 2 or not first:
                    pe.wait_ge(p_exp, b * STEPS + n - 1)
                for part in range(2):
                    end = pe.matmul(ps_s[:, n % 2, :], q_st[:, slot, a, part, t * P:(t + 1) * P], k_st[:, slot, a, :],
                                    start=part == 0, stop=part == 1)
                end.then_inc(s_ready, 1)

            def turn_probs(b, n, first):
                pe.wait_ge(p_exp, b * STEPS + n + 1)
                if n >= 2 or not first:
                    pe.wait_ge(pt_lo, b * STEPS + n - 1)
                for k in range(NT):
                    end = pe.transpose(ps_p[:, n % 2, k, :], probs[:, n % 2, k * P:(k + 1) * P], ident[:])
                end.then_inc(pt_ps, 1)

            def values(b, h, k, first):
                if k == 0:
                    pe.wait_ge(pt_lo, b * STEPS + NT * h + NT)
                    pe.wait_ge(v_lo, b * PAIRS + h // 2 + 1)
                    if h or not first:
                        pe.wait_ge(o_ready, b * H + h)
                for part in range(2):
                    end = pe.matmul(ps_o[:], v_st[:, h % 4, k, :, :], pt2[:, h % 2, part, k, :],
                                    start=k == 0 and part == 0, stop=k == NT - 1 and part == 1)
                if k == NT - 1:
                    end.then_inc(o_ps, 1)

            def step(b, n, part, first=False, last=False):
                if part == 0 and 0 <= n < STEPS:
                    scores(b, n, first)
                if part == 1 and 0 <= n - LAG < STEPS:
                    turn_probs(b, n - LAG, first)
                if part == 2:
                    for h in range(H):
                        for k in range(NT):
                            if n == NT * h + PV_AT[k]:
                                values(b, h, k, first)
                    for what in parts_at(n):
                        shared_part(b, *what, first, last)

            for n in range(CUT - STEPS, CUT):
                for part in range(3):
                    step(0, n, part, first=True)
            with pe.Fori(0, B - 1) as b:
                for n in range(CUT, CUT + STEPS):
                    for part in range(3):
                        step(b, n, part)
                        step(b + 1, n - STEPS, part)
            for n in range(CUT, CUT + STEPS):
                for part in range(3):
                    step(B - 1, n, part, last=True)


def program(nc, x, ctx, ctx_t, g_xattn, g_ffn, w_sim, w_sim_cols, b_sim, w_qv, b_qv, wq, wk, w_vsd, wo, x1, out):
    B, T, _ = x.shape
    with nc.sbuf_tensor("x1_norm", [P, 2, B * T // P], F32) as x1_norm:
        cross_attention(nc, x, ctx, ctx_t, g_xattn, w_sim, w_sim_cols, b_sim, w_qv, b_qv, x1, x1_norm)
        expert_attention(nc, x1, x1_norm, g_ffn, wq, wk, w_vsd, wo, out)


def kernel(x, ctx_1024, g_xattn, g_ffn, L0_xattn_w_sim, L0_xattn_b_sim, L0_xattn_W_qv, L0_xattn_b_qv,
           L0_ffn_Wq, L0_ffn_Wk, L0_ffn_Ws, L0_ffn_Wd, L0_ffn_Wv, L0_ffn_Wo):
    import numpy as np
    import concourse.bacc as bacc
    from concourse.bass_utils import run_bass_kernel_spmd

    x, ctx = np.asarray(x), np.asarray(ctx_1024)
    w_sim, wv, wo = np.asarray(L0_xattn_w_sim), np.asarray(L0_ffn_Wv), np.asarray(L0_ffn_Wo)
    D = x.shape[2]
    arrays = {
        "x": x,
        "ctx": ctx,
        "ctx_t": ctx.transpose(0, 2, 1),
        "g_xattn": np.asarray(g_xattn),
        "g_ffn": np.asarray(g_ffn),
        "w_sim": w_sim,
        "w_sim_cols": w_sim.reshape(3, D // P, P).transpose(2, 0, 1),
        "b_sim": np.asarray(L0_xattn_b_sim),
        "w_qv": np.asarray(L0_xattn_W_qv),
        "b_qv": np.asarray(L0_xattn_b_qv),
        "wq": np.asarray(L0_ffn_Wq),
        "wk": np.asarray(L0_ffn_Wk),
        "w_vsd": np.concatenate([wv.transpose(1, 0, 2).reshape(D, -1), np.asarray(L0_ffn_Ws),
                                 np.asarray(L0_ffn_Wd)], axis=1),
        "wo": wo.reshape(-1, D),
    }
    nc = bacc.Bacc("TRN2", target_bir_lowering=False, num_devices=1)
    feed, args = {}, {}
    for name, a in arrays.items():
        a = np.ascontiguousarray(a)
        feed[f"in_{name}"] = a
        args[name] = nc.dram_tensor(f"in_{name}", a.shape, mybir.dt.from_np(a.dtype), kind="ExternalInput").ap()
    out = nc.dram_tensor("out_dram", x.shape, F32, kind="ExternalOutput").ap()
    x1 = nc.dram_tensor("x1_dram", x.shape, F32, kind="Internal").ap()
    program(nc, **args, x1=x1, out=out)
    r = run_bass_kernel_spmd(nc, [feed], core_ids=[0])
    return r.results[0]["out_dram"]
```
